# Optimizing a Trainium2 kernel written in Bass

```python
import numpy as np
import jax
import jax.numpy as jnp

def _softmax(x, axis=-1):
    return jax.nn.softmax(x, axis=axis)

def _gelu(x):
    return jax.nn.gelu(x, approximate=True)

def _silu(x):
    return jax.nn.silu(x)

def _sigmoid(x):
    return jax.nn.sigmoid(x)

def _layernorm(x, axis=-1, eps=1e-05):
    m = jnp.mean(x, axis=axis, keepdims=True)
    v = jnp.var(x, axis=axis, keepdims=True)
    return (x - m) / jnp.sqrt(v + eps)

def _scatter_add(tgt, idx, src, axis=0):
    return tgt.at[idx].add(src)

def _segment_sum(src, seg, n):
    return jax.ops.segment_sum(src, seg, n)
kernel_name = 'mk_gps_d1_gnn_r8_8fad8c'

def setup_inputs(seed: int=0):
    np.random.seed(seed)
    _w = jnp.asarray

    def _rec_inputs():
        import jax
        import jax.numpy as jnp
        _gk = jax.random.key(seed)
        x = -0.0006008 + 1.001 * jax.random.normal(jax.random.fold_in(_gk, 1), (6250, 256), jnp.float32)
        src = jax.random.randint(jax.random.fold_in(_gk, 2), (200000,), 0, 6250, jnp.int32)
        dst = jnp.minimum((6250 * jax.random.uniform(jax.random.fold_in(_gk, 3), (200000,)) ** 2.0).astype(jnp.int32), 49999)
        _o = jnp.argsort(dst, stable=True)
        src = src[_o]
        dst = dst[_o]
        return (x, src, dst)
    x, src, dst = _rec_inputs()

    def _L0_gnn_setup():
        import jax, jax.numpy as jnp
        import numpy as np
        N = 1250
        E = 40000
        IN_DIM = 256
        HID = 256
        HEADS = 4
        NEG_SLOPE = 0.2
        LN_EPS = 1e-05

        def _gat_conv(h, src, dst, W, att_src, att_dst, bias, heads, concat):
            n = h.shape[0]
            d = W.shape[1] // heads
            xh = (h @ W).reshape(n, heads, d)
            a_s = (xh * att_src).sum(-1)
            a_d = (xh * att_dst).sum(-1)
            alpha = jax.nn.leaky_relu(a_s[src] + a_d[dst], NEG_SLOPE)
            amax = jax.ops.segment_max(alpha, dst, num_segments=n)
            e = jnp.exp(alpha - amax[dst])
            z = jax.ops.segment_sum(e, dst, num_segments=n)
            alpha = e / (z[dst] + 1e-16)
            out = jax.ops.segment_sum(xh[src] * alpha[:, :, None], dst, num_segments=n)
            out = out.reshape(n, heads * d) if concat else out.mean(axis=1)
            return out + bias

        def _layernorm(x, g, b):
            mu = x.mean(-1, keepdims=True)
            var = ((x - mu) ** 2).mean(-1, keepdims=True)
            return (x - mu) / jnp.sqrt(var + LN_EPS) * g + b
        key = jax.random.key(seed)
        ks = jax.random.split(key, 24)

        def p(k, shape, fan_in):
            return jax.random.normal(k, shape, jnp.float32) / np.sqrt(fan_in).astype(np.float32)
        dh = HID // HEADS
        inp = {'x': jax.random.normal(ks[0], (N, IN_DIM), jnp.float32), 'edge_index': jax.random.randint(ks[1], (2, E), 0, N, jnp.int32), 'W0': p(ks[2], (IN_DIM, HID), IN_DIM), 'att_src0': p(ks[3], (HEADS, dh), dh), 'att_dst0': p(ks[4], (HEADS, dh), dh), 'bias0': jnp.zeros((HID,), jnp.float32), 'ln_g0': jnp.ones((HID,), jnp.float32), 'ln_b0': jnp.zeros((HID,), jnp.float32), 'W1': p(ks[5], (HID, HID), HID), 'att_src1': p(ks[6], (HEADS, dh), dh), 'att_dst1': p(ks[7], (HEADS, dh), dh), 'bias1': jnp.zeros((HID,), jnp.float32), 'ln_g1': jnp.ones((HID,), jnp.float32), 'ln_b1': jnp.zeros((HID,), jnp.float32), 'W2': p(ks[8], (HID, HID), HID), 'att_src2': p(ks[9], (1, HID), HID), 'att_dst2': p(ks[10], (1, HID), HID), 'bias2': jnp.zeros((HID,), jnp.float32), 'ln_g2': jnp.ones((HID,), jnp.float32), 'ln_b2': jnp.zeros((HID,), jnp.float32)}
        return inp
    _L0_gnn_all = _L0_gnn_setup()
    _L0_gnn_in = {k: v for k, v in _L0_gnn_all.items() if k in ('W0', 'att_src0', 'att_dst0', 'bias0', 'ln_g0', 'ln_b0', 'W1', 'att_src1', 'att_dst1', 'bias1', 'ln_g1', 'ln_b1', 'W2', 'att_src2', 'att_dst2', 'bias2', 'ln_g2', 'ln_b2')}
    del _L0_gnn_all

    def _L0_mix_setup():
        import jax, jax.numpy as jnp
        import numpy as np
        N, F, C, H = (32, 512, 256, 8)
        D = C // H
        EPS_ATTN = 1e-06
        EPS_LN = 1e-05

        def layer_norm(x, g, b):
            mu = jnp.mean(x, axis=-1, keepdims=True)
            var = jnp.var(x, axis=-1, keepdims=True)
            return (x - mu) * jax.lax.rsqrt(var + EPS_LN) * g + b
        key = jax.random.key(seed)
        ks = jax.random.split(key, 8)
        s = 1.0 / np.sqrt(C)
        return {'x': jax.random.normal(ks[0], (N, F, C), jnp.float32), 'Wqkv': jax.random.uniform(ks[1], (3 * C, C), jnp.float32, -s, s), 'ln1_g': jnp.ones((C,), jnp.float32), 'ln1_b': jnp.zeros((C,), jnp.float32), 'W1': jax.random.uniform(ks[2], (C, C), jnp.float32, -s, s), 'b1': jax.random.uniform(ks[3], (C,), jnp.float32, -s, s), 'W2': jax.random.uniform(ks[4], (C, C), jnp.float32, -s, s), 'b2': jax.random.uniform(ks[5], (C,), jnp.float32, -s, s), 'ln2_g': jnp.ones((C,), jnp.float32), 'ln2_b': jnp.zeros((C,), jnp.float32)}
    _L0_mix_all = _L0_mix_setup()
    _L0_mix_in = {k: v for k, v in _L0_mix_all.items() if k in ('Wqkv', 'ln1_g', 'ln1_b', 'W1', 'b1', 'W2', 'b2', 'ln2_g', 'ln2_b')}
    del _L0_mix_all

    def _L0_ffn_setup():
        import jax, jax.numpy as jnp
        import numpy as np
        E = 8
        K = 2
        D = 256
        H = 512
        DOUT = 256
        EPS = 1e-05
        key = jax.random.key(seed)
        ks = jax.random.split(key, 9)
        s = 0.02
        return {'x': jax.random.normal(ks[0], (4, 1024, D), jnp.float32), 'gamma': 1.0 + 0.05 * jax.random.normal(ks[1], (D,), jnp.float32), 'beta': 0.05 * jax.random.normal(ks[2], (D,), jnp.float32), 'Wr': 0.01 * jax.random.normal(ks[3], (D, E), jnp.float32), 'br': jnp.zeros((E,), jnp.float32), 'W1': s * jax.random.normal(ks[4], (E, D, H), jnp.float32), 'b1': s * jax.random.normal(ks[5], (E, H), jnp.float32), 'W2': s * jax.random.normal(ks[6], (E, H, DOUT), jnp.float32), 'b2': s * jax.random.normal(ks[7], (E, DOUT), jnp.float32)}
    _L0_ffn_all = _L0_ffn_setup()
    _L0_ffn_in = {k: v for k, v in _L0_ffn_all.items() if k in ('gamma', 'beta', 'Wr', 'br', 'W1', 'b1', 'W2', 'b2')}
    del _L0_ffn_all
    return {'x': x, 'src': src, 'dst': dst, 'L0_gnn_W0': _L0_gnn_in['W0'], 'L0_gnn_att_src0': _L0_gnn_in['att_src0'], 'L0_gnn_att_dst0': _L0_gnn_in['att_dst0'], 'L0_gnn_bias0': _L0_gnn_in['bias0'], 'L0_gnn_ln_g0': _L0_gnn_in['ln_g0'], 'L0_gnn_ln_b0': _L0_gnn_in['ln_b0'], 'L0_gnn_W1': _L0_gnn_in['W1'], 'L0_gnn_att_src1': _L0_gnn_in['att_src1'], 'L0_gnn_att_dst1': _L0_gnn_in['att_dst1'], 'L0_gnn_bias1': _L0_gnn_in['bias1'], 'L0_gnn_ln_g1': _L0_gnn_in['ln_g1'], 'L0_gnn_ln_b1': _L0_gnn_in['ln_b1'], 'L0_gnn_W2': _L0_gnn_in['W2'], 'L0_gnn_att_src2': _L0_gnn_in['att_src2'], 'L0_gnn_att_dst2': _L0_gnn_in['att_dst2'], 'L0_gnn_bias2': _L0_gnn_in['bias2'], 'L0_gnn_ln_g2': _L0_gnn_in['ln_g2'], 'L0_gnn_ln_b2': _L0_gnn_in['ln_b2'], 'L0_mix_Wqkv': _L0_mix_in['Wqkv'], 'L0_mix_ln1_g': _L0_mix_in['ln1_g'], 'L0_mix_ln1_b': _L0_mix_in['ln1_b'], 'L0_mix_W1': _L0_mix_in['W1'], 'L0_mix_b1': _L0_mix_in['b1'], 'L0_mix_W2': _L0_mix_in['W2'], 'L0_mix_b2': _L0_mix_in['b2'], 'L0_mix_ln2_g': _L0_mix_in['ln2_g'], 'L0_mix_ln2_b': _L0_mix_in['ln2_b'], 'L0_ffn_gamma': _L0_ffn_in['gamma'], 'L0_ffn_beta': _L0_ffn_in['beta'], 'L0_ffn_Wr': _L0_ffn_in['Wr'], 'L0_ffn_br': _L0_ffn_in['br'], 'L0_ffn_W1': _L0_ffn_in['W1'], 'L0_ffn_b1': _L0_ffn_in['b1'], 'L0_ffn_W2': _L0_ffn_in['W2'], 'L0_ffn_b2': _L0_ffn_in['b2']}

def reference(x, src, dst, L0_gnn_W0, L0_gnn_att_src0, L0_gnn_att_dst0, L0_gnn_bias0, L0_gnn_ln_g0, L0_gnn_ln_b0, L0_gnn_W1, L0_gnn_att_src1, L0_gnn_att_dst1, L0_gnn_bias1, L0_gnn_ln_g1, L0_gnn_ln_b1, L0_gnn_W2, L0_gnn_att_src2, L0_gnn_att_dst2, L0_gnn_bias2, L0_gnn_ln_g2, L0_gnn_ln_b2, L0_mix_Wqkv, L0_mix_ln1_g, L0_mix_ln1_b, L0_mix_W1, L0_mix_b1, L0_mix_W2, L0_mix_b2, L0_mix_ln2_g, L0_mix_ln2_b, L0_ffn_gamma, L0_ffn_beta, L0_ffn_Wr, L0_ffn_br, L0_ffn_W1, L0_ffn_b1, L0_ffn_W2, L0_ffn_b2):
    import jax
    import jax.numpy as jnp

    def _L0_gnn_ref(x, edge_index, W0, att_src0, att_dst0, bias0, ln_g0, ln_b0, W1, att_src1, att_dst1, bias1, ln_g1, ln_b1, W2, att_src2, att_dst2, bias2, ln_g2, ln_b2):
        import jax, jax.numpy as jnp
        import numpy as np
        N = 1250
        E = 40000
        IN_DIM = 256
        HID = 256
        HEADS = 4
        NEG_SLOPE = 0.2
        LN_EPS = 1e-05

        def _gat_conv(h, src, dst, W, att_src, att_dst, bias, heads, concat):
            n = h.shape[0]
            d = W.shape[1] // heads
            xh = (h @ W).reshape(n, heads, d)
            a_s = (xh * att_src).sum(-1)
            a_d = (xh * att_dst).sum(-1)
            alpha = jax.nn.leaky_relu(a_s[src] + a_d[dst], NEG_SLOPE)
            amax = jax.ops.segment_max(alpha, dst, num_segments=n)
            e = jnp.exp(alpha - amax[dst])
            z = jax.ops.segment_sum(e, dst, num_segments=n)
            alpha = e / (z[dst] + 1e-16)
            out = jax.ops.segment_sum(xh[src] * alpha[:, :, None], dst, num_segments=n)
            out = out.reshape(n, heads * d) if concat else out.mean(axis=1)
            return out + bias

        def _layernorm(x, g, b):
            mu = x.mean(-1, keepdims=True)
            var = ((x - mu) ** 2).mean(-1, keepdims=True)
            return (x - mu) / jnp.sqrt(var + LN_EPS) * g + b
        n = x.shape[0]
        loop = jnp.arange(n, dtype=edge_index.dtype)
        src = jnp.concatenate([edge_index[0], loop])
        dst = jnp.concatenate([edge_index[1], loop])
        layers = [(W0, att_src0, att_dst0, bias0, ln_g0, ln_b0, HEADS, True), (W1, att_src1, att_dst1, bias1, ln_g1, ln_b1, HEADS, True), (W2, att_src2, att_dst2, bias2, ln_g2, ln_b2, 1, False)]
        h = x
        for i, (W, a_s, a_d, b, g, be, heads, concat) in enumerate(layers):
            h_new = _layernorm(_gat_conv(h, src, dst, W, a_s, a_d, b, heads, concat), g, be)
            if i > 0:
                h_new = h_new + h
            h = jax.nn.relu(h_new)
        return h

    def _L0_mix_ref(x, Wqkv, ln1_g, ln1_b, W1, b1, W2, b2, ln2_g, ln2_b):
        import jax, jax.numpy as jnp
        import numpy as np
        N, F, C, H = (32, 512, 256, 8)
        D = C // H
        EPS_ATTN = 1e-06
        EPS_LN = 1e-05

        def layer_norm(x, g, b):
            mu = jnp.mean(x, axis=-1, keepdims=True)
            var = jnp.var(x, axis=-1, keepdims=True)
            return (x - mu) * jax.lax.rsqrt(var + EPS_LN) * g + b
        n, f, c = x.shape
        qkv = jnp.einsum('nfc,oc->nfo', x, Wqkv)
        q, k, v = jnp.split(qkv, 3, axis=-1)
        q = q.reshape(n, f, H, D)
        k = k.reshape(n, f, H, D)
        v = v.reshape(n, f, H, D)
        q = jax.nn.elu(q) + 1.0
        k = jax.nn.elu(k) + 1.0
        kv = jnp.einsum('nshd,nshm->nhmd', k, v)
        ksum = jnp.sum(k, axis=1)
        z = 1.0 / (jnp.einsum('nlhd,nhd->nlh', q, ksum) + EPS_ATTN)
        t = jnp.einsum('nlhd,nhmd,nlh->nlhm', q, kv, z)
        t = t.reshape(n, f, c)
        x1 = layer_norm(t + x, ln1_g, ln1_b)
        h = jax.nn.gelu(jnp.einsum('nfc,oc->nfo', x1, W1) + b1, approximate=False)
        y = jnp.einsum('nfc,oc->nfo', h, W2) + b2
        return layer_norm(y + x1, ln2_g, ln2_b)

    def _L0_ffn_ref(x, gamma, beta, Wr, br, W1, b1, W2, b2):
        import jax, jax.numpy as jnp
        import numpy as np
        E = 8
        K = 2
        D = 256
        H = 512
        DOUT = 256
        EPS = 1e-05
        mu = jnp.mean(x, axis=-1, keepdims=True)
        var = jnp.mean(jnp.square(x - mu), axis=-1, keepdims=True)
        xn = (x - mu) * jax.lax.rsqrt(var + EPS) * gamma + beta
        logits = jnp.einsum('bsd,de->bse', xn, Wr) + br
        top_vals, top_idx = jax.lax.top_k(logits, K)
        w = jax.nn.softmax(top_vals, axis=-1)
        w_full = jnp.einsum('bsk,bske->bse', w, jax.nn.one_hot(top_idx, E, dtype=w.dtype))
        y = jnp.zeros(x.shape[:-1] + (DOUT,), x.dtype)
        for e in range(E):
            h = jax.nn.gelu(jnp.einsum('bsd,dh->bsh', xn, W1[e]) + b1[e], approximate=False)
            y_e = jnp.einsum('bsh,hd->bsd', h, W2[e]) + b2[e]
            y = y + y_e * w_full[..., e, None]
        return y
    edge_index = jnp.stack([src, dst])
    xn = _layernorm(x, axis=-1)
    x = x + _L0_gnn_ref(xn, edge_index, L0_gnn_W0, L0_gnn_att_src0, L0_gnn_att_dst0, L0_gnn_bias0, L0_gnn_ln_g0, L0_gnn_ln_b0, L0_gnn_W1, L0_gnn_att_src1, L0_gnn_att_dst1, L0_gnn_bias1, L0_gnn_ln_g1, L0_gnn_ln_b1, L0_gnn_W2, L0_gnn_att_src2, L0_gnn_att_dst2, L0_gnn_bias2, L0_gnn_ln_g2, L0_gnn_ln_b2) + _L0_mix_ref(xn[None], L0_mix_Wqkv, L0_mix_ln1_g, L0_mix_ln1_b, L0_mix_W1, L0_mix_b1, L0_mix_W2, L0_mix_b2, L0_mix_ln2_g, L0_mix_ln2_b)[0]
    x = x + _L0_ffn_ref(_layernorm(x, axis=-1)[None], L0_ffn_gamma, L0_ffn_beta, L0_ffn_Wr, L0_ffn_br, L0_ffn_W1, L0_ffn_b1, L0_ffn_W2, L0_ffn_b2)[0]
    return x

_drawn_inputs = setup_inputs


def setup_inputs(seed=0):
    import zlib

    import numpy as np

    out = dict(_drawn_inputs(seed))
    spreads = {'L0_gnn_bias0': (0.0, 0.1),
     'L0_gnn_ln_g0': (1.0, 0.2),
     'L0_gnn_ln_b0': (0.0, 0.1),
     'L0_gnn_bias1': (0.0, 0.1),
     'L0_gnn_ln_g1': (1.0, 0.2),
     'L0_gnn_ln_b1': (0.0, 0.1),
     'L0_gnn_bias2': (0.0, 0.1),
     'L0_gnn_ln_g2': (1.0, 0.2),
     'L0_gnn_ln_b2': (0.0, 0.1),
     'L0_mix_ln1_g': (1.0, 0.2),
     'L0_mix_ln1_b': (0.0, 0.1),
     'L0_mix_ln2_g': (1.0, 0.2),
     'L0_mix_ln2_b': (0.0, 0.1),
     'L0_ffn_br': (0.0, 0.342)}
    factors = {'L0_gnn_att_dst1': 5.868,
     'L0_gnn_att_src2': 3.795,
     'L0_gnn_att_dst2': 8.0,
     'L0_mix_Wqkv': 8.0,
     'L0_mix_b1': 8.0,
     'L0_mix_b2': 3.89,
     'L0_ffn_gamma': 8.0,
     'L0_ffn_beta': 8.0,
     'L0_ffn_Wr': 3.58,
     'L0_ffn_b1': 25.101,
     'L0_ffn_b2': 8.0}
    for name, (base, spread) in spreads.items():
        noise = np.random.default_rng([zlib.crc32(name.encode()), seed]).standard_normal(out[name].shape)
        drawn = base * np.exp(spread * noise) if base else spread * noise
        out[name] = jnp.asarray(drawn.astype(out[name].dtype))
    for name, factor in factors.items():
        out[name] = (out[name] * factor).astype(out[name].dtype)
    return out
```

```python
from contextlib import ExitStack

import concourse.bass as bass
from concourse import mybir

F32 = mybir.dt.float32
BF16 = mybir.dt.bfloat16
I32 = mybir.dt.int32
ALU = mybir.AluOpType
ACT = mybir.ActivationFunctionType
AX = mybir.AxisListType

P = 128
N = 6250
C = 256
E = 200000
NB = -(-N // P)
TAIL = N - (NB - 1) * P
NPAD = NB * P
H = 4
D = C // H
RW = C + H
GE = 2 * P
TG = -(-E // GE)
WG = 8
WS = 2 * WG
NW = 4 * (-(-(TG + NB - 1) // (4 * WG)))
NG = NW * WG
GC = -(-NG // P)
TC = -(-(TG + 1) // P)
BIG = float(2.0 ** 120)
SLOPE = 0.2
LN_EPS = 1e-5
RING = 4
ROWS_SEEN = "a node block is at most NB - 1, as the walk clamps it"


class Chain:

    def __init__(self, eng, sem, base=0):
        self.eng, self.sem, self.base, self.n = eng, sem, base, 0

    def add(self, ins):
        ins.then_inc(self.sem, 1)
        self.n += 1

    def wait(self):
        self.eng.wait_ge(self.sem, self.base + self.n)

    def link(self, ins):
        self.add(ins)
        self.wait()


def wait_apart(eng, sem, value, passed):
    eng.wait_ge(sem, value)
    eng.sem_inc(passed, 1)


class Phase:

    def __init__(self, nc, name):
        self.nc, self.name, self.ctx, self.sems = nc, name, ExitStack(), []

    def __enter__(self):
        self.ctx.__enter__()
        return self

    def __exit__(self, *a):
        done = self.ctx.__exit__(*a)
        self.nc.clear_and_free_semaphores(self.sems)
        self.nc.all_engine_barrier(sem_only=True)
        return done

    def sb(self, name, shape, dt=F32):
        return self.ctx.enter_context(self.nc.sbuf_tensor(f"{self.name}_{name}", shape, dt))

    def ps(self, name, shape, dt=F32):
        return self.ctx.enter_context(self.nc.psum_tensor(f"{self.name}_{name}", shape, dt))

    def sem(self, name):
        self.sems.append(self.nc.alloc_semaphore(f"{self.name}_{name}"))
        return self.sems[-1]

    def block(self):
        return self.ctx.enter_context(self.nc.Block())


def prepare_walk(nc, src, dst, st, dr):
    pad_rows = TG + 1
    with Phase(nc, "walk") as ph:
        pad = ph.sb("pad", [1, 2, pad_rows * GE - E], I32)
        dstI = ph.sb("dstI", [P, TC, GE], I32)
        dstF = ph.sb("dstF", [P, TC, GE])
        last_blk = ph.sb("last_blk", [P, TC])
        last_int = ph.sb("last_int", [P, TC], I32)
        threshold = ph.sb("threshold", [P, TC])
        passed = ph.sb("passed", [P, TC, GC * P], BF16)
        ones = ph.sb("ones", [P, P], BF16)
        iota_g = ph.sb("iota_g", [P, GC * P])
        iota_gp = ph.sb("iota_gp", [P, GC])
        grp = ph.sb("grp", [P, GC])
        grpI = ph.sb("grpI", [P, GC], I32)
        blk = ph.sb("blk", [P, GC])
        row_blk = ph.sb("row_blk", [P, GC * P])
        wordF = ph.sb("wordF", [P, NW, WG])
        wordS = ph.sb("wordS", [P, NW])
        pow2 = ph.sb("pow2", [P, WG])
        Dg = ph.sb("Dg", [P, GC, 2, P], I32)
        Sg = ph.sb("Sg", [P, GC, 2, P], I32)
        Df = ph.sb("Df", [P, GC, 2, P])
        Sf = ph.sb("Sf", [P, GC, 2, P])
        rel = ph.sb("rel", [P, GC, 2, P])
        last = ph.sb("last", [P, GC, 2, P])
        rst = ph.sb("rst", [P, GC, 2, P], BF16)
        ps_row = ph.ps("ps_row", [P, 2, 512])
        ps_col = ph.ps("ps_col", [P, 512])
        ps_tr = ph.ps("ps_tr", [P, 4, 512])

        pads_set = ph.sem("pads_set")
        edges_in = ph.sem("edges_in")
        pads_in = ph.sem("pads_in")
        dst_in = ph.sem("dst_in")
        iotas = ph.sem("iotas")
        dve = ph.sem("dve")
        compared = ph.sem("compared")
        walked = ph.sem("walked")
        index_ready = ph.sem("index_ready")
        dst_rows = ph.sem("dst_rows")
        src_rows = ph.sem("src_rows")
        rows_ready = ph.sem("rows_ready")
        turned = ph.sem("turned")
        copied = ph.sem("copied")
        reset_ready = ph.sem("reset_ready")
        reset_out = ph.sem("reset_out")
        pool = ph.sem("pool")
        block = ph.block()
        rowT = -(-NG // 2)
        assert rowT <= 512

        flat = dr["dst_pad"].rearrange("t e -> (t e)")
        flat_s = dr["src_pad"].rearrange("t e -> (t e)")

        @block.sync
        def _(sp):
            for to, of in ((flat, dst), (flat_s, src)):
                sp.dma_start(to[0:E].rearrange("(a b) -> a b", a=16),
                             of.rearrange("(a b) -> a b", a=16)).then_inc(edges_in, 16)
            sp.wait_ge(pads_set, 2)
            for n, to in enumerate((flat, flat_s)):
                sp.dma_start(to[E:pad_rows * GE].rearrange("(a b) -> a b", a=1), pad[:, n, :]).then_inc(pads_in, 16)
            sp.wait_ge(edges_in, 32)
            sp.wait_ge(pads_in, 32)
            sp.wait_ge(pool, 1)
            full = (TC - 1) * P
            sp.dma_start(dstI[:, 0:TC - 1, :], dr["dst_pad"][0:full, :].rearrange("(c p) e -> p c e", p=P)).then_inc(dst_in, 16)
            sp.dma_start(dstI[0:pad_rows - full, TC - 1, :], dr["dst_pad"][full:pad_rows, :]).then_inc(dst_in, 16)
            sp.wait_ge(reset_ready, 1)
            for c in range(GC):
                n = min(P, NG - c * P)
                for h in range(H):
                    sp.dma_start(dr["reset"][c * P:c * P + n, h, :, :], rst[0:n, c, :, :]).then_inc(reset_out, 16)
            sp.wait_ge(reset_out, 16 * GC * H)

        @block.gpsimd
        def _(g):
            g.memset(dstI[:, TC - 1, :], 0).then_inc(pool, 1)
            g.memset(pad[:, 0, :], -1).then_inc(pads_set, 1)
            g.memset(pad[:, 1, :], 0).then_inc(pads_set, 1)
            g.iota(iota_g[:, :], [[1, GC * P]], base=0, channel_multiplier=0,
                   allow_small_or_imprecise_dtypes=True).then_inc(iotas, 1)
            g.iota(iota_gp[:, :], [[P, GC]], base=0, channel_multiplier=1,
                   allow_small_or_imprecise_dtypes=True).then_inc(iotas, 1)
            g.iota(st["iota"][:, :], [[1, P]], base=0, channel_multiplier=0,
                   allow_small_or_imprecise_dtypes=True).then_inc(iotas, 1)
            g.memset(st["ident"][:, :], 0.0).then_inc(pool, 1)
            g.wait_ge(pool, 2)
            g.affine_select(out=st["ident"][:, :], in_=st["ident"][:, :], compare_op=ALU.not_equal, fill=1.0,
                            base=0, pattern=[[-1, P]], channel_multiplier=1).then_inc(iotas, 1)
            g.iota(threshold[:, :], [[P, TC]], base=1, channel_multiplier=1,
                   allow_small_or_imprecise_dtypes=True).then_inc(pool, 1)
            g.wait_ge(pool, 3)
            g.affine_select(out=threshold[:, :], in_=threshold[:, :], compare_op=ALU.is_ge, fill=1e6,
                            base=TG - 1, pattern=[[-P, TC]], channel_multiplier=-1).then_inc(iotas, 1)
            g.wait_ge(index_ready, 1)
            for c in range(GC):
                g.indirect_dma_start(Dg[:, c, :, :].rearrange("p a b -> p (a b)"), None, dr["dst_pad"],
                                     bass.IndirectOffsetOnAxis(grpI[:, c:c + 1], 0)).then_inc(dst_rows, 16)
                g.indirect_dma_start(Sg[:, c, :, :].rearrange("p a b -> p (a b)"), None, dr["src_pad"],
                                     bass.IndirectOffsetOnAxis(grpI[:, c:c + 1], 0)).then_inc(src_rows, 16)

        @block.vector
        def _(v):
            ch = Chain(v, dve)
            v.memset(ones[:, :], 1.0).then_inc(iotas, 1)
            for n in range(1, WG):
                ch.add(v.memset(pow2[:, n:n + 1], float(64 * 2 ** (n - 1))))
            v.wait_ge(dst_in, 32)
            ch.link(v.tensor_copy(dstF[:, :, :], dstI[:, :, :]))
            ch.link(v.tensor_reduce(last_blk[:, :], dstF[:, :, :], AX.X, ALU.max))
            ch.link(v.tensor_scalar(last_blk[:, :], last_blk[:, :], 0.0, None, ALU.max))
            ch.link(v.tensor_copy(last_int[:, :], last_blk[:, :]))
            ch.link(v.tensor_scalar(last_int[:, :], last_int[:, :], 7, None, ALU.arith_shift_right))
            ch.link(v.tensor_copy(last_blk[:, :], last_int[:, :]))
            v.wait_ge(iotas, 6)
            ch.link(v.tensor_tensor(threshold[:, :], threshold[:, :], last_blk[:, :], ALU.add))
            for c in range(TC):
                v.tensor_scalar(passed[:, c, :], iota_g[:, :], threshold[:, c:c + 1], None, ALU.is_ge).then_inc(compared, 1)
            v.wait_ge(walked, 1)
            ch.link(v.tensor_copy(grp[:, :], ps_col[:, 0:GC]))
            v.tensor_copy(grpI[:, :], grp[:, :]).then_inc(index_ready, 1)
            ch.link(v.tensor_tensor(blk[:, :], iota_gp[:, :], grp[:, :], ALU.subtract))
            ch.link(v.tensor_scalar(blk[:, :], blk[:, :], float(NB - 1), float(P), ALU.min, ALU.mult))
            for c in range(2):
                ch.add(v.tensor_tensor(row_blk[:, c * rowT:(c + 1) * rowT], iota_g[:, c * rowT:(c + 1) * rowT],
                                       ps_row[:, c, 0:rowT], ALU.subtract))
            ch.wait()
            ch.link(v.tensor_scalar(row_blk[:, 0:NG], row_blk[:, 0:NG], float(NB - 1), None, ALU.min))
            rb = row_blk[:, 0:NG].rearrange("p (w g) -> p w g", g=WG)
            ch.add(v.tensor_copy(wordF[:, :, 0:1], rb[:, :, 0:1]))
            ch.link(v.tensor_tensor(wordF[:, :, 1:WG], rb[:, :, 1:WG], rb[:, :, 0:WG - 1], ALU.subtract))
            ch.link(v.tensor_tensor(wordF[:, :, 1:WG], wordF[:, :, 1:WG],
                                    pow2[:, 1:WG].unsqueeze(1).broadcast_to([P, NW, WG - 1]), ALU.mult))
            ch.link(v.tensor_reduce(wordS[:, :], wordF[:, :, :], AX.X, ALU.add))
            ch.link(v.tensor_copy(st["words"][:, :], wordS[:, :]))
            v.wait_ge(dst_rows, 16 * GC)
            v.wait_ge(src_rows, 16 * GC)
            ch.add(v.tensor_copy(Df[:, :, :, :], Dg[:, :, :, :]))
            v.tensor_copy(Sf[:, :, :, :], Sg[:, :, :, :]).then_inc(rows_ready, 1)
            ch.add(v.memset(rst[:, :, :, 0:1], 0.0))
            ch.add(v.memset(last[:, :, :, P - 1:P], 1.0))
            ch.wait()
            for c in range(GC):
                v.tensor_scalar(rel[:, c, :, :], Df[:, c, :, :], blk[:, c:c + 1], None, ALU.subtract).then_inc(rows_ready, 1)
            v.tensor_tensor(last[:, :, :, 0:P - 1], Df[:, :, :, 0:P - 1], Df[:, :, :, 1:P], ALU.not_equal).then_inc(rows_ready, 1)
            v.wait_ge(rows_ready, 2 + GC)
            v.tensor_scalar(rst[:, :, :, 1:P], last[:, :, :, 0:P - 1], -BIG, None, ALU.mult).then_inc(reset_ready, 1)
            for c in range(GC):
                n = min(P, NG - c * P)
                v.wait_ge(turned, c + 1)
                for m, t in enumerate(("srcT", "relT", "lastT")):
                    for j in range(2):
                        o = (2 * m + j) * P
                        v.tensor_copy(st[t][:, c * P:c * P + n, j],
                                      ps_tr[:, 2 * (c % 2) + o // 512, o % 512:o % 512 + n]).then_inc(copied, 1)
            v.wait_ge(copied, 6 * GC)

        @block.tensor
        def _(pe):
            pe.wait_ge(iotas, 6)
            for c in range(TC):
                pe.wait_ge(compared, c + 1)
                for r in range(2):
                    pe.matmul(ps_row[:, r, 0:rowT], ones[:, :], passed[:, c, r * rowT:(r + 1) * rowT],
                              start=(c == 0), stop=(c == TC - 1))
            for m in range(GC):
                for c in range(TC):
                    mm = pe.matmul(ps_col[:, m:m + 1], passed[:, c, m * P:(m + 1) * P], ones[:, 0:1],
                                   start=(c == 0), stop=(c == TC - 1))
            mm.then_inc(walked, 1)
            pe.wait_ge(rows_ready, 2 + GC)
            for c in range(GC):
                if c >= 2:
                    pe.wait_ge(copied, 6 * (c - 1))
                for m, t in enumerate((Sf, rel, last)):
                    for j in range(2):
                        o = (2 * m + j) * P
                        mm = pe.transpose(ps_tr[:, 2 * (c % 2) + o // 512, o % 512:o % 512 + P],
                                          t[:, c, j, :], st["ident"][:, :])
                mm.then_inc(turned, 1)



def broadcast_row(vec):
    return vec.rearrange("(a n) -> a n", a=1).broadcast_to([P, vec.shape[0]])


def over_tiles(eng, step):
    step(0, 0, False)
    step(0, 1, False)
    with eng.Fori(1, (NB - 1) // 2) as i:
        step(i, 0, False)
        step(i, 1, False)
    step((NB - 1) // 2, 0, True)


def is_zero(i):
    return isinstance(i, int) and i == 0


def tile_rows(dram, i, half, last):
    if last:
        return dram[(NB - 1) * P:N, :]
    return dram[bass.ds((2 * i + half) * P, P), :]


def padded_rows(dram, i, half):
    return dram[bass.ds((2 * i + half) * P, P), :]


def node_phase(nc, layer, st, io, dr):
    first, final = layer == 0, layer == 3
    acc, ADM, own = st["acc"], st["ADM"], st["own"]
    with Phase(nc, f"node{layer}") as ph:
        X = ph.sb("X", [P, 2, C])
        rows = ph.sb("rows", [P, 2, RW])
        prev = ph.sb("prev", [P, 2, C])
        mix = ph.sb("mix", [P, 2, C])
        O = ph.sb("O", [P, 2, C])
        Hn = ph.sb("Hn", [P, 2, C])
        hT = ph.sb("hT", [P, 2, 2, P])
        ext = ph.sb("ext", [P, 2, RW])
        stats = ph.sb("stats", [P, 2, 6])
        mv = ph.sb("mv", [P, 2, 2])
        sd = ph.sb("sd", [P, 2, 1])
        rstd = ph.sb("rstd", [P, 2, 1])
        eps = ph.sb("eps", [P, 1])
        vecs = ph.sb("vecs", [P, 3, C])
        W = ph.sb("W", [P, 2, C])
        WT = ph.sb("WT", [P, 2, C])
        att = ph.sb("att", [P, 2, 2 * H])
        Wx = ph.sb("Wx", [P, 2, RW + H])
        tu = ph.sb("tu", [P, 2, NB * H])
        lr = ph.sb("lr", [P, 2, NB * H])
        es = ph.sb("es", [P, NB, H])
        zr = ph.sb("zr", [P, NB, H])
        psA = [ph.ps(f"psA{k}", [P, 512]) for k in range(2)]
        psB = [ph.ps(f"psB{k}", [P, 512]) for k in range(2)]
        psW = ph.ps("psW", [P, 512])
        psS = ph.ps("psS", [P, 512])

        consts = ph.sem("consts")
        att_clear = ph.sem("att_clear")
        vecs_in = ph.sem("vecs_in")
        weights_in = ph.sem("weights_in")
        w_turned = ph.sem("w_turned")
        wT_ready = ph.sem("wT_ready")
        w_scored = ph.sem("w_scored")
        wx_ready = ph.sem("wx_ready")
        pre = ph.sem("pre")
        es_ready = ph.sem("es_ready")
        loaded = [ph.sem(f"loaded{k}") for k in range(2)]
        chain1 = ph.sem("chain1")
        chain2 = ph.sem("chain2")
        passed = ph.sem("passed")
        stats_ready = ph.sem("stats_ready")
        sd_ready = ph.sem("sd_ready")
        h_ready = ph.sem("h_ready")
        turned = ph.sem("turned")
        hT_ready = ph.sem("hT_ready")
        projected = ph.sem("projected")
        ext_ready = ph.sem("ext_ready")
        h_out = [ph.sem(f"h_out{k}") for k in range(2)]
        ext_out = [ph.sem(f"ext_out{k}") for k in range(2)]
        block = ph.block()

        loads = (first or final) + (not first) + (layer >= 2) + final
        if not final:
            W_dram, a_src, a_dst = io[f"W{layer}"], io[f"att_src{layer}"], io[f"att_dst{layer}"]
            heads = a_src.shape[0]
        n_att = 0 if final else (2 * H if heads == H else 2 * 2 * H)

        def head_view(ap):
            return ap.rearrange("p (h f) -> p h f", h=H)[:, :, 0:D]

        def by_head(ap):
            return ap.rearrange("p (h f) -> p h f", h=H)

        @block.sync
        def _(sp):
            if not first:
                for n, name in enumerate(("bias", "ln_g", "ln_b")):
                    sp.dma_start(vecs[:, n, :], broadcast_row(io[f"{name}{layer - 1}"])).then_inc(vecs_in, 16)
            if not final:
                sp.dma_start(W[:, :, :], W_dram.rearrange("(k p) o -> p k o", p=P)).then_inc(weights_in, 16)
                sp.wait_ge(att_clear, 1)
                for n, a in enumerate((a_src, a_dst)):
                    if heads == H:
                        for h in range(H):
                            o = (h * D) % P
                            sp.dma_start(att[o:o + D, h * D // P, n * H + h:n * H + h + 1],
                                         a[h:h + 1, :].rearrange("a d -> d a")).then_inc(weights_in, 16)
                    else:
                        for k in range(2):
                            for h in range(H):
                                sp.dma_start(att[:, k, n * H + h:n * H + h + 1],
                                             a[0:1, k * P:(k + 1) * P].rearrange("a d -> d a")).then_inc(weights_in, 16)

            def load(i, half, last):
                n = slice(0, TAIL) if last else slice(0, P)
                if first or final:
                    sp.dma_start(X[n, half, :], tile_rows(io["x"], i, half, last)).then_inc(loaded[half], 16)
                if not first:
                    sp.dma_start(rows[:, half, :], padded_rows(dr["rows"], i, half)).then_inc(loaded[half], 16)
                if layer >= 2:
                    sp.dma_start(prev[:, half, :], padded_rows(dr["h"], i, half)).then_inc(loaded[half], 16)
                if final:
                    sp.dma_start(mix[:, half, :], padded_rows(dr["mix"], i, half)).then_inc(loaded[half], 16)

            load(0, 0, False)
            load(0, 1, False)
            with sp.Fori(1, (NB - 1) // 2) as i:
                sp.wait_ge(h_ready, 2 * i)
                load(i, 0, False)
                sp.wait_ge(h_ready, 2 * i + 1)
                load(i, 1, False)
            sp.wait_ge(h_ready, NB - 1)
            load((NB - 1) // 2, 0, True)

        @block.gpsimd
        def _(g):
            g.memset(att[:, :, :], 0.0).then_inc(att_clear, 1)
            g.memset(eps[:, :], LN_EPS).then_inc(consts, 1)
            if first:
                g.memset(acc[:, :, :], 0.0).then_inc(consts, 1)

            def step(i, half, last):
                b = 2 * i + half
                g.wait_ge(h_ready, b + 2)
                to = "x2" if final else "h"
                g.dma_start(padded_rows(dr[to], i, half), Hn[:, half, :]).then_inc(h_out[half], 16)
                if not final:
                    g.wait_ge(ext_ready, b + 3)
                    g.dma_start(padded_rows(dr["rows"], i, half), ext[:, half, :]).then_inc(ext_out[half], 16)

            over_tiles(g, step)
            if not first and not final:
                g.memset(acc[:, :, :], 0.0).then_inc(consts, 1)
            for half in range(2):
                n = NB // 2 + (half == 0)
                g.wait_ge(h_out[half], 16 * n)
                if not final:
                    g.wait_ge(ext_out[half], 16 * n)

        @block.vector
        def _(v):
            v.sem_inc(h_ready, 1)
            c0 = Chain(v, pre)
            if not final:
                v.wait_ge(w_turned, 1)
                v.tensor_copy(WT[:, :, :].rearrange("p a b -> p (a b)"), psW[:, :]).then_inc(wT_ready, 1)
                v.wait_ge(w_scored, 1)
                for k in range(2):
                    for n in range(2):
                        sc = psS[:, k * 2 * H + n * H:k * 2 * H + (n + 1) * H]
                        if n:
                            v.tensor_copy(Wx[:, k, RW:RW + H], sc).then_inc(wx_ready, 1)
                        else:
                            v.tensor_copy(by_head(Wx[:, k, 0:RW])[:, :, D], sc).then_inc(wx_ready, 1)
                    v.tensor_copy(head_view(Wx[:, k, 0:RW]), by_head(W[:, k, :])).then_inc(wx_ready, 1)
            if not first:
                as_, ad_, ms_ = own[:, :, :], ADM[:, :, 0:H], ADM[:, :, H:2 * H]
                tv = [tu[:, k, :].rearrange("p (b h) -> p b h", h=H) for k in range(2)]
                c0.add(v.tensor_tensor(tv[0], as_, ad_, ALU.add))
                c0.link(v.tensor_tensor(tv[1], ms_, ad_, ALU.add))
                c0.link(v.scalar_tensor_tensor(out=lr[:, :, :], in0=tu[:, :, :], scalar=SLOPE, in1=tu[:, :, :],
                                               op0=ALU.mult, op1=ALU.max))
                c0.link(v.tensor_tensor(tu[:, 0, :], lr[:, 0, :], lr[:, 1, :], ALU.subtract))
                v.wait_ge(es_ready, 1)
                sums = acc[:, :, :].rearrange("p b (h f) -> p b h f", h=H)[:, :, :, D]
                c0.link(v.tensor_tensor(zr[:, :, :], sums, es[:, :, :], ALU.add))
                c0.link(v.tensor_scalar(zr[:, :, :], zr[:, :, :], 1e-16, None, ALU.add))
                c0.link(v.reciprocal(zr[:, :, :], zr[:, :, :]))
                v.wait_ge(vecs_in, 48)

            N1 = 1 if first else 5
            N2 = 1 if first else 3 + (layer >= 2) + final

            def gather_in(i, half, last):
                b = 2 * i + half
                ch = Chain(v, chain1, b * N1)
                v.wait_ge(loaded[half], 16 * loads * (i + 1))
                if first:
                    o = X[:, half, :]
                else:
                    o = O[:, half, :]
                    oh = by_head(o)
                    a = acc[:, bass.ds(b, 1), :].rearrange("p a (h f) -> p (a h) f", h=H)[:, :, 0:D]
                    e = es[:, bass.ds(b, 1), :].rearrange("p a h -> p (a h)").unsqueeze(2).broadcast_to([P, H, D])
                    z = zr[:, bass.ds(b, 1), :].rearrange("p a h -> p (a h)").unsqueeze(2).broadcast_to([P, H, D])
                    ch.link(v.tensor_tensor(oh, head_view(rows[:, half, :]), e, ALU.mult))
                    ch.link(v.tensor_tensor(oh, oh, a, ALU.add))
                    ch.link(v.tensor_tensor(oh, oh, z, ALU.mult))
                    ch.link(v.tensor_tensor(o, o, vecs[:, 0, :], ALU.add))
                ch.add(v.bn_stats(stats[:, half, :], o))
                wait_apart(v, chain1, ch.base + ch.n, passed)
                v.bn_aggr(mv[:, half, :], stats[:, half, :]).then_inc(stats_ready, 1)
                assert ch.n == N1

            def finish(i, half, last):
                b = 2 * i + half
                ch = Chain(v, chain2, b * N2)
                o = X[:, half, :] if first else O[:, half, :]
                hn = Hn[:, half, :]
                v.wait_ge(sd_ready, b + 1)
                ch.link(v.reciprocal(rstd[:, half, :], sd[:, half, :]))
                if not is_zero(i):
                    v.wait_ge(h_out[half], 16 * i)
                if not final:
                    v.wait_ge(turned, b + 1)
                if first:
                    v.tensor_scalar(hn, o, mv[:, half, 0:1], rstd[:, half, :], ALU.subtract, ALU.mult).then_inc(h_ready, 1)
                else:
                    ch.link(v.scalar_tensor_tensor(out=o, in0=o, scalar=mv[:, half, 0:1], in1=vecs[:, 1, :],
                                                   op0=ALU.subtract, op1=ALU.mult))
                    ch.link(v.scalar_tensor_tensor(out=o, in0=o, scalar=rstd[:, half, :], in1=vecs[:, 2, :],
                                                   op0=ALU.mult, op1=ALU.add))
                    if layer >= 2:
                        ch.link(v.tensor_tensor(o, o, prev[:, half, :], ALU.add))
                    if final:
                        ch.link(v.scalar_tensor_tensor(out=o, in0=o, scalar=0.0, in1=X[:, half, :],
                                                       op0=ALU.max, op1=ALU.add))
                        v.tensor_tensor(hn, o, mix[:, half, :], ALU.add).then_inc(h_ready, 1)
                    else:
                        v.tensor_scalar(hn, o, 0.0, None, ALU.max).then_inc(h_ready, 1)
                assert ch.n == N2

            gather_in(0, 0, False)

            def step(i, half, last):
                if not last:
                    v.wait_ge(h_ready, 2 * i + half + 1)
                    gather_in(i + half, 1 - half, False)
                finish(i, half, last)

            over_tiles(v, step)

        @block.scalar
        def _(a):
            a.wait_ge(consts, 1 + first)
            if not final:
                for s in (hT_ready, ext_ready):
                    a.sem_inc(s, 2)
            if not first:
                a.wait_ge(pre, 4)
                a.activation(es[:, :, :], tu[:, 0, :].rearrange("p (b h) -> p b h", h=H), ACT.Exp).then_inc(es_ready, 1)

            def std(half, b):
                a.wait_ge(stats_ready, b + 1)
                a.activation(sd[:, half, :], mv[:, half, 1:2], ACT.Sqrt, bias=eps[:, :]).then_inc(sd_ready, 1)

            std(0, 0)

            def step(i, half, last):
                b = 2 * i + half
                if not last:
                    std(1 - half, b + 1)
                if final:
                    return
                a.wait_ge(turned, b + 3)
                a.wait_ge(projected, b + 1)
                a.activation(hT[:, half, :, :].rearrange("p a b -> p (a b)"), psA[half][:, 0:C], ACT.Copy).then_inc(hT_ready, 1)
                a.wait_ge(projected, b + 3)
                if not is_zero(i):
                    a.wait_ge(ext_out[half], 16 * i)
                scores = by_head(psB[half][:, 0:RW])[:, :, D]
                a.activation(ADM[:, bass.ds(b, 1), 0:H].rearrange("p a h -> p (a h)"), psB[half][:, RW:RW + H], ACT.Copy)
                a.activation(ADM[:, bass.ds(b, 1), H:2 * H].rearrange("p a h -> p (a h)"), scores, ACT.Copy)
                a.activation(own[:, bass.ds(b, 1), :].rearrange("p a h -> p (a h)"), scores, ACT.Copy)
                a.activation(ext[:, half, :], psB[half][:, 0:RW], ACT.Copy).then_inc(ext_ready, 1)

            over_tiles(a, step)

        @block.tensor
        def _(pe):
            if final:
                return
            pe.sem_inc(turned, 2)
            pe.sem_inc(projected, 2)
            pe.wait_ge(weights_in, 16 * (1 + n_att))
            for k in range(2):
                for o in range(2):
                    mm = pe.transpose(psW[:, (o * 2 + k) * P:(o * 2 + k + 1) * P], W[:, k, o * P:(o + 1) * P], st["ident"][:, :])
            mm.then_inc(w_turned, 1)
            pe.wait_ge(wT_ready, 1)
            for k in range(2):
                for o in range(2):
                    mm = pe.matmul(psS[:, k * 2 * H:(k + 1) * 2 * H], WT[:, o, k * P:(k + 1) * P], att[:, o, :],
                                   start=(o == 0), stop=(o == 1))
            mm.then_inc(w_scored, 1)
            pe.wait_ge(wx_ready, 6)

            def step(i, half, last):
                b = 2 * i + half
                pe.wait_ge(h_ready, b + 2)
                pe.wait_ge(hT_ready, b + 1)
                for k in range(2):
                    mm = pe.transpose(psA[half][:, k * P:(k + 1) * P], Hn[:, half, k * P:(k + 1) * P], st["ident"][:, :])
                mm.then_inc(turned, 1)
                pe.wait_ge(hT_ready, b + 3)
                pe.wait_ge(ext_ready, b + 1)
                for k in range(2):
                    mm = pe.matmul(psB[half][:, 0:RW + H], hT[:, half, k, :], Wx[:, k, :], start=(k == 0), stop=(k == 1))
                mm.then_inc(projected, 1)

            over_tiles(pe, step)


def edge_phase(nc, layer, st, dr):
    acc, ADM, ident, iota = st["acc"], st["ADM"], st["ident"], st["iota"]
    srcT, relT, lastT, words = (st[n] for n in ("srcT", "relT", "lastT", "words"))
    S3 = WS * H
    with Phase(nc, f"edges{layer}") as ph:
        G = [ph.sb(f"G{r}", [P, WS, RW]) for r in range(RING)]
        index = [ph.sb(f"index{r}", [P, WS], I32) for r in range(RING)]
        reset = ph.sb("reset", [S3, RING, P], BF16)
        OH = [ph.sb(f"OH{k}", [P, WS, P]) for k in range(2)]
        OHT = [ph.sb(f"OHT{k}", [P, WS, P]) for k in range(2)]
        score = [ph.sb(f"score{k}", [P, S3]) for k in range(2)]
        run = ph.sb("run", [S3, P])
        lastv = ph.sb("lastv", [P, WS, H + 1])
        absent = ph.sb("absent", [P, WS])
        seg = ph.sb("seg", [P, WS, H])
        segm = ph.sb("segm", [P, WG, H])
        adv = ph.sb("adv", [P, S3])
        tu = ph.sb("tu", [P, 2, S3])
        lr = ph.sb("lr", [P, 2, S3])
        diff = ph.sb("diff", [P, S3])
        old = ph.sb("old", [P, 2, H])
        fl = ph.sb("fl", [P, 2, H])
        fd = ph.sb("fd", [P, H])
        fade = ph.sb("fade", [P, H])
        ps_s = ph.ps("ps_s", [P, 512])
        ps_t = [ph.ps(f"ps_t{k}", [P, 512]) for k in range(2)]
        ps_seg = ph.ps("ps_seg", [P, WS, 8])
        ps_ad = ph.ps("ps_ad", [P, WS, 8])
        ps_o = [ph.ps(f"ps_o{k}", [P, 512]) for k in range(2)]

        index_ready = ph.sem("index_ready")
        gathered = [ph.sem(f"gathered{r}") for r in range(RING)]
        reset_in = [ph.sem(f"reset_in{r}") for r in range(RING)]
        score_ready = ph.sem("score_ready")
        score_turned = ph.sem("score_turned")
        ran = ph.sem("ran")
        run_turned = ph.sem("run_turned")
        lastv_ready = ph.sem("lastv_ready")
        oh_ready = ph.sem("oh_ready")
        oh_turned = ph.sem("oh_turned")
        oht_ready = ph.sem("oht_ready")
        seg_ready = ph.sem("seg_ready")
        max_ready = ph.sem("max_ready")
        ad_ready = ph.sem("ad_ready")
        diff_ready = ph.sem("diff_ready")
        weights_ready = ph.sem("weights_ready")
        fd_ready = ph.sem("fd_ready")
        fade_ready = ph.sem("fade_ready")
        weighed = ph.sem("weighed")
        summed = ph.sem("summed")
        added = ph.sem("added")
        chain_a = ph.sem("chain_a")
        chain_m = ph.sem("chain_m")
        chain_f = ph.sem("chain_f")
        chain_d = ph.sem("chain_d")
        passed = ph.sem("passed")
        passed_pool = ph.sem("passed_pool")
        faded = ph.sem("faded")
        block = ph.block()

        def by_head(ap):
            return ap.rearrange("p s (h f) -> p s h f", h=H)

        def ghj(ap):
            return ap.rearrange("p (g j) h -> p g h j", j=2)

        def as_ghj(ap):
            return ap.rearrange("p (g h j) -> p g h j", h=H, j=2)

        def over_windows(eng, step):
            with eng.Fori(0, NW // RING - 1) as i:
                for r in range(RING):
                    step(i, r, False)
            for r in range(RING):
                step(NW // RING - 1, r, r == RING - 1)

        def blocks_of(eng, w):
            word = eng.value_load(words[0:1, bass.ds(w, 1)], min_val=0, max_val=64 * 2 ** (WG - 1) - 1)
            b = eng.snap(word & 63)
            for g in range(WG):
                b = nc.s_assert_within(b, 0, NB - 1, skip_runtime_bounds_check_because=ROWS_SEEN)
                yield b
                if g < WG - 1:
                    b = eng.snap(b + ((word >> (6 + g)) & 1))

        @block.sync
        def _(sp):
            def step(i, r, last):
                w = 4 * i + r
                sp.wait_ge(ran, w + 1)
                sp.dma_start(reset[:, r, :], dr["reset"].rearrange("g h j e -> (g h j) e")[bass.ds(w * S3, S3), :]
                             ).then_inc(reset_in[r], 16)

            over_windows(sp, step)

        @block.gpsimd
        def _(g):
            def step(i, r, last):
                w = 4 * i + r
                g.wait_ge(index_ready, w + 1)
                wait_apart(g, summed, WG * (w + 1), passed_pool)
                for s in range(WS):
                    g.indirect_dma_start(G[r][:, s, :], None, dr["rows"],
                                         bass.IndirectOffsetOnAxis(index[r][:, s:s + 1], 0)).then_inc(gathered[r], 16)

            over_windows(g, step)

        @block.scalar
        def _(a):
            a.sem_inc(oht_ready, 2)
            a.sem_inc(score_ready, 2)

            def make_index(w, r, i):
                if i is not None:
                    a.wait_ge(gathered[r], 16 * WS * i)
                a.activation(index[r][:, :], srcT[:, bass.ds(w * WG, WG), :].rearrange("p g j -> p (g j)"), ACT.Copy
                             ).then_inc(index_ready, 1)

            def first_stage(w, i, r):
                k = r % 2
                for c in range(4):
                    a.wait_ge(oh_turned, 4 * w + c + 1)
                    if c == 0:
                        a.wait_ge(ad_ready, w + 1)
                    a.activation(OHT[k][:, 4 * c:4 * c + 4, :].rearrange("p s e -> p (s e)"), ps_t[c % 2][:, :], ACT.Copy
                                 ).then_inc(oht_ready, 1)
                a.wait_ge(gathered[r], 16 * WS * (i + 1))
                a.wait_ge(diff_ready, w + 1)
                a.activation(as_ghj(score[k][:, :]), ghj(by_head(G[r][:, :, :])[:, :, :, D]), ACT.Copy
                             ).then_inc(score_ready, 1)

            def weigh(w, r):
                a.wait_ge(diff_ready, w + 3)
                a.activation(ghj(by_head(G[r][:, :, :])[:, :, :, D]), as_ghj(diff[:, :]), ACT.Exp).then_inc(weights_ready, 1)
                a.wait_ge(fd_ready, w + 1)
                a.wait_ge(faded, w)
                a.activation(fade[:, :], fd[:, :], ACT.Exp).then_inc(fade_ready, 1)

            for r in range(RING):
                make_index(r, r, None)
            first_stage(0, 0, 0)
            weigh(0, 0)

            def step(i, r, last):
                w = 4 * i + r
                n = (r + 1) % RING
                if not isinstance(i, int):
                    make_index(w + RING, r, i + 1)
                if not last:
                    first_stage(w + 1, i + (r + 1) // RING, n)
                    weigh(w + 1, n)

            over_windows(a, step)

        @block.tensor
        def _(pe):
            pe.sem_inc(summed, WG * RING)
            pe.sem_inc(ad_ready, 2)

            def turn_onehots(w, r):
                for c in range(4):
                    pe.wait_ge(oh_ready, 4 * w + c + 1)
                    pe.wait_ge(oht_ready, 4 * w + c + 1)
                    for s in range(4):
                        mm = pe.transpose(ps_t[c % 2][:, s * P:(s + 1) * P], OH[r % 2][:, 4 * c + s, :], ident[:, :])
                    mm.then_inc(oh_turned, 1)

            def turn_scores(w, r):
                pe.wait_ge(score_ready, w + 3)
                wait_apart(pe, ran, w + RING, passed)
                pe.transpose(ps_s[0:S3, 0:P], score[r % 2][:, :], ident[:, :]).then_inc(score_turned, 1)

            def turn_run(w):
                pe.wait_ge(ran, w + 1 + RING)
                wait_apart(pe, lastv_ready, w, passed)
                pe.transpose(ps_s[:, 256:256 + S3], run[:, :], ident[0:S3, 0:S3]).then_inc(run_turned, 1)

            def segments(w, r):
                pe.wait_ge(lastv_ready, w + 1)
                for s in range(WS):
                    mm = pe.matmul(ps_seg[:, s, 0:H + 1], OH[r % 2][:, s, :], lastv[:, s, :], start=True, stop=True)
                mm.then_inc(seg_ready, 1)

            def spread(w, r):
                for g, b in enumerate(blocks_of(pe, w)):
                    if g == 0:
                        pe.wait_ge(oht_ready, 4 * w + 6)
                        pe.wait_ge(max_ready, w + 1)
                        pe.wait_ge(diff_ready, w + 2)
                    for j in range(2):
                        s = 2 * g + j
                        mm = pe.matmul(ps_ad[:, s, :], OHT[r % 2][:, s, :],
                                       ADM[:, bass.ds(b, 1), :].rearrange("p a x -> p (a x)"), start=True, stop=True)
                mm.then_inc(ad_ready, 1)

            def sums(w, r, groups):
                for g in groups:
                    if g % 2 == 0:
                        pe.wait_ge(weighed, 4 * w + g // 2 + 1)
                    pe.wait_ge(added, WG * w + g + 1)
                    for j in range(2):
                        mm = pe.matmul(ps_o[g % 2][:, 0:RW], OH[r % 2][:, 2 * g + j, :], G[r][:, 2 * g + j, :],
                                       start=(j == 0), stop=(j == 1))
                    mm.then_inc(summed, 1)

            turn_onehots(0, 0)
            turn_scores(0, 0)
            turn_run(0)
            segments(0, 0)
            spread(0, 0)

            def step(i, r, last):
                w = 4 * i + r
                n = (r + 1) % RING
                sums(w, r, range(0, 2))
                if not last:
                    turn_onehots(w + 1, n)
                    turn_scores(w + 1, n)
                sums(w, r, range(2, 5))
                if not last:
                    turn_run(w + 1)
                sums(w, r, range(5, 6))
                if not last:
                    segments(w + 1, n)
                sums(w, r, range(6, WG))
                if not last:
                    spread(w + 1, n)

            over_windows(pe, step)

        @block.vector
        def _(v):
            v.sem_inc(ran, RING)
            v.sem_inc(diff_ready, 2)
            v.sem_inc(added, 2)

            def onehots(w, r, c):
                v.wait_ge(summed, WG * w + WG * (RING - 1))
                rel = relT[:, bass.ds(w * WG + 2 * c, 2), :].rearrange("p g j -> p (g j)")
                v.tensor_tensor(OH[r % 2][:, 4 * c:4 * c + 4, :], iota[:, :].unsqueeze(1).broadcast_to([P, 4, P]),
                                rel.unsqueeze(2).broadcast_to([P, 4, P]), ALU.is_equal).then_inc(oh_ready, 1)

            def scan(w, i, r):
                v.wait_ge(score_turned, w + 1)
                v.wait_ge(reset_in[r], 16 * (i + 1))
                v.wait_ge(run_turned, w)
                v.tensor_tensor_scan(run[:, :], reset[:, r, :], ps_s[0:S3, 0:P], -BIG, ALU.add, ALU.max).then_inc(ran, 1)

            def last_values(w):
                v.wait_ge(run_turned, w + 1)
                v.wait_ge(seg_ready, w)
                ls = lastT[:, bass.ds(w * WG, WG), :]
                v.tensor_copy(lastv[:, :, H], ls.rearrange("p g j -> p (g j)")).then_inc(chain_a, 1)
                for h in range(H):
                    ins = v.tensor_tensor(lastv[:, :, h].rearrange("p (g j) -> p g j", j=2),
                                          as_ghj(ps_s[:, 256:256 + S3])[:, :, h, :], ls, ALU.mult)
                    ins.then_inc(*((lastv_ready, 1) if h == H - 1 else (chain_a, 1)))

            def segment_max(w):
                ch = Chain(v, chain_a, (H + 2) * w + H)
                v.wait_ge(seg_ready, w + 1)
                ch.link(v.tensor_scalar(absent[:, :], ps_seg[:, :, H], 1.0, BIG, ALU.subtract, ALU.mult))
                ch.link(v.tensor_tensor(seg[:, :, :], ps_seg[:, :, 0:H], absent[:, :].unsqueeze(2).broadcast_to([P, WS, H]), ALU.add))
                assert ch.n == 2

            def block_row(ap, b):
                return ap[:, bass.ds(b, 1), :].rearrange("p a h -> p (a h)")

            def maxima_begin(w, b):
                ch = Chain(v, chain_m, (WG + 5) * w)
                pair = seg[:, :, :].rearrange("p (g j) h -> p g j h", j=2)
                ch.add(v.tensor_tensor(old[:, 0, :], block_row(ADM[:, :, H:2 * H], b), block_row(ADM[:, :, 0:H], b), ALU.add))
                ch.link(v.tensor_tensor(segm[:, :, :], pair[:, :, 0, :], pair[:, :, 1, :], ALU.max))
                return ch

            def maximum(g, b, ch):
                if g > 0:
                    ch.wait()
                ms = block_row(ADM[:, :, H:2 * H], b)
                ins = v.tensor_tensor(ms, ms, segm[:, g, :], ALU.max)
                if g == WG - 1:
                    ins.then_inc(max_ready, 1)
                else:
                    ch.add(ins)

            def fading(w, b):
                ch = Chain(v, chain_f, 2 * w)
                v.wait_ge(max_ready, w + 1)
                ch.link(v.tensor_tensor(old[:, 1, :], block_row(ADM[:, :, H:2 * H], b), block_row(ADM[:, :, 0:H], b), ALU.add))
                ch.link(v.scalar_tensor_tensor(out=fl[:, :, :], in0=old[:, :, :], scalar=SLOPE, in1=old[:, :, :],
                                               op0=ALU.mult, op1=ALU.max))
                v.wait_ge(fade_ready, w)
                v.tensor_tensor(fd[:, :], fl[:, 0, :], fl[:, 1, :], ALU.subtract).then_inc(fd_ready, 1)

            def spread_terms(w, r):
                ch = Chain(v, chain_m, (WG + 5) * w + WG + 1)
                v.wait_ge(ad_ready, w + 3)
                ad, ms = ghj(ps_ad[:, :, 0:H]), ghj(ps_ad[:, :, H:2 * H])
                ch.add(v.tensor_copy(as_ghj(adv[:, :]), ad))
                ch.link(v.tensor_tensor(as_ghj(tu[:, 0, :]), as_ghj(score[r % 2][:, :]), ad, ALU.add))
                ch.link(v.tensor_tensor(as_ghj(tu[:, 1, :]), ms, as_ghj(adv[:, :]), ALU.add))
                ch.link(v.scalar_tensor_tensor(out=lr[:, :, :], in0=tu[:, :, :], scalar=SLOPE, in1=tu[:, :, :],
                                               op0=ALU.mult, op1=ALU.max))
                assert ch.n == 4
                v.wait_ge(weights_ready, w)
                v.tensor_tensor(diff[:, :], lr[:, 0, :], lr[:, 1, :], ALU.subtract).then_inc(chain_d, 1)
                v.wait_ge(chain_d, w + 1)
                v.tensor_scalar(diff[:, :], diff[:, :], 0.0, None, ALU.min).then_inc(diff_ready, 1)

            def weigh(w, r, c):
                v.wait_ge(weights_ready, w + 1)
                g4 = G[r][:, 4 * c:4 * c + 4, :].rearrange("p s (h f) -> p (s h) f", h=H)
                v.tensor_tensor(g4[:, :, 0:D], g4[:, :, 0:D], g4[:, :, D:D + 1].broadcast_to([P, 4 * H, D]), ALU.mult
                                ).then_inc(weighed, 1)

            def fade_sums(w, b):
                v.wait_ge(fade_ready, w + 1)
                v.wait_ge(added, WG * w + 2)
                a = block_row(acc, b).rearrange("p (h f) -> p h f", h=H)
                v.tensor_tensor(a, a, fade[:, :].unsqueeze(2).broadcast_to([P, H, D + 1]), ALU.mult).then_inc(faded, 1)

            def add(w, g, b):
                v.wait_ge(summed, WG * w + g + 1 + WG * RING)
                if g == 0:
                    v.wait_ge(faded, w + 1)
                else:
                    v.wait_ge(added, WG * w + g + 2)
                a = block_row(acc, b)
                v.tensor_tensor(a, a, ps_o[g % 2][:, 0:RW], ALU.add).then_inc(added, 1)

            for w in range(2):
                for c in range(4):
                    onehots(w, w, c)
            scan(0, 0, 0)
            last_values(0)
            segment_max(0)
            for g, b in enumerate(blocks_of(v, 0)):
                if g == 0:
                    b0 = b
                    ch = maxima_begin(0, b)
                maximum(g, b, ch)
            fading(0, b0)
            spread_terms(0, 0)

            def step(i, r, last):
                w = 4 * i + r
                n = (r + 1) % RING
                more = not (isinstance(i, int) and r >= 2)
                weigh(w, r, 0)
                weigh(w, r, 1)
                this = blocks_of(v, w)
                b = next(this)
                fade_sums(w, b)
                add(w, 0, b)
                add(w, 1, next(this))
                weigh(w, r, 2)
                add(w, 2, next(this))
                weigh(w, r, 3)
                add(w, 3, next(this))
                if not last:
                    scan(w + 1, i + (r + 1) // RING, n)
                add(w, 4, next(this))
                if not last:
                    last_values(w + 1)
                add(w, 5, next(this))
                if not last:
                    segment_max(w + 1)
                add(w, 6, next(this))
                b = next(this)
                if last:
                    add(w, 7, b)
                    return
                following = blocks_of(v, w + 1)
                b0 = next(following)
                ch = maxima_begin(w + 1, b0)
                maximum(0, b0, ch)
                add(w, 7, b)
                for g, b in enumerate(following, 1):
                    maximum(g, b, ch)
                fading(w + 1, b0)
                if more:
                    onehots(w + 2, r, 0)
                    onehots(w + 2, r, 1)
                spread_terms(w + 1, n)
                if more:
                    onehots(w + 2, r, 2)
                    onehots(w + 2, r, 3)

            over_windows(v, step)
            v.wait_ge(added, WG * NW + 2)


def normalize_tiles(nc, name, buf, gain, offset):
    with Phase(nc, name) as ph:
        stats = ph.sb("stats", [P, NB, 6])
        mv = ph.sb("mv", [P, NB, 2])
        sd = ph.sb("sd", [P, NB])
        rstd = ph.sb("rstd", [P, NB])
        eps = ph.sb("eps", [P, 1])
        vecs = ph.sb("vecs", [P, 2, C])
        eps_set = ph.sem("eps_set")
        vecs_in = ph.sem("vecs_in")
        stats_done = ph.sem("stats_done")
        moments = ph.sem("moments")
        sd_ready = ph.sem("sd_ready")
        rstd_ready = ph.sem("rstd_ready")
        centred = ph.sem("centred")
        scaled = ph.sem("scaled")
        block = ph.block()

        def tile(t, b):
            return t[:, bass.ds(b, 1), :].rearrange("p a c -> p (a c)")

        @block.sync
        def _(sp):
            if gain is not None:
                for n, vec in enumerate((gain, offset)):
                    sp.dma_start(vecs[:, n, :], broadcast_row(vec)).then_inc(vecs_in, 16)

        @block.gpsimd
        def _(g):
            g.memset(eps[:, :], LN_EPS).then_inc(eps_set, 1)

        @block.scalar
        def _(a):
            a.wait_ge(eps_set, 1)
            a.wait_ge(moments, NB)
            a.activation(sd[:, :], mv[:, :, 1], ACT.Sqrt, bias=eps[:, :]).then_inc(sd_ready, 1)

        @block.vector
        def _(v):
            with v.Fori(0, NB) as b:
                v.bn_stats(tile(stats, b), tile(buf, b)).then_inc(stats_done, 1)
            v.wait_ge(stats_done, NB)
            for b in range(NB):
                v.bn_aggr(mv[:, b, :], stats[:, b, :]).then_inc(moments, 1)
            v.wait_ge(sd_ready, 1)
            v.reciprocal(rstd[:, :], sd[:, :]).then_inc(rstd_ready, 1)
            v.wait_ge(rstd_ready, 1)
            if gain is None:
                with v.Fori(0, NB) as b:
                    v.tensor_scalar(tile(buf, b), tile(buf, b), tile(mv, b)[:, 0:1], rstd[:, bass.ds(b, 1)],
                                    ALU.subtract, ALU.mult).then_inc(scaled, 1)
            else:
                v.wait_ge(vecs_in, 32)
                with v.Fori(0, NB) as b:
                    v.scalar_tensor_tensor(out=tile(buf, b), in0=tile(buf, b), scalar=tile(mv, b)[:, 0:1],
                                           in1=vecs[:, 0, :], op0=ALU.subtract, op1=ALU.mult).then_inc(centred, 1)
                v.wait_ge(centred, NB)
                with v.Fori(0, NB) as b:
                    v.scalar_tensor_tensor(out=tile(buf, b), in0=tile(buf, b), scalar=rstd[:, bass.ds(b, 1)],
                                           in1=vecs[:, 1, :], op0=ALU.mult, op1=ALU.add).then_inc(scaled, 1)
            v.wait_ge(scaled, NB)


def move_tiles(nc, name, to, of):
    with Phase(nc, name) as ph:
        moved = ph.sem("moved")
        cleared = ph.sem("cleared")
        block = ph.block()

        def rows(ap, a, z):
            return ap[:, :, :] if len(ap.shape) == 3 else ap.rearrange("(b p) c -> p b c", p=P)[:, a:z, :]

        @block.vector
        def _(v):
            if len(of.shape) == 2 and of.shape[0] == N:
                v.memset(to[:, NB - 1, :], 0.0).then_inc(cleared, 1)

        @block.sync
        def _(sp):
            if len(of.shape) == 2 and of.shape[0] == N:
                full = (NB - 1) * P
                sp.dma_start(to[:, 0:NB - 1, :], of[0:full, :].rearrange("(b p) c -> p b c", p=P)).then_inc(moved, 16)
                sp.wait_ge(cleared, 1)
                sp.dma_start(to[0:TAIL, NB - 1, :], of[full:N, :]).then_inc(moved, 16)
                sp.wait_ge(moved, 32)
            else:
                sp.dma_start(rows(to, 0, NB), rows(of, 0, NB)).then_inc(moved, 16)
                sp.wait_ge(moved, 16)


M_HEADS = 8
M_D = C // M_HEADS
GH = P // M_D


def turn_weights(nc, name, w_dram, out, ident):
    rows = w_dram.shape[0]
    with Phase(nc, name) as ph:
        w = ph.sb("w", [P, rows // P, C])
        ps = [ph.ps(f"ps{k}", [P, 512]) for k in range(2)]
        w_in = ph.sem("w_in")
        turned = ph.sem("turned")
        copied = ph.sem("copied")
        block = ph.block()

        @block.sync
        def _(sp):
            sp.dma_start(w[:, :, :], w_dram.rearrange("(r p) c -> p r c", p=P)).then_inc(w_in, 16)

        @block.tensor
        def _(pe):
            pe.wait_ge(w_in, 16)
            for r in range(rows // P):
                if r >= 2:
                    pe.wait_ge(copied, r - 1)
                for k in range(2):
                    mm = pe.transpose(ps[r % 2][:, k * P:(k + 1) * P], w[:, r, k * P:(k + 1) * P], ident[:, :])
                mm.then_inc(turned, 1)

        @block.vector
        def _(v):
            for r in range(rows // P):
                v.wait_ge(turned, r + 1)
                v.tensor_copy(out[:, :, r * P:(r + 1) * P], ps[r % 2][:, 0:C].rearrange("p (k o) -> p k o", k=2)
                              ).then_inc(copied, 1)
            v.wait_ge(copied, rows // P)


def tile_of(t, b):
    return t[:, bass.ds(b, 1), :].rearrange("p a c -> p (a c)")


def stage_tiles(g, buf, stage, staged, turned):
    def step(i, half, last):
        b = 2 * i + half
        g.wait_ge(turned, b + 1)
        g.tensor_copy(stage[:, half, :], tile_of(buf, b)).then_inc(staged, 1)

    over_tiles(g, step)


def turn_tile(pe, stage, half, ps, ident):
    for k in range(2):
        mm = pe.transpose(ps[:, k * P:(k + 1) * P], stage[:, half, k * P:(k + 1) * P], ident[:, :])
    return mm


def mix_keys(nc, st, XN, WT, KV):
    ident = st["ident"]
    VW = P + 2
    with Phase(nc, "keys") as ph:
        stage = ph.sb("stage", [P, 2, C])
        xs = ph.sb("xs", [P, 2, C])
        low = ph.sb("low", [P, 2, C])
        ex = ph.sb("ex", [P, 2, C])
        kp = ph.sb("kp", [P, 2, C])
        v1 = ph.sb("v1", [P, 2, 2, VW])
        psA = [ph.ps(f"psA{k}", [P, 512]) for k in range(2)]
        psK = [ph.ps(f"psK{k}", [P, 512]) for k in range(2)]
        psV = [ph.ps(f"psV{k}", [P, 512]) for k in range(2)]
        staged = ph.sem("staged")
        turned = ph.sem("turned")
        xT_ready = ph.sem("xT_ready")
        kv_ready = ph.sem("kv_ready")
        low_ready = ph.sem("low_ready")
        ex_ready = ph.sem("ex_ready")
        v_ready = ph.sem("v_ready")
        kp_ready = ph.sem("kp_ready")
        outer = ph.sem("outer")
        ones_set = ph.sem("ones_set")
        cleared = ph.sem("cleared")
        kv_out = ph.sem("kv_out")
        block = ph.block()

        @block.gpsimd
        def _(g):
            g.memset(v1[:, :, :, P:VW], 1.0).then_inc(ones_set, 1)
            g.memset(KV[:, :, :], 0.0).then_inc(cleared, 1)
            stage_tiles(g, XN, stage, staged, turned)

        @block.tensor
        def _(pe):
            for s in (turned, kv_ready, outer):
                pe.sem_inc(s, 2)
            pe.wait_ge(ones_set, 1)

            def keys_values(b, half):
                pe.wait_ge(staged, b + 1)
                pe.wait_ge(xT_ready, b + 1)
                turn_tile(pe, stage, half, psA[half], ident).then_inc(turned, 1)
                pe.wait_ge(xT_ready, b + 3)
                pe.wait_ge(kp_ready, b + 1)
                pe.wait_ge(v_ready, b + 1)
                for k in range(2):
                    mm = pe.matmul(psK[half][:, :], xs[:, half, k * P:(k + 1) * P], WT[:, k, C:3 * C],
                                   start=(k == 0), stop=(k == 1))
                mm.then_inc(kv_ready, 1)

            def outers(b, half, first, last):
                n = TAIL if last else P
                pe.wait_ge(kp_ready, b + 3)
                pe.wait_ge(v_ready, b + 3)
                for g in range(2):
                    mm = pe.matmul(psV[g][:, 0:VW], kp[0:n, half, g * P:(g + 1) * P], v1[0:n, half, g, :],
                                   start=first, stop=last)
                mm.then_inc(outer, 1)

            keys_values(0, 0)
            keys_values(1, 1)
            outers(0, 0, True, False)
            with pe.Fori(1, (NB - 1) // 2) as i:
                keys_values(2 * i, 0)
                outers(2 * i - 1, 1, False, False)
                keys_values(2 * i + 1, 1)
                outers(2 * i, 0, False, False)
            keys_values(NB - 1, 0)
            outers(NB - 2, 1, False, False)
            outers(NB - 1, 0, False, True)

        @block.scalar
        def _(a):
            a.sem_inc(xT_ready, 2)
            a.sem_inc(v_ready, 2)
            a.wait_ge(ones_set, 1)

            def step(i, half, last):
                b = 2 * i + half
                a.wait_ge(turned, b + 3)
                a.wait_ge(kv_ready, b + 1)
                a.activation(xs[:, half, :], psA[half][:, 0:C], ACT.Copy).then_inc(xT_ready, 1)
                a.wait_ge(kv_ready, b + 3)
                a.wait_ge(outer, b + 1)
                a.activation(v1[:, half, :, 0:P], psK[half][:, C:2 * C].rearrange("p (g c) -> p g c", g=2), ACT.Copy
                             ).then_inc(v_ready, 1)
                a.wait_ge(low_ready, b + 1)
                a.wait_ge(kp_ready, b + 1)
                a.activation(ex[:, half, :], low[:, half, :], ACT.Exp).then_inc(ex_ready, 1)

            over_tiles(a, step)

        @block.vector
        def _(v):
            v.sem_inc(kp_ready, 2)

            def step(i, half, last):
                b = 2 * i + half
                v.wait_ge(kv_ready, b + 3)
                v.wait_ge(kp_ready, b + 1)
                v.wait_ge(v_ready, b + 3)
                v.tensor_scalar(low[:, half, :], psK[half][:, 0:C], 0.0, None, ALU.min).then_inc(low_ready, 1)
                v.wait_ge(ex_ready, b + 1)
                v.wait_ge(outer, b + 1)
                v.scalar_tensor_tensor(out=kp[:, half, :], in0=psK[half][:, 0:C], scalar=0.0, in1=ex[:, half, :],
                                       op0=ALU.max, op1=ALU.add).then_inc(kp_ready, 1)

            over_tiles(v, step)
            v.wait_ge(outer, NB + 2)
            v.wait_ge(cleared, 1)
            for g in range(2):
                for h in range(GH):
                    r = slice(h * M_D, (h + 1) * M_D)
                    v.tensor_copy(KV[r, g, r], psV[g][r, r]).then_inc(kv_out, 1)
                    v.tensor_copy(KV[r, g, P + h:P + h + 1], psV[g][r, P:P + 1]).then_inc(kv_out, 1)
            v.wait_ge(kv_out, 4 * GH)


def mix_queries(nc, st, XN, WT, KV):
    ident = st["ident"]
    with Phase(nc, "queries") as ph:
        stage = ph.sb("stage", [P, 2, C])
        xs = ph.sb("xs", [P, 2, C])
        low = ph.sb("low", [P, 2, C])
        ex = ph.sb("ex", [P, 2, C])
        qp = ph.sb("qp", [P, 2, C])
        den = ph.sb("den", [P, 2, M_HEADS])
        t = ph.sb("t", [P, 2, C])
        psA = [ph.ps(f"psA{k}", [P, 512]) for k in range(2)]
        psQ = [ph.ps(f"psQ{k}", [P, 512]) for k in range(2)]
        psT = [ph.ps(f"psT{k}", [P, 512]) for k in range(2)]
        staged = ph.sem("staged")
        turned = ph.sem("turned")
        xT_ready = ph.sem("xT_ready")
        q_ready = ph.sem("q_ready")
        low_ready = ph.sem("low_ready")
        ex_ready = ph.sem("ex_ready")
        qp_ready = ph.sem("qp_ready")
        read = ph.sem("read")
        chain = ph.sem("chain")
        mixed = ph.sem("mixed")
        block = ph.block()
        KW = P + GH

        @block.gpsimd
        def _(g):
            stage_tiles(g, XN, stage, staged, turned)

        @block.tensor
        def _(pe):
            for s in (turned, q_ready, read):
                pe.sem_inc(s, 2)

            def queries(b, half):
                pe.wait_ge(staged, b + 1)
                pe.wait_ge(xT_ready, b + 1)
                turn_tile(pe, stage, half, psA[half], ident).then_inc(turned, 1)
                pe.wait_ge(xT_ready, b + 3)
                pe.wait_ge(qp_ready, b + 1)
                for g in range(2):
                    for k in range(2):
                        mm = pe.matmul(psQ[half][:, g * P:(g + 1) * P], WT[:, k, g * P:(g + 1) * P],
                                       xs[:, half, k * P:(k + 1) * P], start=(k == 0), stop=(k == 1))
                mm.then_inc(q_ready, 1)

            def reads(b, half):
                pe.wait_ge(qp_ready, b + 3)
                pe.wait_ge(mixed, b + 1)
                for g in range(2):
                    mm = pe.matmul(psT[half][:, g * KW:(g + 1) * KW], qp[:, half, g * P:(g + 1) * P], KV[:, g, :],
                                   start=True, stop=True)
                mm.then_inc(read, 1)

            queries(0, 0)

            def step(i, half, last):
                b = 2 * i + half
                if not last:
                    queries(b + 1, 1 - half)
                reads(b, half)

            over_tiles(pe, step)

        @block.scalar
        def _(a):
            a.sem_inc(xT_ready, 2)

            def step(i, half, last):
                b = 2 * i + half
                a.wait_ge(turned, b + 3)
                a.wait_ge(q_ready, b + 1)
                a.activation(xs[:, half, :], psA[half][:, 0:C], ACT.Copy).then_inc(xT_ready, 1)
                a.wait_ge(low_ready, b + 1)
                a.wait_ge(qp_ready, b + 1)
                a.activation(ex[:, half, :], low[:, half, :], ACT.Exp).then_inc(ex_ready, 1)

            over_tiles(a, step)

        @block.vector
        def _(v):
            v.sem_inc(qp_ready, 2)
            v.sem_inc(mixed, 2)

            def feature(b, half):
                v.wait_ge(q_ready, b + 3)
                v.wait_ge(qp_ready, b + 1)
                v.tensor_scalar(low[:, half, :], psQ[half][:, 0:C], 0.0, None, ALU.min).then_inc(low_ready, 1)
                v.wait_ge(ex_ready, b + 1)
                v.wait_ge(read, b + 1)
                v.scalar_tensor_tensor(out=qp[:, half, :], in0=psQ[half][:, 0:C], scalar=0.0, in1=ex[:, half, :],
                                       op0=ALU.max, op1=ALU.add).then_inc(qp_ready, 1)

            def result(b, half):
                ch = Chain(v, chain, 3 * b)
                v.wait_ge(read, b + 3)
                v.wait_ge(mixed, b + 1)
                r = psT[half][:, 0:2 * KW].rearrange("p (g k) -> p g k", g=2)
                d = den[:, half, :].rearrange("p (g h) -> p g h", g=2)
                ch.link(v.tensor_scalar(d, r[:, :, P:KW], 1e-6, None, ALU.add))
                ch.link(v.reciprocal(den[:, half, :], den[:, half, :]))
                for g in range(2):
                    ins = v.tensor_tensor(t[:, half, g * P:(g + 1) * P].rearrange("p (h m) -> p h m", h=GH),
                                          r[:, g, 0:P].rearrange("p (h m) -> p h m", h=GH),
                                          d[:, g, :].unsqueeze(2).broadcast_to([P, GH, M_D]), ALU.mult)
                    if g:
                        ch.link(ins)
                assert ch.n == 3
                v.wait_ge(staged, b + 1)
                v.tensor_tensor(tile_of(XN, b), tile_of(XN, b), t[:, half, :], ALU.add).then_inc(mixed, 1)

            feature(0, 0)

            def step(i, half, last):
                b = 2 * i + half
                if not last:
                    feature(b + 1, 1 - half)
                result(b, half)

            over_tiles(v, step)
            v.wait_ge(mixed, NB + 2)


def mix_mlp(nc, st, io, XN, W1T, W2T):
    ident = st["ident"]
    with Phase(nc, "mlp") as ph:
        stage = ph.sb("stage", [P, 2, C])
        xs = ph.sb("xs", [P, 2, C])
        hs = ph.sb("hs", [P, 2, C])
        b1 = ph.sb("b1", [P, 2])
        b2 = ph.sb("b2", [P, C])
        t = ph.sb("t", [P, 2, C])
        psA = [ph.ps(f"psA{k}", [P, 512]) for k in range(2)]
        psH = [ph.ps(f"psH{k}", [P, 512]) for k in range(2)]
        psY = [ph.ps(f"psY{k}", [P, 512]) for k in range(2)]
        biases_in = ph.sem("biases_in")
        staged = ph.sem("staged")
        turned = ph.sem("turned")
        xT_ready = ph.sem("xT_ready")
        hidden = ph.sem("hidden")
        gelu_ready = ph.sem("gelu_ready")
        y_ready = ph.sem("y_ready")
        biased = ph.sem("biased")
        added = ph.sem("added")
        block = ph.block()

        @block.sync
        def _(sp):
            with nc.allow_non_contiguous_dma(reason="256 words, once"):
                sp.dma_start(b1[:, :], io["mix_b1"].rearrange("(k p) -> p k", p=P)).then_inc(biases_in, 16)
            sp.dma_start(b2[:, :], broadcast_row(io["mix_b2"])).then_inc(biases_in, 16)

        @block.gpsimd
        def _(g):
            stage_tiles(g, XN, stage, staged, turned)

        @block.tensor
        def _(pe):
            for s in (turned, hidden, y_ready):
                pe.sem_inc(s, 2)

            def up(b, half):
                pe.wait_ge(staged, b + 1)
                pe.wait_ge(xT_ready, b + 1)
                turn_tile(pe, stage, half, psA[half], ident).then_inc(turned, 1)
                pe.wait_ge(xT_ready, b + 3)
                pe.wait_ge(gelu_ready, b + 1)
                for g in range(2):
                    for k in range(2):
                        mm = pe.matmul(psH[half][:, g * P:(g + 1) * P], W1T[:, k, g * P:(g + 1) * P],
                                       xs[:, half, k * P:(k + 1) * P], start=(k == 0), stop=(k == 1))
                mm.then_inc(hidden, 1)

            def down(b, half):
                pe.wait_ge(gelu_ready, b + 3)
                pe.wait_ge(biased, b + 1)
                for k in range(2):
                    mm = pe.matmul(psY[half][:, 0:C], hs[:, half, k * P:(k + 1) * P], W2T[:, k, :],
                                   start=(k == 0), stop=(k == 1))
                mm.then_inc(y_ready, 1)

            up(0, 0)

            def step(i, half, last):
                b = 2 * i + half
                if not last:
                    up(b + 1, 1 - half)
                down(b, half)

            over_tiles(pe, step)

        @block.scalar
        def _(a):
            a.sem_inc(xT_ready, 2)
            a.sem_inc(gelu_ready, 2)
            a.wait_ge(biases_in, 32)

            def turn(b, half):
                a.wait_ge(turned, b + 3)
                a.wait_ge(hidden, b + 1)
                a.activation(xs[:, half, :], psA[half][:, 0:C], ACT.Copy).then_inc(xT_ready, 1)

            turn(0, 0)

            def step(i, half, last):
                b = 2 * i + half
                if not last:
                    turn(b + 1, 1 - half)
                a.wait_ge(hidden, b + 3)
                a.wait_ge(y_ready, b + 1)
                for g in range(2):
                    ins = a.activation(hs[:, half, g * P:(g + 1) * P], psH[half][:, g * P:(g + 1) * P], ACT.Gelu,
                                       bias=b1[:, g:g + 1])
                ins.then_inc(gelu_ready, 1)

            over_tiles(a, step)

        @block.vector
        def _(v):
            v.sem_inc(biased, 2)
            v.sem_inc(added, 1)
            v.wait_ge(biases_in, 32)

            def step(i, half, last):
                b = 2 * i + half
                v.wait_ge(y_ready, b + 3)
                v.wait_ge(added, b + 1)
                v.tensor_tensor(t[:, half, :], psY[half][:, 0:C], b2[:, :], ALU.add).then_inc(biased, 1)
                v.wait_ge(biased, b + 3)
                v.wait_ge(staged, b + 1)
                v.tensor_tensor(tile_of(XN, b), tile_of(XN, b), t[:, half, :], ALU.add).then_inc(added, 1)

            over_tiles(v, step)
            v.wait_ge(added, NB + 1)


EX = 8
FH = 512
HC = FH // P
GT = 4


def route(nc, st, io, XN, xT, wts):
    ident, iota = st["ident"], st["iota"]
    with Phase(nc, "route") as ph:
        stage = ph.sb("stage", [P, 2, C])
        xs = ph.sb("xs", [P, 2, C])
        Wr = ph.sb("Wr", [P, 2, EX])
        br = ph.sb("br", [P, EX])
        lg = ph.sb("lg", [P, NB, EX])
        top = ph.sb("top", [P, NB, 8])
        topi = ph.sb("topi", [P, NB, 8], mybir.dt.uint32)
        topf = ph.sb("topf", [P, NB, 2])
        gap = ph.sb("gap", [P, NB])
        w = ph.sb("w", [P, NB, 2])
        den = ph.sb("den", [P, NB])
        pick = ph.sb("pick", [P, 2, NB, EX])
        psA = [ph.ps(f"psA{k}", [P, 512]) for k in range(2)]
        psL = [ph.ps(f"psL{k}", [P, 512]) for k in range(2)]
        router_in = ph.sem("router_in")
        staged = ph.sem("staged")
        turned = ph.sem("turned")
        xT_ready = ph.sem("xT_ready")
        kept = ph.sem("kept")
        logits = ph.sem("logits")
        biased = ph.sem("biased")
        topped = ph.sem("topped")
        found = ph.sem("found")
        chain = ph.sem("chain")
        gap_ready = ph.sem("gap_ready")
        exp_ready = ph.sem("exp_ready")
        block = ph.block()

        @block.sync
        def _(sp):
            sp.dma_start(Wr[:, :, :], io["ffn_Wr"].rearrange("(k p) e -> p k e", p=P)).then_inc(router_in, 16)
            sp.dma_start(br[:, :], broadcast_row(io["ffn_br"])).then_inc(router_in, 16)

        @block.gpsimd
        def _(g):
            stage_tiles(g, XN, stage, staged, turned)

        @block.tensor
        def _(pe):
            for s in (turned, logits):
                pe.sem_inc(s, 2)
            pe.wait_ge(router_in, 32)

            def step(i, half, last):
                b = 2 * i + half
                pe.wait_ge(staged, b + 1)
                pe.wait_ge(kept, b - 1 + 2)
                turn_tile(pe, stage, half, psA[half], ident).then_inc(turned, 1)
                pe.wait_ge(xT_ready, b + 3)
                pe.wait_ge(biased, b + 1)
                for k in range(2):
                    mm = pe.matmul(psL[half][:, 0:EX], xs[:, half, k * P:(k + 1) * P], Wr[:, k, :],
                                   start=(k == 0), stop=(k == 1))
                mm.then_inc(logits, 1)

            over_tiles(pe, step)

        @block.scalar
        def _(a):
            a.sem_inc(xT_ready, 2)
            a.sem_inc(kept, 2)

            def step(i, half, last):
                b = 2 * i + half
                a.wait_ge(turned, b + 3)
                a.wait_ge(logits, b + 1)
                a.activation(xs[:, half, :], psA[half][:, 0:C], ACT.Copy).then_inc(xT_ready, 1)
                a.activation(xT[:, :, bass.ds(b * P, P)], psA[half][:, 0:C].rearrange("p (k t) -> p k t", k=2), ACT.Copy
                             ).then_inc(kept, 1)

            over_tiles(a, step)
            a.wait_ge(gap_ready, 1)
            a.activation(w[:, :, 1], gap[:, :], ACT.Exp).then_inc(exp_ready, 1)

        @block.vector
        def _(v):
            v.sem_inc(biased, 2)
            v.wait_ge(router_in, 32)

            def step(i, half, last):
                b = 2 * i + half
                v.wait_ge(logits, b + 3)
                v.tensor_tensor(tile_of(lg, b), psL[half][:, 0:EX], br[:, :], ALU.add).then_inc(biased, 1)

            over_tiles(v, step)
            v.wait_ge(biased, NB + 2)
            for b in range(NB):
                v.max(top[:, b, :], lg[:, b, :]).then_inc(topped, 1)
            v.wait_ge(topped, NB)
            for b in range(NB):
                v.max_index(topi[:, b, :], top[:, b, :], lg[:, b, :]).then_inc(found, 1)
            v.tensor_tensor(gap[:, :], top[:, :, 1], top[:, :, 0], ALU.subtract).then_inc(gap_ready, 1)
            v.wait_ge(found, NB)
            ch = Chain(v, chain)
            ch.link(v.tensor_copy(topf[:, :, :], topi[:, :, 0:2]))
            v.wait_ge(exp_ready, 1)
            ch.link(v.tensor_scalar(den[:, :], w[:, :, 1], 1.0, None, ALU.add))
            ch.link(v.reciprocal(den[:, :], den[:, :]))
            ch.add(v.tensor_copy(w[:, :, 0], den[:, :]))
            ch.link(v.tensor_tensor(w[:, :, 1], w[:, :, 1], den[:, :], ALU.mult))
            places = iota[:, 0:EX].unsqueeze(1).broadcast_to([P, NB, EX])
            for k in range(2):
                ch.add(v.tensor_tensor(pick[:, k, :, :], places, topf[:, :, k:k + 1].broadcast_to([P, NB, EX]), ALU.is_equal))
            ch.wait()
            for k in range(2):
                ch.add(v.tensor_tensor(pick[:, k, :, :], pick[:, k, :, :], w[:, :, k:k + 1].broadcast_to([P, NB, EX]), ALU.mult))
            ch.wait()
            ch.link(v.tensor_tensor(wts[:, :, :], pick[:, 0, :, :], pick[:, 1, :, :], ALU.add))


def experts(nc, st, io, xT, wts, dr, out):
    ident = st["ident"]
    with Phase(nc, "experts") as ph:
        W1 = ph.sb("W1", [P, EX, 2, FH])
        W2 = ph.sb("W2", [P, EX, HC, C])
        b1 = ph.sb("b1", [P, EX, HC])
        b2 = ph.sb("b2", [EX, C])
        wst = ph.sb("wst", [P, GT, EX])
        wT = ph.sb("wT", [EX, GT * P])
        hT = ph.sb("hT", [P, 2, HC, GT * P])
        Y = ph.sb("Y", [P, 2, GT, C])
        X2 = ph.sb("X2", [P, 2, GT, C])
        psH = [ph.ps(f"psH{k}", [P, 512]) for k in range(HC)]
        psY = [ph.ps(f"psY{k}", [P, 512]) for k in range(GT)]
        w1_in = ph.sem("w1_in")
        w2_in = ph.sem("w2_in")
        x2_in = [ph.sem(f"x2_in{k}") for k in range(2)]
        staged = ph.sem("staged")
        w_turned = ph.sem("w_turned")
        wT_ready = ph.sem("wT_ready")
        hidden = ph.sem("hidden")
        gelu_ready = ph.sem("gelu_ready")
        y_ready = ph.sem("y_ready")
        y_read = ph.sem("y_read")
        stored = ph.sem("stored")
        y_out = [ph.sem(f"y_out{k}") for k in range(2)]
        block = ph.block()
        FULL = NB // GT
        assert NB % GT == 1 and FULL % 2 == 0
        R = EX + 1

        def over_groups(eng, step):
            with eng.Fori(0, FULL // 2) as i:
                step(i, 0, GT)
                step(i, 1, GT)
            step(FULL // 2, 0, 1)

        @block.sync
        def _(sp):
            for e in range(EX):
                sp.dma_start(W1[:, e, :, :], io["ffn_W1"][e].rearrange("(k p) f -> p k f", p=P)).then_inc(w1_in, 16)
            with nc.allow_non_contiguous_dma(reason="4096 words, once"):
                sp.dma_start(b1[:, :, :], io["ffn_b1"].rearrange("e (c p) -> p e c", p=P)).then_inc(w1_in, 16)
            sp.dma_start(b2[:, :], io["ffn_b2"]).then_inc(w2_in, 16)
            for e in range(EX):
                sp.dma_start(W2[:, e, :, :], io["ffn_W2"][e].rearrange("(c p) o -> p c o", p=P)).then_inc(w2_in, 16)

            def step(i, half, nt):
                q = 2 * i + half
                sp.wait_ge(stored, q + 1)
                sp.dma_start(X2[:, half, 0:nt, :], dr["x2"][bass.ds(q * GT * P, nt * P), :].rearrange("(t p) c -> p t c", p=P)
                             ).then_inc(x2_in[half], 16)

            over_groups(sp, step)

        @block.gpsimd
        def _(g):
            g.sem_inc(stored, 2)

            def step(i, half, nt):
                q = 2 * i + half
                g.wait_ge(w_turned, q + 1)
                g.tensor_copy(wst[:, 0:nt, :], wts[:, bass.ds(q * GT, nt), :]).then_inc(staged, 1)
                g.wait_ge(y_read, (q + 1) * R * GT + 1 if nt == GT else q * R * GT + R + 1)
                if nt == GT:
                    g.dma_start(out[bass.ds(q * GT * P, GT * P), :].rearrange("(t p) c -> p t c", p=P), Y[:, half, :, :]
                                ).then_inc(y_out[half], 16)
                else:
                    g.dma_start(out[(NB - 1) * P:N, :], Y[0:TAIL, half, 0, :]).then_inc(y_out[half], 16)
                g.wait_ge(y_out[half], 16 * (i + 1))
                g.sem_inc(stored, 1)

            over_groups(g, step)

        @block.tensor
        def _(pe):
            pe.sem_inc(w_turned, 1)
            pe.sem_inc(y_ready, 1)
            pe.wait_ge(w1_in, 16 * (EX + 1))
            pe.wait_ge(w2_in, 16 * (EX + 1))

            def step(i, half, nt):
                q = 2 * i + half
                h0 = q * EX * HC
                y0 = q * R * GT + 1

                def up(e):
                    for c in range(HC):
                        pe.wait_ge(gelu_ready, h0 + e * HC + c + 1)
                        if e == 0:
                            pe.wait_ge(wT_ready, q + 1)
                        for k in range(2):
                            mm = pe.matmul(psH[c][:, 0:nt * P], W1[:, e, k, c * P:(c + 1) * P],
                                           xT[:, k, bass.ds(q * GT * P, nt * P)], start=(k == 0), stop=(k == 1))
                        mm.then_inc(hidden, 1)

                def down(e):
                    pe.wait_ge(gelu_ready, h0 + (e + 2) * HC)
                    for t in range(nt):
                        pe.wait_ge(y_read, y0 + (e + 1) * nt + t + 1 - nt)
                        for c in range(HC):
                            mm = pe.matmul(psY[t][:, 0:C], hT[:, e % 2, c, t * P:(t + 1) * P], W2[:, e, c, :],
                                           start=(c == 0), stop=(c == HC - 1))
                        mm.then_inc(y_ready, 1)

                pe.wait_ge(staged, q + 1)
                pe.wait_ge(gelu_ready, h0 + HC)
                for t in range(nt):
                    mm = pe.transpose(psH[0][0:EX, t * P:(t + 1) * P], wst[:, t, :], ident[:, :])
                mm.then_inc(w_turned, 1)
                pe.wait_ge(wT_ready, q + 1)
                pe.wait_ge(y_read, y0)
                for t in range(nt):
                    pe.matmul(psY[t][:, 0:C], wT[:, t * P:(t + 1) * P], b2[:, :], start=True, stop=True).then_inc(y_ready, 1)
                up(0)
                for e in range(1, EX):
                    up(e)
                    down(e - 1)
                down(EX - 1)

            over_groups(pe, step)

        @block.scalar
        def _(a):
            a.sem_inc(gelu_ready, HC)
            a.wait_ge(w1_in, 16 * (EX + 1))

            def step(i, half, nt):
                q = 2 * i + half
                h0 = q * EX * HC
                y0 = q * R * GT + 1
                a.wait_ge(w_turned, q + 2)
                a.wait_ge(y_ready, y0)
                a.activation(wT[:, 0:nt * P], psH[0][0:EX, 0:nt * P], ACT.Copy).then_inc(wT_ready, 1)
                for e in range(EX):
                    if e >= 2:
                        a.wait_ge(y_ready, y0 + e * nt)
                    for c in range(HC):
                        a.wait_ge(hidden, h0 + e * HC + c + 1)
                        a.activation(hT[:, e % 2, c, 0:nt * P], psH[c][:, 0:nt * P], ACT.Gelu, bias=b1[:, e, c:c + 1]
                                     ).then_inc(gelu_ready, 1)

            over_groups(a, step)

        @block.vector
        def _(v):
            v.sem_inc(y_read, 1)

            def step(i, half, nt):
                q = 2 * i + half
                y0 = q * R * GT + 1
                v.wait_ge(x2_in[half], 16 * (i + 1))
                v.wait_ge(stored, q + 1)
                for e in range(-1, EX):
                    for t in range(nt):
                        v.wait_ge(y_ready, y0 + (e + 1) * nt + t + 1)
                        y = Y[:, half, t, :]
                        if e < 0:
                            ins = v.tensor_tensor(y, psY[t][:, 0:C], X2[:, half, t, :], ALU.add)
                        else:
                            v.wait_ge(y_read, y0 + e * nt + t + 1)
                            ins = v.scalar_tensor_tensor(out=y, in0=psY[t][:, 0:C],
                                                         scalar=wts[:, bass.ds(q * GT + t, 1), e:e + 1].rearrange("p a b -> p (a b)"),
                                                         in1=y, op0=ALU.mult, op1=ALU.add)
                        ins.then_inc(y_read, 1)

            over_groups(v, step)


def build(nc, io, out):
    def dram(name, shape, dt=F32):
        return nc.dram_tensor(name, shape, dt, kind="Internal").ap()

    dr = {"src_pad": dram("src_pad", (TG + 1, GE), I32), "dst_pad": dram("dst_pad", (TG + 1, GE), I32),
          "reset": dram("reset", (NG, H, 2, P), BF16), "rows": dram("rows", (NPAD, RW)),
          "h": dram("h", (NPAD, C)), "mix": dram("mix", (NPAD, C)), "x2": dram("x2", (NPAD, C))}

    with ExitStack() as ctx:
        def sb(name, shape, dt=F32):
            return ctx.enter_context(nc.sbuf_tensor(name, shape, dt))

        st = {"ident": sb("ident", [P, P]), "iota": sb("iota", [P, P])}
        with ExitStack() as inner:
            def sbi(name, shape, dt=F32):
                return inner.enter_context(nc.sbuf_tensor(name, shape, dt))

            for n in ("srcT", "relT", "lastT"):
                st[n] = sbi(n, [P, NG, 2])
            st["words"] = sbi("words", [P, NW], I32)
            prepare_walk(nc, io["src"], io["dst"], st, dr)

            with ExitStack() as mx:
                XN = mx.enter_context(nc.sbuf_tensor("XN", [P, NB, C], F32))
                WT = mx.enter_context(nc.sbuf_tensor("WT", [P, 2, 3 * C], F32))
                W1T = mx.enter_context(nc.sbuf_tensor("W1T", [P, 2, C], F32))
                W2T = mx.enter_context(nc.sbuf_tensor("W2T", [P, 2, C], F32))
                KV = mx.enter_context(nc.sbuf_tensor("KV", [P, 2, P + GH], F32))
                turn_weights(nc, "turn_qkv", io["mix_Wqkv"], WT, st["ident"])
                turn_weights(nc, "turn_w1", io["mix_W1"], W1T, st["ident"])
                turn_weights(nc, "turn_w2", io["mix_W2"], W2T, st["ident"])
                move_tiles(nc, "load_x", XN, io["x"])
                normalize_tiles(nc, "norm_x", XN, None, None)
                mix_keys(nc, st, XN, WT, KV)
                mix_queries(nc, st, XN, WT, KV)
                normalize_tiles(nc, "norm_mix1", XN, io["mix_ln1_g"], io["mix_ln1_b"])
                mix_mlp(nc, st, io, XN, W1T, W2T)
                normalize_tiles(nc, "norm_mix2", XN, io["mix_ln2_g"], io["mix_ln2_b"])
                move_tiles(nc, "store_mix", dr["mix"], XN)

            st["acc"] = sbi("acc", [P, NB, RW])
            st["ADM"] = sbi("ADM", [P, NB, 2 * H])
            st["own"] = sbi("own", [P, NB, H])
            node_phase(nc, 0, st, io, dr)
            for layer in range(3):
                edge_phase(nc, layer, st, dr)
                node_phase(nc, layer + 1, st, io, dr)

        xT = sb("xT", [P, 2, NPAD])
        wts = sb("wts", [P, NB, EX])
        with nc.sbuf_tensor("XF", [P, NB, C], F32) as XF:
            move_tiles(nc, "load_x2", XF, dr["x2"])
            normalize_tiles(nc, "norm_x2", XF, None, None)
            normalize_tiles(nc, "norm_ffn", XF, io["ffn_gamma"], io["ffn_beta"])
            route(nc, st, io, XF, xT, wts)
        experts(nc, st, io, xT, wts, dr, out)


_GNN = [f"L0_gnn_{n}{layer}" for layer in range(3) for n in ("W", "att_src", "att_dst", "bias", "ln_g", "ln_b")]
_MIX = [f"L0_mix_{n}" for n in ("Wqkv", "ln1_g", "ln1_b", "W1", "b1", "W2", "b2", "ln2_g", "ln2_b")]
_FFN = [f"L0_ffn_{n}" for n in ("gamma", "beta", "Wr", "br", "W1", "b1", "W2", "b2")]
_INS = ["x", "src", "dst"] + _GNN + _MIX + _FFN


def kernel(**inputs):
    import numpy as _np
    import concourse.bacc as _bacc
    from concourse.bass_utils import run_bass_kernel_spmd as _run

    nc = _bacc.Bacc("TRN2", target_bir_lowering=False, num_devices=1)
    arrays, io = {}, {}
    for name in _INS:
        a = _np.ascontiguousarray(inputs[name])
        arrays[f"in_{name}"] = a
        short = name.replace("L0_gnn_", "").replace("L0_", "")
        io[short] = nc.dram_tensor(f"in_{name}", a.shape, mybir.dt.from_np(a.dtype), kind="ExternalInput").ap()
    out = nc.dram_tensor("out", (N, C), F32, kind="ExternalOutput").ap()
    build(nc, io, out)
    r = _run(nc, [arrays], core_ids=[0])
    return r.results[0]["out"]
```

```python
from contextlib import ExitStack
from itertools import zip_longest

import concourse.bass as bass
from concourse import mybir

F32 = mybir.dt.float32
BF16 = mybir.dt.bfloat16
I32 = mybir.dt.int32
ALU = mybir.AluOpType
ACT = mybir.ActivationFunctionType
AX = mybir.AxisListType

P = 128
N = 6250
C = 256
E = 200000
NB = -(-N // P)
TAIL = N - (NB - 1) * P
NPAD = NB * P
H = 4
D = C // H
RW = C + H
GE = 2 * P
TG = -(-E // GE)
WG = 8
WS = 2 * WG
NW = 4 * (-(-(TG + NB - 1) // (4 * WG)))
NG = NW * WG
GC = -(-NG // P)
TC = -(-(TG + 1) // P)
BIG = float(2.0 ** 120)
SLOPE = 0.2
LN_EPS = 1e-5
RING = 4
ROWS_SEEN = "a node block is at most NB - 1, as the walk clamps it"


class Chain:

    def __init__(self, eng, sem, base=0):
        self.eng, self.sem, self.base, self.n = eng, sem, base, 0

    def add(self, ins):
        ins.then_inc(self.sem, 1)
        self.n += 1

    def wait(self):
        self.eng.wait_ge(self.sem, self.base + self.n)

    def link(self, ins):
        self.add(ins)
        self.wait()


def wait_apart(eng, sem, value, passed):
    eng.wait_ge(sem, value)
    eng.sem_inc(passed, 1)


class Phase:

    def __init__(self, nc, name):
        self.nc, self.name, self.ctx, self.sems = nc, name, ExitStack(), []

    def __enter__(self):
        self.ctx.__enter__()
        return self

    def __exit__(self, *a):
        done = self.ctx.__exit__(*a)
        self.nc.clear_and_free_semaphores(self.sems)
        self.nc.all_engine_barrier(sem_only=True)
        return done

    def sb(self, name, shape, dt=F32):
        return self.ctx.enter_context(self.nc.sbuf_tensor(f"{self.name}_{name}", shape, dt))

    def ps(self, name, shape, dt=F32):
        return self.ctx.enter_context(self.nc.psum_tensor(f"{self.name}_{name}", shape, dt))

    def sem(self, name):
        self.sems.append(self.nc.alloc_semaphore(f"{self.name}_{name}"))
        return self.sems[-1]

    def block(self):
        return self.ctx.enter_context(self.nc.Block())


def prepare_walk(nc, src, dst, st, dr):
    pad_rows = TG + 1
    with Phase(nc, "walk") as ph:
        pad = ph.sb("pad", [1, 2, pad_rows * GE - E], I32)
        dstI = ph.sb("dstI", [P, TC, GE], I32)
        dstF = ph.sb("dstF", [P, TC, GE])
        last_blk = ph.sb("last_blk", [P, TC])
        last_int = ph.sb("last_int", [P, TC], I32)
        threshold = ph.sb("threshold", [P, TC])
        passed = ph.sb("passed", [P, TC, GC * P], BF16)
        ones = ph.sb("ones", [P, P], BF16)
        iota_g = ph.sb("iota_g", [P, GC * P])
        iota_gp = ph.sb("iota_gp", [P, GC])
        grp = ph.sb("grp", [P, GC])
        grpI = ph.sb("grpI", [P, GC], I32)
        blk = ph.sb("blk", [P, GC])
        row_blk = ph.sb("row_blk", [P, GC * P])
        wordF = ph.sb("wordF", [P, NW, WG])
        wordS = ph.sb("wordS", [P, NW])
        pow2 = ph.sb("pow2", [P, WG])
        rise = ph.sb("rise", [P, NW, WG])
        Dg = ph.sb("Dg", [P, GC, 2, P], I32)
        Sg = ph.sb("Sg", [P, GC, 2, P], I32)
        Df = ph.sb("Df", [P, GC, 2, P])
        Sf = ph.sb("Sf", [P, GC, 2, P])
        rel = ph.sb("rel", [P, GC, 2, P])
        last = ph.sb("last", [P, GC, 2, P])
        rst = ph.sb("rst", [P, GC, 2, P], BF16)
        ps_row = ph.ps("ps_row", [P, 2, 512])
        ps_col = ph.ps("ps_col", [P, 512])
        ps_tr = ph.ps("ps_tr", [P, 4, 512])

        pads_set = ph.sem("pads_set")
        edges_in = ph.sem("edges_in")
        pads_in = ph.sem("pads_in")
        dst_in = ph.sem("dst_in")
        iotas = ph.sem("iotas")
        dve = ph.sem("dve")
        compared = ph.sem("compared")
        walked = ph.sem("walked")
        index_ready = ph.sem("index_ready")
        dst_rows = ph.sem("dst_rows")
        src_rows = ph.sem("src_rows")
        rows_ready = ph.sem("rows_ready")
        turned = ph.sem("turned")
        copied = ph.sem("copied")
        reset_ready = ph.sem("reset_ready")
        reset_out = ph.sem("reset_out")
        pool = ph.sem("pool")
        block = ph.block()
        rowT = -(-NG // 2)
        assert rowT <= 512

        flat = dr["dst_pad"].rearrange("t e -> (t e)")
        flat_s = dr["src_pad"].rearrange("t e -> (t e)")

        @block.sync
        def _(sp):
            for to, of in ((flat, dst), (flat_s, src)):
                sp.dma_start(to[0:E].rearrange("(a b) -> a b", a=16),
                             of.rearrange("(a b) -> a b", a=16)).then_inc(edges_in, 16)
            sp.wait_ge(pads_set, 2)
            for n, to in enumerate((flat, flat_s)):
                sp.dma_start(to[E:pad_rows * GE].rearrange("(a b) -> a b", a=1), pad[:, n, :]).then_inc(pads_in, 16)
            sp.wait_ge(edges_in, 32)
            sp.wait_ge(pads_in, 32)
            sp.wait_ge(pool, 1)
            full = (TC - 1) * P
            sp.dma_start(dstI[:, 0:TC - 1, :], dr["dst_pad"][0:full, :].rearrange("(c p) e -> p c e", p=P)).then_inc(dst_in, 16)
            sp.dma_start(dstI[0:pad_rows - full, TC - 1, :], dr["dst_pad"][full:pad_rows, :]).then_inc(dst_in, 16)
            sp.wait_ge(reset_ready, 1)
            for c in range(GC):
                n = min(P, NG - c * P)
                for h in range(H):
                    sp.dma_start(dr["reset"][c * P:c * P + n, h, :, :], rst[0:n, c, :, :]).then_inc(reset_out, 16)
            sp.wait_ge(reset_out, 16 * GC * H)

        @block.gpsimd
        def _(g):
            g.memset(dstI[:, TC - 1, :], 0).then_inc(pool, 1)
            g.memset(pad[:, 0, :], -1).then_inc(pads_set, 1)
            g.memset(pad[:, 1, :], 0).then_inc(pads_set, 1)
            g.iota(iota_g[:, :], [[1, GC * P]], base=0, channel_multiplier=0,
                   allow_small_or_imprecise_dtypes=True).then_inc(iotas, 1)
            g.iota(iota_gp[:, :], [[P, GC]], base=0, channel_multiplier=1,
                   allow_small_or_imprecise_dtypes=True).then_inc(iotas, 1)
            g.iota(st["iota"][:, :], [[1, P]], base=0, channel_multiplier=0,
                   allow_small_or_imprecise_dtypes=True).then_inc(iotas, 1)
            g.memset(st["ident"][:, :], 0.0).then_inc(pool, 1)
            g.wait_ge(pool, 2)
            g.affine_select(out=st["ident"][:, :], in_=st["ident"][:, :], compare_op=ALU.not_equal, fill=1.0,
                            base=0, pattern=[[-1, P]], channel_multiplier=1).then_inc(iotas, 1)
            g.iota(threshold[:, :], [[P, TC]], base=1, channel_multiplier=1,
                   allow_small_or_imprecise_dtypes=True).then_inc(pool, 1)
            g.wait_ge(pool, 3)
            g.affine_select(out=threshold[:, :], in_=threshold[:, :], compare_op=ALU.is_ge, fill=1e6,
                            base=TG - 1, pattern=[[-P, TC]], channel_multiplier=-1).then_inc(iotas, 1)
            g.wait_ge(index_ready, 1)
            for c in range(GC):
                g.indirect_dma_start(Dg[:, c, :, :].rearrange("p a b -> p (a b)"), None, dr["dst_pad"],
                                     bass.IndirectOffsetOnAxis(grpI[:, c:c + 1], 0)).then_inc(dst_rows, 16)
                g.indirect_dma_start(Sg[:, c, :, :].rearrange("p a b -> p (a b)"), None, dr["src_pad"],
                                     bass.IndirectOffsetOnAxis(grpI[:, c:c + 1], 0)).then_inc(src_rows, 16)

        @block.vector
        def _(v):
            ch = Chain(v, dve)
            v.memset(ones[:, :], 1.0).then_inc(iotas, 1)
            for n in range(1, WG):
                ch.add(v.memset(pow2[:, n:n + 1], float(64 * 2 ** (n - 1))))
            v.wait_ge(dst_in, 32)
            ch.link(v.tensor_copy(dstF[:, :, :], dstI[:, :, :]))
            ch.link(v.tensor_reduce(last_blk[:, :], dstF[:, :, :], AX.X, ALU.max))
            ch.link(v.tensor_scalar(last_blk[:, :], last_blk[:, :], 0.0, None, ALU.max))
            ch.link(v.tensor_copy(last_int[:, :], last_blk[:, :]))
            ch.link(v.tensor_scalar(last_int[:, :], last_int[:, :], 7, None, ALU.arith_shift_right))
            ch.link(v.tensor_copy(last_blk[:, :], last_int[:, :]))
            v.wait_ge(iotas, 6)
            ch.link(v.tensor_tensor(threshold[:, :], threshold[:, :], last_blk[:, :], ALU.add))
            for c in range(TC):
                v.tensor_scalar(passed[:, c, :], iota_g[:, :], threshold[:, c:c + 1], None, ALU.is_ge).then_inc(compared, 1)
            v.wait_ge(walked, 1)
            ch.link(v.tensor_copy(grp[:, :], ps_col[:, 0:GC]))
            v.tensor_copy(grpI[:, :], grp[:, :]).then_inc(index_ready, 1)
            ch.link(v.tensor_tensor(blk[:, :], iota_gp[:, :], grp[:, :], ALU.subtract))
            ch.link(v.tensor_scalar(blk[:, :], blk[:, :], float(NB - 1), float(P), ALU.min, ALU.mult))
            for c in range(2):
                ch.add(v.tensor_tensor(row_blk[:, c * rowT:(c + 1) * rowT], iota_g[:, c * rowT:(c + 1) * rowT],
                                       ps_row[:, c, 0:rowT], ALU.subtract))
            ch.wait()
            ch.link(v.tensor_scalar(row_blk[:, 0:NG], row_blk[:, 0:NG], float(NB - 1), None, ALU.min))
            rb = row_blk[:, 0:NG].rearrange("p (w g) -> p w g", g=WG)
            ch.add(v.tensor_copy(wordF[:, :, 0:1], rb[:, :, 0:1]))
            ch.link(v.tensor_tensor(wordF[:, :, 1:WG], rb[:, :, 1:WG], rb[:, :, 0:WG - 1], ALU.subtract))
            ch.link(v.tensor_scalar(rise[:, :, 1:WG], wordF[:, :, 1:WG], -BIG, None, ALU.mult))
            for h in range(H):
                up = st["rises"][:, :, 0, h * WG:(h + 1) * WG]
                down = st["rises"][:, :, 1, h * WG:(h + 1) * WG]
                ch.add(v.tensor_copy(up[:, :, 1:WG], rise[:, :, 1:WG]))
                for n in range(1, WG):
                    ch.add(v.tensor_copy(down[:, :, n:n + 1], rise[:, :, WG - n:WG - n + 1]))
                for to in (up, down):
                    ch.add(v.memset(to[:, :, 0:1], -BIG))
            ch.link(v.tensor_tensor(wordF[:, :, 1:WG], wordF[:, :, 1:WG],
                                    pow2[:, 1:WG].unsqueeze(1).broadcast_to([P, NW, WG - 1]), ALU.mult))
            ch.link(v.tensor_reduce(wordS[:, :], wordF[:, :, :], AX.X, ALU.add))
            ch.link(v.tensor_copy(st["words"][:, :], wordS[:, :]))
            v.wait_ge(dst_rows, 16 * GC)
            v.wait_ge(src_rows, 16 * GC)
            ch.add(v.tensor_copy(Df[:, :, :, :], Dg[:, :, :, :]))
            v.tensor_copy(Sf[:, :, :, :], Sg[:, :, :, :]).then_inc(rows_ready, 1)
            ch.add(v.memset(rst[:, :, :, 0:1], 0.0))
            ch.add(v.memset(last[:, :, :, P - 1:P], 1.0))
            ch.wait()
            for c in range(GC):
                v.tensor_scalar(rel[:, c, :, :], Df[:, c, :, :], blk[:, c:c + 1], None, ALU.subtract).then_inc(rows_ready, 1)
            v.tensor_tensor(last[:, :, :, 0:P - 1], Df[:, :, :, 0:P - 1], Df[:, :, :, 1:P], ALU.not_equal).then_inc(rows_ready, 1)
            v.wait_ge(rows_ready, 2 + GC)
            v.tensor_scalar(rst[:, :, :, 1:P], last[:, :, :, 0:P - 1], -BIG, None, ALU.mult).then_inc(reset_ready, 1)
            for c in range(GC):
                n = min(P, NG - c * P)
                v.wait_ge(turned, c + 1)
                for m, t in enumerate(("srcT", "relT", "lastT")):
                    for j in range(2):
                        o = (2 * m + j) * P
                        v.tensor_copy(st[t][:, c * P:c * P + n, j],
                                      ps_tr[:, 2 * (c % 2) + o // 512, o % 512:o % 512 + n]).then_inc(copied, 1)
            v.wait_ge(copied, 6 * GC)

        @block.tensor
        def _(pe):
            pe.wait_ge(iotas, 6)
            for c in range(TC):
                pe.wait_ge(compared, c + 1)
                for r in range(2):
                    pe.matmul(ps_row[:, r, 0:rowT], ones[:, :], passed[:, c, r * rowT:(r + 1) * rowT],
                              start=(c == 0), stop=(c == TC - 1))
            for m in range(GC):
                for c in range(TC):
                    mm = pe.matmul(ps_col[:, m:m + 1], passed[:, c, m * P:(m + 1) * P], ones[:, 0:1],
                                   start=(c == 0), stop=(c == TC - 1))
            mm.then_inc(walked, 1)
            pe.wait_ge(rows_ready, 2 + GC)
            for c in range(GC):
                if c >= 2:
                    pe.wait_ge(copied, 6 * (c - 1))
                for m, t in enumerate((Sf, rel, last)):
                    for j in range(2):
                        o = (2 * m + j) * P
                        mm = pe.transpose(ps_tr[:, 2 * (c % 2) + o // 512, o % 512:o % 512 + P],
                                          t[:, c, j, :], st["ident"][:, :])
                mm.then_inc(turned, 1)



def broadcast_row(vec):
    return vec.rearrange("(a n) -> a n", a=1).broadcast_to([P, vec.shape[0]])


def over_tiles(eng, step):
    step(0, 0, False)
    step(0, 1, False)
    with eng.Fori(1, (NB - 1) // 2) as i:
        step(i, 0, False)
        step(i, 1, False)
    step((NB - 1) // 2, 0, True)


TILE_RING = 4


def over_ring(eng, step):
    assert NB % TILE_RING == 1
    for slot in range(TILE_RING):
        step(0, slot, False)
    with eng.Fori(1, NB // TILE_RING) as i:
        for slot in range(TILE_RING):
            step(i, slot, False)
    step(NB // TILE_RING, 0, True)


def ring_rows(dram, i, slot, last):
    if last:
        return dram[(NB - 1) * P:N, :]
    return padded_ring_rows(dram, i, slot)


def padded_ring_rows(dram, i, slot):
    return dram[bass.ds((TILE_RING * i + slot) * P, P), :]


def is_zero(i):
    return isinstance(i, int) and i == 0


def node_phase(nc, layer, st, io, dr):
    first, final = layer == 0, layer == 3
    acc, ADM, own = st["acc"], st["ADM"], st["own"]
    with Phase(nc, f"node{layer}") as ph:
        X = ph.sb("X", [P, TILE_RING, C])
        rows = ph.sb("rows", [P, TILE_RING, RW])
        prev = ph.sb("prev", [P, TILE_RING, C])
        mix = ph.sb("mix", [P, TILE_RING, C])
        O = ph.sb("O", [P, TILE_RING, C])
        Hn = ph.sb("Hn", [P, TILE_RING, C])
        hT = ph.sb("hT", [P, TILE_RING, 2, P])
        ext = ph.sb("ext", [P, TILE_RING, RW])
        stats = ph.sb("stats", [P, TILE_RING, 6])
        mv = ph.sb("mv", [P, TILE_RING, 2])
        sd = ph.sb("sd", [P, TILE_RING, 1])
        rstd = ph.sb("rstd", [P, TILE_RING, 1])
        eps = ph.sb("eps", [P, 1])
        vecs = ph.sb("vecs", [P, 3, C])
        W = ph.sb("W", [P, 2, C])
        WT = ph.sb("WT", [P, 2, C])
        att = ph.sb("att", [P, 2, 2 * H])
        Wx = ph.sb("Wx", [P, 2, RW + H])
        tu = ph.sb("tu", [P, 2, NB * H])
        lr = ph.sb("lr", [P, 2, NB * H])
        es = ph.sb("es", [P, NB, H])
        zr = ph.sb("zr", [P, NB, H])
        psA = [ph.ps(f"psA{k}", [P, 512]) for k in range(2)]
        psB = [ph.ps(f"psB{k}", [P, 512]) for k in range(2)]
        psW = ph.ps("psW", [P, 512])
        psS = ph.ps("psS", [P, 512])

        consts = ph.sem("consts")
        att_clear = ph.sem("att_clear")
        vecs_in = ph.sem("vecs_in")
        weights_in = ph.sem("weights_in")
        w_turned = ph.sem("w_turned")
        wT_ready = ph.sem("wT_ready")
        w_scored = ph.sem("w_scored")
        wx_ready = ph.sem("wx_ready")
        pre = ph.sem("pre")
        es_ready = ph.sem("es_ready")
        loaded = [ph.sem(f"loaded{k}") for k in range(TILE_RING)]
        chain1 = ph.sem("chain1")
        chain2 = ph.sem("chain2")
        passed = ph.sem("passed")
        stats_ready = ph.sem("stats_ready")
        sd_ready = ph.sem("sd_ready")
        h_ready = ph.sem("h_ready")
        turned = ph.sem("turned")
        hT_ready = ph.sem("hT_ready")
        projected = ph.sem("projected")
        ext_ready = ph.sem("ext_ready")
        h_out = [ph.sem(f"h_out{k}") for k in range(TILE_RING)]
        ext_out = [ph.sem(f"ext_out{k}") for k in range(TILE_RING)]
        block = ph.block()

        loads = (first or final) + (not first) + (layer >= 2) + final
        if not final:
            W_dram, a_src, a_dst = io[f"W{layer}"], io[f"att_src{layer}"], io[f"att_dst{layer}"]
            heads = a_src.shape[0]
        n_att = 0 if final else (2 * H if heads == H else 2 * 2 * H)

        def head_view(ap):
            return ap.rearrange("p (h f) -> p h f", h=H)[:, :, 0:D]

        def by_head(ap):
            return ap.rearrange("p (h f) -> p h f", h=H)

        @block.sync
        def _(sp):
            if not first:
                for n, name in enumerate(("bias", "ln_g", "ln_b")):
                    sp.dma_start(vecs[:, n, :], broadcast_row(io[f"{name}{layer - 1}"])).then_inc(vecs_in, 16)
            if not final:
                sp.dma_start(W[:, :, :], W_dram.rearrange("(k p) o -> p k o", p=P)).then_inc(weights_in, 16)
                sp.wait_ge(att_clear, 1)
                for n, a in enumerate((a_src, a_dst)):
                    if heads == H:
                        for h in range(H):
                            o = (h * D) % P
                            sp.dma_start(att[o:o + D, h * D // P, n * H + h:n * H + h + 1],
                                         a[h:h + 1, :].rearrange("a d -> d a")).then_inc(weights_in, 16)
                    else:
                        for k in range(2):
                            for h in range(H):
                                sp.dma_start(att[:, k, n * H + h:n * H + h + 1],
                                             a[0:1, k * P:(k + 1) * P].rearrange("a d -> d a")).then_inc(weights_in, 16)

            def load(i, slot, last):
                n = slice(0, TAIL) if last else slice(0, P)
                if first or final:
                    sp.dma_start(X[n, slot, :], ring_rows(io["x"], i, slot, last)).then_inc(loaded[slot], 16)
                if not first:
                    sp.dma_start(rows[:, slot, :], padded_ring_rows(dr["rows"], i, slot)).then_inc(loaded[slot], 16)
                if layer >= 2:
                    sp.dma_start(prev[:, slot, :], padded_ring_rows(dr["h"], i, slot)).then_inc(loaded[slot], 16)
                if final:
                    sp.dma_start(mix[:, slot, :], padded_ring_rows(dr["mix"], i, slot)).then_inc(loaded[slot], 16)

            for slot in range(TILE_RING):
                load(0, slot, False)
            with sp.Fori(1, NB // TILE_RING) as i:
                for slot in range(TILE_RING):
                    sp.wait_ge(h_ready, TILE_RING * (i - 1) + slot + 2)
                    load(i, slot, False)
            sp.wait_ge(h_ready, NB - TILE_RING + 1)
            load(NB // TILE_RING, 0, True)

        @block.gpsimd
        def _(g):
            g.memset(att[:, :, :], 0.0).then_inc(att_clear, 1)
            g.memset(eps[:, :], LN_EPS).then_inc(consts, 1)
            if first:
                g.memset(acc[:, :, :], 0.0).then_inc(consts, 1)

            def step(i, slot, last):
                b = TILE_RING * i + slot
                g.wait_ge(h_ready, b + 2)
                to = "x2" if final else "h"
                g.dma_start(padded_ring_rows(dr[to], i, slot), Hn[:, slot, :]).then_inc(h_out[slot], 16)
                if not final:
                    g.wait_ge(ext_ready, b + 3)
                    g.dma_start(padded_ring_rows(dr["rows"], i, slot), ext[:, slot, :]).then_inc(ext_out[slot], 16)

            over_ring(g, step)
            if not first and not final:
                g.memset(acc[:, :, :], 0.0).then_inc(consts, 1)
            for slot in range(TILE_RING):
                n = NB // TILE_RING + (slot == 0)
                g.wait_ge(h_out[slot], 16 * n)
                if not final:
                    g.wait_ge(ext_out[slot], 16 * n)

        @block.vector
        def _(v):
            v.sem_inc(h_ready, 1)
            c0 = Chain(v, pre)
            if not final:
                v.wait_ge(w_turned, 1)
                v.tensor_copy(WT[:, :, :].rearrange("p a b -> p (a b)"), psW[:, :]).then_inc(wT_ready, 1)
                v.wait_ge(w_scored, 1)
                for k in range(2):
                    for n in range(2):
                        sc = psS[:, k * 2 * H + n * H:k * 2 * H + (n + 1) * H]
                        if n:
                            v.tensor_copy(Wx[:, k, RW:RW + H], sc).then_inc(wx_ready, 1)
                        else:
                            v.tensor_copy(by_head(Wx[:, k, 0:RW])[:, :, D], sc).then_inc(wx_ready, 1)
                    v.tensor_copy(head_view(Wx[:, k, 0:RW]), by_head(W[:, k, :])).then_inc(wx_ready, 1)
            if not first:
                as_, ad_, ms_ = own[:, :, :], ADM[:, :, 0:H], ADM[:, :, H:2 * H]
                tv = [tu[:, k, :].rearrange("p (b h) -> p b h", h=H) for k in range(2)]
                c0.add(v.tensor_tensor(tv[0], as_, ad_, ALU.add))
                c0.link(v.tensor_tensor(tv[1], ms_, ad_, ALU.add))
                c0.link(v.scalar_tensor_tensor(out=lr[:, :, :], in0=tu[:, :, :], scalar=SLOPE, in1=tu[:, :, :],
                                               op0=ALU.mult, op1=ALU.max))
                c0.link(v.tensor_tensor(tu[:, 0, :], lr[:, 0, :], lr[:, 1, :], ALU.subtract))
                v.wait_ge(es_ready, 1)
                sums = acc[:, :, :].rearrange("p b (h f) -> p b h f", h=H)[:, :, :, D]
                c0.link(v.tensor_tensor(zr[:, :, :], sums, es[:, :, :], ALU.add))
                c0.link(v.tensor_scalar(zr[:, :, :], zr[:, :, :], 1e-16, None, ALU.add))
                c0.link(v.reciprocal(zr[:, :, :], zr[:, :, :]))
                v.wait_ge(vecs_in, 48)

            N1 = 1 if first else 5
            N2 = 1 if first else 3 + (layer >= 2) + final

            def gather_in(i, slot, last):
                b = TILE_RING * i + slot
                ch = Chain(v, chain1, b * N1)
                v.wait_ge(loaded[slot], 16 * loads * (i + 1))
                if first:
                    o = X[:, slot, :]
                else:
                    o = O[:, slot, :]
                    oh = by_head(o)
                    a = acc[:, bass.ds(b, 1), :].rearrange("p a (h f) -> p (a h) f", h=H)[:, :, 0:D]
                    e = es[:, bass.ds(b, 1), :].rearrange("p a h -> p (a h)").unsqueeze(2).broadcast_to([P, H, D])
                    z = zr[:, bass.ds(b, 1), :].rearrange("p a h -> p (a h)").unsqueeze(2).broadcast_to([P, H, D])
                    ch.add(v.tensor_tensor(oh, head_view(rows[:, slot, :]), e, ALU.mult))
                    yield
                    ch.wait()
                    ch.add(v.tensor_tensor(oh, oh, a, ALU.add))
                    yield
                    ch.wait()
                    ch.add(v.tensor_tensor(oh, oh, z, ALU.mult))
                    yield
                    ch.wait()
                    ch.add(v.tensor_tensor(o, o, vecs[:, 0, :], ALU.add))
                    yield
                    ch.wait()
                ch.add(v.bn_stats(stats[:, slot, :], o))
                yield
                wait_apart(v, chain1, ch.base + ch.n, passed)
                v.bn_aggr(mv[:, slot, :], stats[:, slot, :]).then_inc(stats_ready, 1)
                assert ch.n == N1

            def finish(i, slot, last):
                b = TILE_RING * i + slot
                ch = Chain(v, chain2, b * N2)
                o = X[:, slot, :] if first else O[:, slot, :]
                hn = Hn[:, slot, :]
                v.wait_ge(sd_ready, b + 1)
                ch.add(v.reciprocal(rstd[:, slot, :], sd[:, slot, :]))
                yield
                ch.wait()
                if not is_zero(i):
                    v.wait_ge(h_out[slot], 16 * i)
                if not final:
                    v.wait_ge(turned, b + 1)
                if first:
                    v.tensor_scalar(hn, o, mv[:, slot, 0:1], rstd[:, slot, :], ALU.subtract, ALU.mult).then_inc(h_ready, 1)
                else:
                    ch.add(v.scalar_tensor_tensor(out=o, in0=o, scalar=mv[:, slot, 0:1], in1=vecs[:, 1, :],
                                                  op0=ALU.subtract, op1=ALU.mult))
                    yield
                    ch.wait()
                    ch.add(v.scalar_tensor_tensor(out=o, in0=o, scalar=rstd[:, slot, :], in1=vecs[:, 2, :],
                                                  op0=ALU.mult, op1=ALU.add))
                    yield
                    ch.wait()
                    if layer >= 2:
                        ch.add(v.tensor_tensor(o, o, prev[:, slot, :], ALU.add))
                        yield
                        ch.wait()
                    if final:
                        ch.add(v.scalar_tensor_tensor(out=o, in0=o, scalar=0.0, in1=X[:, slot, :],
                                                      op0=ALU.max, op1=ALU.add))
                        yield
                        ch.wait()
                        v.tensor_tensor(hn, o, mix[:, slot, :], ALU.add).then_inc(h_ready, 1)
                    else:
                        v.tensor_scalar(hn, o, 0.0, None, ALU.max).then_inc(h_ready, 1)
                assert ch.n == N2

            for _ in gather_in(0, 0, False):
                pass

            def step(i, slot, last):
                following = iter(()) if last else gather_in(i + (slot + 1) // TILE_RING, (slot + 1) % TILE_RING, False)
                for _ in zip_longest(following, finish(i, slot, last)):
                    pass

            over_ring(v, step)

        @block.scalar
        def _(a):
            a.wait_ge(consts, 1 + first)
            if not final:
                for s in (hT_ready, ext_ready):
                    a.sem_inc(s, 2)
            if not first:
                a.wait_ge(pre, 4)
                a.activation(es[:, :, :], tu[:, 0, :].rearrange("p (b h) -> p b h", h=H), ACT.Exp).then_inc(es_ready, 1)

            def std(slot, b):
                a.wait_ge(stats_ready, b + 1)
                a.activation(sd[:, slot, :], mv[:, slot, 1:2], ACT.Sqrt, bias=eps[:, :]).then_inc(sd_ready, 1)

            std(0, 0)

            def step(i, slot, last):
                b = TILE_RING * i + slot
                if not last:
                    std((slot + 1) % TILE_RING, b + 1)
                if final:
                    return
                a.wait_ge(turned, b + 3)
                a.wait_ge(projected, b + 1)
                a.activation(hT[:, slot, :, :].rearrange("p a b -> p (a b)"), psA[slot % 2][:, 0:C], ACT.Copy).then_inc(hT_ready, 1)
                a.wait_ge(projected, b + 3)
                if not is_zero(i):
                    a.wait_ge(ext_out[slot], 16 * i)
                scores = by_head(psB[slot % 2][:, 0:RW])[:, :, D]
                a.activation(ADM[:, bass.ds(b, 1), 0:H].rearrange("p a h -> p (a h)"), psB[slot % 2][:, RW:RW + H], ACT.Copy)
                a.activation(ADM[:, bass.ds(b, 1), H:2 * H].rearrange("p a h -> p (a h)"), scores, ACT.Copy)
                a.activation(own[:, bass.ds(b, 1), :].rearrange("p a h -> p (a h)"), scores, ACT.Copy)
                a.activation(ext[:, slot, :], psB[slot % 2][:, 0:RW], ACT.Copy).then_inc(ext_ready, 1)

            over_ring(a, step)

        @block.tensor
        def _(pe):
            if final:
                return
            pe.sem_inc(turned, 2)
            pe.sem_inc(projected, 2)
            pe.wait_ge(weights_in, 16 * (1 + n_att))
            for k in range(2):
                for o in range(2):
                    mm = pe.transpose(psW[:, (o * 2 + k) * P:(o * 2 + k + 1) * P], W[:, k, o * P:(o + 1) * P], st["ident"][:, :])
            mm.then_inc(w_turned, 1)
            pe.wait_ge(wT_ready, 1)
            for k in range(2):
                for o in range(2):
                    mm = pe.matmul(psS[:, k * 2 * H:(k + 1) * 2 * H], WT[:, o, k * P:(k + 1) * P], att[:, o, :],
                                   start=(o == 0), stop=(o == 1))
            mm.then_inc(w_scored, 1)
            pe.wait_ge(wx_ready, 6)

            def step(i, slot, last):
                b = TILE_RING * i + slot
                pe.wait_ge(h_ready, b + 2)
                pe.wait_ge(hT_ready, b + 1)
                for k in range(2):
                    mm = pe.transpose(psA[slot % 2][:, k * P:(k + 1) * P], Hn[:, slot, k * P:(k + 1) * P], st["ident"][:, :])
                mm.then_inc(turned, 1)
                pe.wait_ge(hT_ready, b + 3)
                pe.wait_ge(ext_ready, b + 1)
                for k in range(2):
                    mm = pe.matmul(psB[slot % 2][:, 0:RW + H], hT[:, slot, k, :], Wx[:, k, :], start=(k == 0), stop=(k == 1))
                mm.then_inc(projected, 1)

            over_ring(pe, step)


def edge_phase(nc, layer, st, dr):
    acc, ADM, ident, iota = st["acc"], st["ADM"], st["ident"], st["iota"]
    srcT, relT, lastT, words, rises = (st[n] for n in ("srcT", "relT", "lastT", "words", "rises"))
    S3 = WS * H
    GH4 = WG * H
    BANKS = 4
    with Phase(nc, f"edges{layer}") as ph:
        G = [ph.sb(f"G{r}", [P, WS, RW]) for r in range(RING)]
        index = [ph.sb(f"index{r}", [P, WS], I32) for r in range(RING)]
        reset = ph.sb("reset", [S3, RING, P], BF16)
        identb = ph.sb("identb", [P, P], BF16)
        OHb = [ph.sb(f"OHb{k}", [P, WS, P], BF16) for k in range(2)]
        OH = [ph.sb(f"OH{k}", [P, WS, P]) for k in range(2)]
        OHT = ph.sb("OHT", [P, WS, P], BF16)
        score = [ph.sb(f"score{k}", [P, S3]) for k in range(2)]
        run = ph.sb("run", [S3, P])
        masked = ph.sb("masked", [P, S3])
        rest = ph.sb("rest", [P, S3])
        lastv = ph.sb("lastv", [P, 3, WS, 8], BF16)
        absent = ph.sb("absent", [P, WS])
        seg = ph.sb("seg", [P, WS, H])
        here = ph.sb("here", [P, H, WG])
        before = ph.sb("before", [P, H, WG])
        after = ph.sb("after", [P, H, WG])
        node = [ph.sb(f"node{k}", [P, WG, 2 * H]) for k in range(2)]
        top = ph.sb("top", [P, WG, H])
        logit = ph.sb("logit", [P, WG + 1, H])
        fin = ph.sb("fin", [P, WG + 1, 2 * H])
        rest2 = ph.sb("rest2", [P, WG * 2 * H])
        parts = ph.sb("parts", [P, 3, WG, 2 * H], BF16)
        tu = ph.sb("tu", [P, S3])
        lr = ph.sb("lr", [P, S3])
        diff = ph.sb("diff", [P, S3])
        fd = ph.sb("fd", [P, H])
        fade = ph.sb("fade", [P, H])
        ps_s = ph.ps("ps_s", [P, 512])
        ps_t = [ph.ps(f"ps_t{k}", [P, 1024], BF16) for k in range(2)]
        ps_small = ph.ps("ps_small", [P, 2, WS, 8])
        ps_seg, ps_ad = ps_small[:, 0, :, :], ps_small[:, 1, :, :]
        ps_o = [ph.ps(f"ps_o{k}", [P, 512]) for k in range(BANKS)]

        consts = ph.sem("consts")
        index_ready = ph.sem("index_ready")
        gathered = [ph.sem(f"gathered{r}") for r in range(RING)]
        reset_in = [ph.sem(f"reset_in{r}") for r in range(RING)]
        score_ready = ph.sem("score_ready")
        score_turned = ph.sem("score_turned")
        ran = ph.sem("ran")
        run_turned = ph.sem("run_turned")
        lastv_ready = ph.sem("lastv_ready")
        oh_ready = ph.sem("oh_ready")
        oh_turned = ph.sem("oh_turned")
        oht_ready = ph.sem("oht_ready")
        ohf_ready = ph.sem("ohf_ready")
        node_ready = ph.sem("node_ready")
        seg_ready = ph.sem("seg_ready")
        top_ready = ph.sem("top_ready")
        top_kept = ph.sem("top_kept")
        parts_ready = ph.sem("parts_ready")
        ad_ready = ph.sem("ad_ready")
        diff_ready = ph.sem("diff_ready")
        weights_ready = ph.sem("weights_ready")
        fd_ready = ph.sem("fd_ready")
        fade_ready = ph.sem("fade_ready")
        weighed = ph.sem("weighed")
        summed = ph.sem("summed")
        added = ph.sem("added")
        faded = ph.sem("faded")
        chain = ph.sem("chain")
        passed = ph.sem("passed")
        passed_pool = ph.sem("passed_pool")
        block = ph.block()

        def by_head(ap):
            return ap.rearrange("p s (h f) -> p s h f", h=H)

        def ghj(ap):
            return ap.rearrange("p (g j) h -> p g h j", j=2)

        def as_ghj(ap):
            return ap.rearrange("p (g h j) -> p g h j", h=H, j=2)

        def row(ap, b):
            return ap[:, bass.ds(b, 1), :].rearrange("p a h -> p (a h)")

        def over_windows(eng, step):
            with eng.Fori(0, NW // RING - 1) as i:
                for r in range(RING):
                    step(i, r, False)
            for r in range(RING):
                step(NW // RING - 1, r, r == RING - 1)

        def exists(i, r, ahead):
            return not isinstance(i, int) or r + ahead < RING

        def blocks_of(eng, w):
            word = eng.value_load(words[0:1, bass.ds(w, 1)], min_val=0, max_val=64 * 2 ** (WG - 1) - 1)
            b = eng.snap(word & 63)
            for g in range(WG):
                b = nc.s_assert_within(b, 0, NB - 1, skip_runtime_bounds_check_because=ROWS_SEEN)
                yield b
                if g < WG - 1:
                    b = eng.snap(b + ((word >> (6 + g)) & 1))

        @block.sync
        def _(sp):
            def step(i, r, last):
                w = 4 * i + r
                sp.wait_ge(ran, w + 1)
                sp.dma_start(reset[:, r, :], dr["reset"].rearrange("g h j e -> (g h j) e")[bass.ds(w * S3, S3), :]
                             ).then_inc(reset_in[r], 16)

            over_windows(sp, step)

        @block.gpsimd
        def _(g):
            def step(i, r, last):
                w = 4 * i + r
                g.wait_ge(index_ready, w + 1)
                wait_apart(g, summed, WG * (w + 1), passed_pool)
                for s in range(WS):
                    g.indirect_dma_start(G[r][:, s, :], None, dr["rows"],
                                         bass.IndirectOffsetOnAxis(index[r][:, s:s + 1], 0)).then_inc(gathered[r], 16)

            over_windows(g, step)

        @block.scalar
        def _(a):
            a.sem_inc(oht_ready, 2)

            def make_index(w, r, i):
                if i is not None:
                    a.wait_ge(gathered[r], 16 * WS * i)
                a.activation(index[r][:, :], srcT[:, bass.ds(w * WG, WG), :].rearrange("p g j -> p (g j)"), ACT.Copy
                             ).then_inc(index_ready, 1)

            def copy_onehots(w, r):
                for c in range(2):
                    a.wait_ge(oh_turned, 2 * w + c + 1)
                    if c == 0:
                        a.wait_ge(ad_ready, w + 1)
                    a.activation(OHT[:, 8 * c:8 * c + 8, :].rearrange("p s e -> p (s e)"), ps_t[c][:, :], ACT.Copy
                                 ).then_inc(oht_ready, 1)
                a.wait_ge(summed, WG * w + WG * (RING - 1))
                for c in range(2):
                    a.activation(OH[r % 2][:, 8 * c:8 * c + 8, :], OHb[r % 2][:, 8 * c:8 * c + 8, :], ACT.Copy
                                 ).then_inc(ohf_ready, 1)

            def copy_scores(w, i, r):
                a.wait_ge(gathered[r], 16 * WS * (i + 1))
                a.wait_ge(diff_ready, w + 1)
                a.activation(as_ghj(score[r % 2][:, :]), ghj(by_head(G[r][:, :, :])[:, :, :, D]), ACT.Copy
                             ).then_inc(score_ready, 1)

            def load_node(w, r):
                for g, b in enumerate(blocks_of(a, w)):
                    if g == 0:
                        a.wait_ge(top_kept, WG * w + 1)
                    ins = a.activation(node[r % 2][:, g, :], row(ADM, b), ACT.Copy)
                ins.then_inc(node_ready, 1)

            def keep_top(w):
                for g, b in enumerate(blocks_of(a, w)):
                    if g == 0:
                        a.wait_ge(top_ready, w + 1)
                    else:
                        a.wait_ge(top_kept, WG * w + g + 1)
                    a.activation(row(ADM[:, :, H:2 * H], b), top[:, g, :], ACT.Copy).then_inc(top_kept, 1)

            def exponentials(w, r):
                a.wait_ge(diff_ready, w + 3)
                a.activation(ghj(by_head(G[r][:, :, :])[:, :, :, D]), as_ghj(diff[:, :]), ACT.Exp).then_inc(weights_ready, 1)
                a.wait_ge(fd_ready, w + 1)
                a.wait_ge(faded, w)
                a.activation(fade[:, :], fd[:, :], ACT.Exp).then_inc(fade_ready, 1)

            for r in range(RING):
                make_index(r, r, None)
            a.sem_inc(top_kept, 1)
            load_node(0, 0)
            copy_onehots(0, 0)
            copy_scores(0, 0, 0)
            exponentials(0, 0)
            copy_scores(1, 0, 1)
            keep_top(0)
            load_node(1, 1)

            def step(i, r, last):
                w = 4 * i + r
                n = (r + 1) % RING
                if not isinstance(i, int):
                    make_index(w + RING, r, i + 1)
                if last:
                    return
                copy_onehots(w + 1, n)
                exponentials(w + 1, n)
                if exists(i, r, 2):
                    copy_scores(w + 2, i + (r + 2) // RING, (r + 2) % RING)
                keep_top(w + 1)
                if exists(i, r, 2):
                    load_node(w + 2, r)

            over_windows(a, step)

        @block.tensor
        def _(pe):
            pe.sem_inc(summed, WG * RING)
            pe.sem_inc(ad_ready, 1)
            pe.wait_ge(consts, 3)

            def turn_onehots(w, r, c):
                pe.wait_ge(oh_ready, 4 * w + 2 * c + 2)
                pe.wait_ge(oht_ready, 2 * w + c + 1)
                for s in range(8):
                    mm = pe.transpose(ps_t[c][:, s * P:(s + 1) * P], OHb[r % 2][:, 8 * c + s, :], identb[:, :])
                mm.then_inc(oh_turned, 1)

            def turn_scores(w, r):
                pe.wait_ge(score_ready, w + 1)
                wait_apart(pe, ran, w + RING, passed)
                pe.transpose(ps_s[0:S3, 0:P], score[r % 2][:, :], ident[:, :]).then_inc(score_turned, 1)

            def turn_run(w):
                pe.wait_ge(ran, w + 1 + RING)
                wait_apart(pe, lastv_ready, w, passed)
                pe.transpose(ps_s[:, 256:256 + S3], run[:, :], ident[0:S3, 0:S3]).then_inc(run_turned, 1)

            def segments(w, r):
                pe.wait_ge(lastv_ready, w + 1)
                for s in range(WS):
                    for k in range(3):
                        mm = pe.matmul(ps_seg[:, s, 0:H + 1], OHb[r % 2][:, s, :], lastv[:, k, s, 0:H + 1],
                                       start=(k == 0), stop=(k == 2))
                mm.then_inc(seg_ready, 1)

            def spread(w, r):
                pe.wait_ge(oht_ready, 2 * w + 4)
                pe.wait_ge(parts_ready, w + 1)
                for s in range(WS):
                    for k in range(3):
                        mm = pe.matmul(ps_ad[:, s, :], OHT[:, s, :], parts[:, k, s // 2, :],
                                       start=(k == 0), stop=(k == 2))
                mm.then_inc(ad_ready, 1)

            def sums(w, r, groups):
                for g in groups:
                    if g % 4 == 0:
                        pe.wait_ge(ohf_ready, 2 * w + g // 4 + 1)
                    if g % 2 == 0:
                        pe.wait_ge(weighed, 4 * w + g // 2 + 1)
                    pe.wait_ge(added, WG * w + g + 1)
                    for j in range(2):
                        mm = pe.matmul(ps_o[g % BANKS][:, 0:RW], OH[r % 2][:, 2 * g + j, :], G[r][:, 2 * g + j, :],
                                       start=(j == 0), stop=(j == 1))
                    mm.then_inc(summed, 1)

            turn_onehots(0, 0, 0)
            turn_onehots(0, 0, 1)
            turn_scores(0, 0)
            turn_run(0)
            segments(0, 0)
            spread(0, 0)
            turn_onehots(1, 1, 0)
            turn_onehots(1, 1, 1)
            turn_scores(1, 1)

            def step(i, r, last):
                w = 4 * i + r
                n = (r + 1) % RING
                if not last:
                    turn_run(w + 1)
                sums(w, r, range(0, 1))
                if not last:
                    segments(w + 1, n)
                sums(w, r, range(1, 3))
                if not last:
                    spread(w + 1, n)
                sums(w, r, range(3, 6))
                if exists(i, r, 2):
                    turn_onehots(w + 2, r, 0)
                sums(w, r, range(6, WG))
                if exists(i, r, 2):
                    turn_onehots(w + 2, r, 1)
                    turn_scores(w + 2, r)

            over_windows(pe, step)

        @block.vector
        def _(v):
            v.sem_inc(ran, RING)
            v.sem_inc(diff_ready, 2)
            v.sem_inc(added, BANKS)
            v.tensor_copy(identb[:, :], ident[:, :]).then_inc(consts, 1)
            v.memset(lastv[:, :, :, :], 0.0).then_inc(consts, 1)
            v.memset(fin[:, :, :], 0.0).then_inc(consts, 1)
            v.wait_ge(consts, 3)

            def onehots(w, r, c, again=True):
                if again and c == 0:
                    v.wait_ge(ohf_ready, 2 * (w - 2) + 2)
                rel = relT[:, bass.ds(w * WG + 2 * c, 2), :].rearrange("p g j -> p (g j)")
                v.tensor_tensor(OHb[r % 2][:, 4 * c:4 * c + 4, :], iota[:, :].unsqueeze(1).broadcast_to([P, 4, P]),
                                rel.unsqueeze(2).broadcast_to([P, 4, P]), ALU.is_equal).then_inc(oh_ready, 1)

            STEPS = 21

            def split(ch, x, to, left):
                ch.link(v.tensor_copy(to[0], x))
                ch.link(v.tensor_tensor(left, x, to[0], ALU.subtract))
                ch.link(v.tensor_copy(to[1], left))
                return v.tensor_tensor(to[2], left, to[1], ALU.subtract)

            def scan(w, i, r):
                v.wait_ge(score_turned, w + 1)
                v.wait_ge(reset_in[r], 16 * (i + 1))
                v.wait_ge(run_turned, w)
                v.tensor_tensor_scan(run[:, :], reset[:, r, :], ps_s[0:S3, 0:P], -BIG, ALU.add, ALU.max).then_inc(ran, 1)
                return Chain(v, chain, STEPS * w)

            def last_values(w, ch):
                v.wait_ge(run_turned, w + 1)
                v.wait_ge(seg_ready, w)
                ls = lastT[:, bass.ds(w * WG, WG), :]
                ch.add(v.tensor_copy(lastv[:, 0, :, H], ls.rearrange("p g j -> p (g j)")))
                ch.link(v.tensor_tensor(as_ghj(masked[:, :]), as_ghj(ps_s[:, 256:256 + S3]),
                                        ls.unsqueeze(2).broadcast_to([P, WG, H, 2]), ALU.mult))
                split(ch, as_ghj(masked[:, :]), [ghj(lastv[:, k, :, 0:H]) for k in range(3)],
                      as_ghj(rest[:, :])).then_inc(lastv_ready, 1)

            def node_terms(w, r, ch):
                v.wait_ge(node_ready, w + 1)
                nd = node[r % 2]
                ch.add(v.tensor_tensor(logit[:, WG, :], nd[:, 0, 0:H], nd[:, 0, H:2 * H], ALU.add))
                ch.add(v.tensor_copy(fin[:, 0:WG, 0:H], nd[:, :, 0:H]))

            def maxima(w, r, ch):
                v.wait_ge(seg_ready, w + 1)
                ch.link(v.tensor_scalar(absent[:, :], ps_seg[:, :, H], 1.0, BIG, ALU.subtract, ALU.mult))
                ch.link(v.tensor_tensor(seg[:, :, :], ps_seg[:, :, 0:H], absent[:, :].unsqueeze(2).broadcast_to([P, WS, H]), ALU.add))
                pair = seg[:, :, :].rearrange("p (g j) h -> p h g j", j=2)
                ch.link(v.tensor_tensor(here[:, :, :], pair[:, :, :, 0], pair[:, :, :, 1], ALU.max))
                ch.link(v.tensor_tensor(here[:, :, :], here[:, :, :], node[r % 2][:, :, H:2 * H].rearrange("p g h -> p h g"), ALU.max))
                flat = [t[:, :, :].rearrange("p h g -> p (h g)") for t in (here, before, after)]
                rise = [rises[:, bass.ds(w, 1), k, :].rearrange("p a x -> p (a x)") for k in range(2)]
                ch.add(v.tensor_tensor_scan(flat[1], rise[0], flat[0], -BIG, ALU.add, ALU.max))
                ch.link(v.tensor_tensor_scan(flat[2][:, ::-1], rise[1], flat[0][:, ::-1], -BIG, ALU.add, ALU.max))
                v.wait_ge(top_kept, WG * w + 1)
                v.tensor_tensor(top[:, :, :].rearrange("p g h -> p h g"), before[:, :, :], after[:, :, :], ALU.max).then_inc(top_ready, 1)
                v.wait_ge(top_ready, w + 1)

            def greatest(w, r, ch):
                ch.link(v.tensor_tensor(logit[:, 0:WG, :], top[:, :, :], node[r % 2][:, :, 0:H], ALU.add))
                ch.link(v.scalar_tensor_tensor(out=fin[:, :, H:2 * H], in0=logit[:, :, :], scalar=SLOPE, in1=logit[:, :, :],
                                               op0=ALU.mult, op1=ALU.max))
                x = fin[:, 0:WG, :]
                split(ch, x, [parts[:, k, :, :] for k in range(3)],
                      rest2[:, :].rearrange("p (g x) -> p g x", g=WG)).then_inc(parts_ready, 1)
                v.wait_ge(fade_ready, w)
                v.tensor_tensor(fd[:, :], fin[:, WG, H:2 * H], fin[:, 0, H:2 * H], ALU.subtract).then_inc(fd_ready, 1)

            def spread_terms(w, r, ch):
                v.wait_ge(ad_ready, w + 2)
                ch.link(v.tensor_tensor(as_ghj(tu[:, :]), as_ghj(score[r % 2][:, :]), ghj(ps_ad[:, :, 0:H]), ALU.add))
                ch.link(v.scalar_tensor_tensor(out=lr[:, :], in0=tu[:, :], scalar=SLOPE, in1=tu[:, :],
                                               op0=ALU.mult, op1=ALU.max))
                v.wait_ge(weights_ready, w)
                ch.link(v.tensor_tensor(as_ghj(diff[:, :]), as_ghj(lr[:, :]), ghj(ps_ad[:, :, H:2 * H]), ALU.subtract))
                v.tensor_scalar(diff[:, :], diff[:, :], 0.0, None, ALU.min).then_inc(diff_ready, 1)
                assert ch.n == STEPS, ch.n

            def weigh(w, r, c):
                v.wait_ge(weights_ready, w + 1)
                g4 = G[r][:, 4 * c:4 * c + 4, :].rearrange("p s (h f) -> p (s h) f", h=H)
                v.tensor_tensor(g4[:, :, 0:D], g4[:, :, 0:D], g4[:, :, D:D + 1].broadcast_to([P, 4 * H, D]), ALU.mult
                                ).then_inc(weighed, 1)

            def fade_sums(w, b):
                v.wait_ge(fade_ready, w + 1)
                v.wait_ge(added, WG * w + BANKS)
                a = row(acc, b).rearrange("p (h f) -> p h f", h=H)
                v.tensor_tensor(a, a, fade[:, :].unsqueeze(2).broadcast_to([P, H, D + 1]), ALU.mult).then_inc(faded, 1)

            def add(w, g, b):
                v.wait_ge(summed, WG * w + g + 1 + WG * RING)
                if g == 0:
                    v.wait_ge(faded, w + 1)
                else:
                    v.wait_ge(added, WG * w + g + BANKS)
                a = row(acc, b)
                v.tensor_tensor(a, a, ps_o[g % BANKS][:, 0:RW], ALU.add).then_inc(added, 1)

            for w in range(2):
                for c in range(4):
                    onehots(w, w, c, False)
            ch = scan(0, 0, 0)
            last_values(0, ch)
            node_terms(0, 0, ch)
            maxima(0, 0, ch)
            greatest(0, 0, ch)
            spread_terms(0, 0, ch)

            def step(i, r, last):
                w = 4 * i + r
                n = (r + 1) % RING
                if not last:
                    ch = scan(w + 1, i + (r + 1) // RING, n)
                weigh(w, r, 0)
                if not last:
                    last_values(w + 1, ch)
                    node_terms(w + 1, n, ch)
                weigh(w, r, 1)
                if not last:
                    maxima(w + 1, n, ch)
                    greatest(w + 1, n, ch)
                this = blocks_of(v, w)
                b = next(this)
                fade_sums(w, b)
                add(w, 0, b)
                weigh(w, r, 2)
                add(w, 1, next(this))
                if not last:
                    spread_terms(w + 1, n, ch)
                weigh(w, r, 3)
                for g in range(2, WG):
                    add(w, g, next(this))
                    if g < 6 and exists(i, r, 2):
                        onehots(w + 2, r, g - 2)

            over_windows(v, step)
            v.wait_ge(added, WG * NW + BANKS)


def normalize_tiles(nc, name, buf, gain, offset):
    with Phase(nc, name) as ph:
        stats = ph.sb("stats", [P, NB, 6])
        mv = ph.sb("mv", [P, NB, 2])
        sd = ph.sb("sd", [P, NB])
        rstd = ph.sb("rstd", [P, NB])
        eps = ph.sb("eps", [P, 1])
        vecs = ph.sb("vecs", [P, 2, C])
        eps_set = ph.sem("eps_set")
        vecs_in = ph.sem("vecs_in")
        stats_done = ph.sem("stats_done")
        moments = ph.sem("moments")
        sd_ready = ph.sem("sd_ready")
        rstd_ready = ph.sem("rstd_ready")
        centred = ph.sem("centred")
        scaled = ph.sem("scaled")
        block = ph.block()

        @block.sync
        def _(sp):
            if gain is not None:
                for n, vec in enumerate((gain, offset)):
                    sp.dma_start(vecs[:, n, :], broadcast_row(vec)).then_inc(vecs_in, 16)

        @block.gpsimd
        def _(g):
            g.memset(eps[:, :], LN_EPS).then_inc(eps_set, 1)

        @block.scalar
        def _(a):
            a.wait_ge(eps_set, 1)
            a.wait_ge(moments, NB)
            a.activation(sd[:, :], mv[:, :, 1], ACT.Sqrt, bias=eps[:, :]).then_inc(sd_ready, 1)

        @block.vector
        def _(v):
            for b in range(NB):
                v.bn_stats(stats[:, b, :], buf[:, b, :]).then_inc(stats_done, 1)
            v.wait_ge(stats_done, NB)
            for b in range(NB):
                v.bn_aggr(mv[:, b, :], stats[:, b, :]).then_inc(moments, 1)
            v.wait_ge(sd_ready, 1)
            v.reciprocal(rstd[:, :], sd[:, :]).then_inc(rstd_ready, 1)
            v.wait_ge(rstd_ready, 1)
            if gain is None:
                for b in range(NB):
                    v.tensor_scalar(buf[:, b, :], buf[:, b, :], mv[:, b, 0:1], rstd[:, b:b + 1],
                                    ALU.subtract, ALU.mult).then_inc(scaled, 1)
            else:
                v.wait_ge(vecs_in, 32)
                for b in range(NB):
                    v.scalar_tensor_tensor(out=buf[:, b, :], in0=buf[:, b, :], scalar=mv[:, b, 0:1],
                                           in1=vecs[:, 0, :], op0=ALU.subtract, op1=ALU.mult).then_inc(centred, 1)
                v.wait_ge(centred, NB)
                for b in range(NB):
                    v.scalar_tensor_tensor(out=buf[:, b, :], in0=buf[:, b, :], scalar=rstd[:, b:b + 1],
                                           in1=vecs[:, 1, :], op0=ALU.mult, op1=ALU.add).then_inc(scaled, 1)
            v.wait_ge(scaled, NB)


def move_tiles(nc, name, to, of):
    with Phase(nc, name) as ph:
        moved = ph.sem("moved")
        cleared = ph.sem("cleared")
        block = ph.block()

        def rows(ap, a, z):
            return ap[:, :, :] if len(ap.shape) == 3 else ap.rearrange("(b p) c -> p b c", p=P)[:, a:z, :]

        @block.vector
        def _(v):
            if len(of.shape) == 2 and of.shape[0] == N:
                v.memset(to[:, NB - 1, :], 0.0).then_inc(cleared, 1)

        @block.sync
        def _(sp):
            if len(of.shape) == 2 and of.shape[0] == N:
                full = (NB - 1) * P
                sp.dma_start(to[:, 0:NB - 1, :], of[0:full, :].rearrange("(b p) c -> p b c", p=P)).then_inc(moved, 16)
                sp.wait_ge(cleared, 1)
                sp.dma_start(to[0:TAIL, NB - 1, :], of[full:N, :]).then_inc(moved, 16)
                sp.wait_ge(moved, 32)
            else:
                sp.dma_start(rows(to, 0, NB), rows(of, 0, NB)).then_inc(moved, 16)
                sp.wait_ge(moved, 16)


M_HEADS = 8
M_D = C // M_HEADS
GH = P // M_D


def turn_weights(nc, name, w_dram, out, ident):
    rows = w_dram.shape[0]
    with Phase(nc, name) as ph:
        w = ph.sb("w", [P, rows // P, C])
        ps = [ph.ps(f"ps{k}", [P, 512]) for k in range(2)]
        w_in = ph.sem("w_in")
        turned = ph.sem("turned")
        copied = ph.sem("copied")
        block = ph.block()

        @block.sync
        def _(sp):
            sp.dma_start(w[:, :, :], w_dram.rearrange("(r p) c -> p r c", p=P)).then_inc(w_in, 16)

        @block.tensor
        def _(pe):
            pe.wait_ge(w_in, 16)
            for r in range(rows // P):
                if r >= 2:
                    pe.wait_ge(copied, r - 1)
                for k in range(2):
                    mm = pe.transpose(ps[r % 2][:, k * P:(k + 1) * P], w[:, r, k * P:(k + 1) * P], ident[:, :])
                mm.then_inc(turned, 1)

        @block.vector
        def _(v):
            for r in range(rows // P):
                v.wait_ge(turned, r + 1)
                v.tensor_copy(out[:, :, r * P:(r + 1) * P], ps[r % 2][:, 0:C].rearrange("p (k o) -> p k o", k=2)
                              ).then_inc(copied, 1)
            v.wait_ge(copied, rows // P)


def tile_of(t, b):
    return t[:, bass.ds(b, 1), :].rearrange("p a c -> p (a c)")


def stage_tiles(g, buf, stage, staged, turned):
    def step(i, half, last):
        b = 2 * i + half
        g.wait_ge(turned, b + 1)
        g.tensor_copy(stage[:, half, :], tile_of(buf, b)).then_inc(staged, 1)

    over_tiles(g, step)


def turn_tile(pe, stage, half, ps, ident):
    for k in range(2):
        mm = pe.transpose(ps[:, k * P:(k + 1) * P], stage[:, half, k * P:(k + 1) * P], ident[:, :])
    return mm


def mix_keys(nc, st, XN, WT, KV):
    ident = st["ident"]
    VW = P + 2
    with Phase(nc, "keys") as ph:
        stage = ph.sb("stage", [P, 2, C])
        xs = ph.sb("xs", [P, 2, C])
        low = ph.sb("low", [P, 2, C])
        ex = ph.sb("ex", [P, 2, C])
        kp = ph.sb("kp", [P, 2, C])
        v1 = ph.sb("v1", [P, 2, 2, VW])
        psA = [ph.ps(f"psA{k}", [P, 512]) for k in range(2)]
        psK = [ph.ps(f"psK{k}", [P, 512]) for k in range(2)]
        psV = [ph.ps(f"psV{k}", [P, 512]) for k in range(2)]
        staged = ph.sem("staged")
        turned = ph.sem("turned")
        xT_ready = ph.sem("xT_ready")
        kv_ready = ph.sem("kv_ready")
        low_ready = ph.sem("low_ready")
        ex_ready = ph.sem("ex_ready")
        v_ready = ph.sem("v_ready")
        kp_ready = ph.sem("kp_ready")
        outer = ph.sem("outer")
        ones_set = ph.sem("ones_set")
        cleared = ph.sem("cleared")
        kv_out = ph.sem("kv_out")
        block = ph.block()

        @block.gpsimd
        def _(g):
            g.memset(v1[:, :, :, P:VW], 1.0).then_inc(ones_set, 1)
            g.memset(KV[:, :, :], 0.0).then_inc(cleared, 1)
            stage_tiles(g, XN, stage, staged, turned)

        @block.tensor
        def _(pe):
            for s in (turned, kv_ready, outer):
                pe.sem_inc(s, 2)
            pe.wait_ge(ones_set, 1)

            def keys_values(b, half):
                pe.wait_ge(staged, b + 1)
                pe.wait_ge(xT_ready, b + 1)
                turn_tile(pe, stage, half, psA[half], ident).then_inc(turned, 1)
                pe.wait_ge(xT_ready, b + 3)
                pe.wait_ge(kp_ready, b + 1)
                pe.wait_ge(v_ready, b + 1)
                for k in range(2):
                    mm = pe.matmul(psK[half][:, :], xs[:, half, k * P:(k + 1) * P], WT[:, k, C:3 * C],
                                   start=(k == 0), stop=(k == 1))
                mm.then_inc(kv_ready, 1)

            def outers(b, half, first, last):
                n = TAIL if last else P
                pe.wait_ge(kp_ready, b + 3)
                pe.wait_ge(v_ready, b + 3)
                for g in range(2):
                    mm = pe.matmul(psV[g][:, 0:VW], kp[0:n, half, g * P:(g + 1) * P], v1[0:n, half, g, :],
                                   start=first, stop=last)
                mm.then_inc(outer, 1)

            keys_values(0, 0)
            keys_values(1, 1)
            outers(0, 0, True, False)
            with pe.Fori(1, (NB - 1) // 2) as i:
                keys_values(2 * i, 0)
                outers(2 * i - 1, 1, False, False)
                keys_values(2 * i + 1, 1)
                outers(2 * i, 0, False, False)
            keys_values(NB - 1, 0)
            outers(NB - 2, 1, False, False)
            outers(NB - 1, 0, False, True)

        @block.scalar
        def _(a):
            a.sem_inc(xT_ready, 2)
            a.sem_inc(v_ready, 2)
            a.wait_ge(ones_set, 1)

            def step(i, half, last):
                b = 2 * i + half
                a.wait_ge(turned, b + 3)
                a.wait_ge(kv_ready, b + 1)
                a.activation(xs[:, half, :], psA[half][:, 0:C], ACT.Copy).then_inc(xT_ready, 1)
                a.wait_ge(kv_ready, b + 3)
                a.wait_ge(outer, b + 1)
                a.activation(v1[:, half, :, 0:P], psK[half][:, C:2 * C].rearrange("p (g c) -> p g c", g=2), ACT.Copy
                             ).then_inc(v_ready, 1)
                a.wait_ge(low_ready, b + 1)
                a.wait_ge(kp_ready, b + 1)
                a.activation(ex[:, half, :], low[:, half, :], ACT.Exp).then_inc(ex_ready, 1)

            over_tiles(a, step)

        @block.vector
        def _(v):
            v.sem_inc(kp_ready, 2)

            def step(i, half, last):
                b = 2 * i + half
                v.wait_ge(kv_ready, b + 3)
                v.wait_ge(kp_ready, b + 1)
                v.wait_ge(v_ready, b + 3)
                v.tensor_scalar(low[:, half, :], psK[half][:, 0:C], 0.0, None, ALU.min).then_inc(low_ready, 1)
                v.wait_ge(ex_ready, b + 1)
                v.wait_ge(outer, b + 1)
                v.scalar_tensor_tensor(out=kp[:, half, :], in0=psK[half][:, 0:C], scalar=0.0, in1=ex[:, half, :],
                                       op0=ALU.max, op1=ALU.add).then_inc(kp_ready, 1)

            over_tiles(v, step)
            v.wait_ge(outer, NB + 2)
            v.wait_ge(cleared, 1)
            for g in range(2):
                for h in range(GH):
                    r = slice(h * M_D, (h + 1) * M_D)
                    v.tensor_copy(KV[r, g, r], psV[g][r, r]).then_inc(kv_out, 1)
                    v.tensor_copy(KV[r, g, P + h:P + h + 1], psV[g][r, P:P + 1]).then_inc(kv_out, 1)
            v.wait_ge(kv_out, 4 * GH)


def mix_queries(nc, st, XN, WT, KV):
    ident = st["ident"]
    with Phase(nc, "queries") as ph:
        stage = ph.sb("stage", [P, 2, C])
        xs = ph.sb("xs", [P, 2, C])
        low = ph.sb("low", [P, 2, C])
        ex = ph.sb("ex", [P, 2, C])
        qp = ph.sb("qp", [P, 2, C])
        den = ph.sb("den", [P, 2, M_HEADS])
        t = ph.sb("t", [P, 2, C])
        psA = [ph.ps(f"psA{k}", [P, 512]) for k in range(2)]
        psQ = [ph.ps(f"psQ{k}", [P, 512]) for k in range(2)]
        psT = [ph.ps(f"psT{k}", [P, 512]) for k in range(2)]
        staged = ph.sem("staged")
        turned = ph.sem("turned")
        xT_ready = ph.sem("xT_ready")
        q_ready = ph.sem("q_ready")
        low_ready = ph.sem("low_ready")
        ex_ready = ph.sem("ex_ready")
        qp_ready = ph.sem("qp_ready")
        read = ph.sem("read")
        chain = ph.sem("chain")
        mixed = ph.sem("mixed")
        block = ph.block()
        KW = P + GH

        @block.gpsimd
        def _(g):
            stage_tiles(g, XN, stage, staged, turned)

        @block.tensor
        def _(pe):
            for s in (turned, q_ready, read):
                pe.sem_inc(s, 2)

            def queries(b, half):
                pe.wait_ge(staged, b + 1)
                pe.wait_ge(xT_ready, b + 1)
                turn_tile(pe, stage, half, psA[half], ident).then_inc(turned, 1)
                pe.wait_ge(xT_ready, b + 3)
                pe.wait_ge(qp_ready, b + 1)
                for g in range(2):
                    for k in range(2):
                        mm = pe.matmul(psQ[half][:, g * P:(g + 1) * P], WT[:, k, g * P:(g + 1) * P],
                                       xs[:, half, k * P:(k + 1) * P], start=(k == 0), stop=(k == 1))
                mm.then_inc(q_ready, 1)

            def reads(b, half):
                pe.wait_ge(qp_ready, b + 3)
                pe.wait_ge(mixed, b + 1)
                for g in range(2):
                    mm = pe.matmul(psT[half][:, g * KW:(g + 1) * KW], qp[:, half, g * P:(g + 1) * P], KV[:, g, :],
                                   start=True, stop=True)
                mm.then_inc(read, 1)

            queries(0, 0)

            def step(i, half, last):
                b = 2 * i + half
                if not last:
                    queries(b + 1, 1 - half)
                reads(b, half)

            over_tiles(pe, step)

        @block.scalar
        def _(a):
            a.sem_inc(xT_ready, 2)

            def step(i, half, last):
                b = 2 * i + half
                a.wait_ge(turned, b + 3)
                a.wait_ge(q_ready, b + 1)
                a.activation(xs[:, half, :], psA[half][:, 0:C], ACT.Copy).then_inc(xT_ready, 1)
                a.wait_ge(low_ready, b + 1)
                a.wait_ge(qp_ready, b + 1)
                a.activation(ex[:, half, :], low[:, half, :], ACT.Exp).then_inc(ex_ready, 1)

            over_tiles(a, step)

        @block.vector
        def _(v):
            v.sem_inc(qp_ready, 2)
            v.sem_inc(mixed, 2)

            def feature(b, half):
                v.wait_ge(q_ready, b + 3)
                v.wait_ge(qp_ready, b + 1)
                v.tensor_scalar(low[:, half, :], psQ[half][:, 0:C], 0.0, None, ALU.min).then_inc(low_ready, 1)
                v.wait_ge(ex_ready, b + 1)
                v.wait_ge(read, b + 1)
                v.scalar_tensor_tensor(out=qp[:, half, :], in0=psQ[half][:, 0:C], scalar=0.0, in1=ex[:, half, :],
                                       op0=ALU.max, op1=ALU.add).then_inc(qp_ready, 1)

            def result(b, half):
                ch = Chain(v, chain, 3 * b)
                v.wait_ge(read, b + 3)
                v.wait_ge(mixed, b + 1)
                r = psT[half][:, 0:2 * KW].rearrange("p (g k) -> p g k", g=2)
                d = den[:, half, :].rearrange("p (g h) -> p g h", g=2)
                ch.link(v.tensor_scalar(d, r[:, :, P:KW], 1e-6, None, ALU.add))
                ch.link(v.reciprocal(den[:, half, :], den[:, half, :]))
                for g in range(2):
                    ins = v.tensor_tensor(t[:, half, g * P:(g + 1) * P].rearrange("p (h m) -> p h m", h=GH),
                                          r[:, g, 0:P].rearrange("p (h m) -> p h m", h=GH),
                                          d[:, g, :].unsqueeze(2).broadcast_to([P, GH, M_D]), ALU.mult)
                    if g:
                        ch.link(ins)
                assert ch.n == 3
                v.wait_ge(staged, b + 1)
                v.tensor_tensor(tile_of(XN, b), tile_of(XN, b), t[:, half, :], ALU.add).then_inc(mixed, 1)

            feature(0, 0)

            def step(i, half, last):
                b = 2 * i + half
                if not last:
                    feature(b + 1, 1 - half)
                result(b, half)

            over_tiles(v, step)
            v.wait_ge(mixed, NB + 2)


def mix_mlp(nc, st, io, XN, W1T, W2T):
    ident = st["ident"]
    with Phase(nc, "mlp") as ph:
        stage = ph.sb("stage", [P, 2, C])
        xs = ph.sb("xs", [P, 2, C])
        hs = ph.sb("hs", [P, 2, C])
        b1 = ph.sb("b1", [P, 2])
        b2 = ph.sb("b2", [P, C])
        t = ph.sb("t", [P, 2, C])
        psA = [ph.ps(f"psA{k}", [P, 512]) for k in range(2)]
        psH = [ph.ps(f"psH{k}", [P, 512]) for k in range(2)]
        psY = [ph.ps(f"psY{k}", [P, 512]) for k in range(2)]
        biases_in = ph.sem("biases_in")
        staged = ph.sem("staged")
        turned = ph.sem("turned")
        xT_ready = ph.sem("xT_ready")
        hidden = ph.sem("hidden")
        gelu_ready = ph.sem("gelu_ready")
        y_ready = ph.sem("y_ready")
        biased = ph.sem("biased")
        added = ph.sem("added")
        block = ph.block()

        @block.sync
        def _(sp):
            with nc.allow_non_contiguous_dma(reason="256 words, once"):
                sp.dma_start(b1[:, :], io["mix_b1"].rearrange("(k p) -> p k", p=P)).then_inc(biases_in, 16)
            sp.dma_start(b2[:, :], broadcast_row(io["mix_b2"])).then_inc(biases_in, 16)

        @block.gpsimd
        def _(g):
            stage_tiles(g, XN, stage, staged, turned)

        @block.tensor
        def _(pe):
            for s in (turned, hidden, y_ready):
                pe.sem_inc(s, 2)

            def up(b, half):
                pe.wait_ge(staged, b + 1)
                pe.wait_ge(xT_ready, b + 1)
                turn_tile(pe, stage, half, psA[half], ident).then_inc(turned, 1)
                pe.wait_ge(xT_ready, b + 3)
                pe.wait_ge(gelu_ready, b + 1)
                for g in range(2):
                    for k in range(2):
                        mm = pe.matmul(psH[half][:, g * P:(g + 1) * P], W1T[:, k, g * P:(g + 1) * P],
                                       xs[:, half, k * P:(k + 1) * P], start=(k == 0), stop=(k == 1))
                mm.then_inc(hidden, 1)

            def down(b, half):
                pe.wait_ge(gelu_ready, b + 3)
                pe.wait_ge(biased, b + 1)
                for k in range(2):
                    mm = pe.matmul(psY[half][:, 0:C], hs[:, half, k * P:(k + 1) * P], W2T[:, k, :],
                                   start=(k == 0), stop=(k == 1))
                mm.then_inc(y_ready, 1)

            up(0, 0)

            def step(i, half, last):
                b = 2 * i + half
                if not last:
                    up(b + 1, 1 - half)
                down(b, half)

            over_tiles(pe, step)

        @block.scalar
        def _(a):
            a.sem_inc(xT_ready, 2)
            a.sem_inc(gelu_ready, 2)
            a.wait_ge(biases_in, 32)

            def turn(b, half):
                a.wait_ge(turned, b + 3)
                a.wait_ge(hidden, b + 1)
                a.activation(xs[:, half, :], psA[half][:, 0:C], ACT.Copy).then_inc(xT_ready, 1)

            turn(0, 0)

            def step(i, half, last):
                b = 2 * i + half
                if not last:
                    turn(b + 1, 1 - half)
                a.wait_ge(hidden, b + 3)
                a.wait_ge(y_ready, b + 1)
                for g in range(2):
                    ins = a.activation(hs[:, half, g * P:(g + 1) * P], psH[half][:, g * P:(g + 1) * P], ACT.Gelu,
                                       bias=b1[:, g:g + 1])
                ins.then_inc(gelu_ready, 1)

            over_tiles(a, step)

        @block.vector
        def _(v):
            v.sem_inc(biased, 2)
            v.sem_inc(added, 1)
            v.wait_ge(biases_in, 32)

            def step(i, half, last):
                b = 2 * i + half
                v.wait_ge(y_ready, b + 3)
                v.wait_ge(added, b + 1)
                v.tensor_tensor(t[:, half, :], psY[half][:, 0:C], b2[:, :], ALU.add).then_inc(biased, 1)
                v.wait_ge(biased, b + 3)
                v.wait_ge(staged, b + 1)
                v.tensor_tensor(tile_of(XN, b), tile_of(XN, b), t[:, half, :], ALU.add).then_inc(added, 1)

            over_tiles(v, step)
            v.wait_ge(added, NB + 1)


EX = 8
FH = 512
HC = FH // P
GT = 4


def route(nc, st, io, XN, xT, wts):
    ident, iota = st["ident"], st["iota"]
    with Phase(nc, "route") as ph:
        stage = ph.sb("stage", [P, 2, C])
        xs = ph.sb("xs", [P, 2, C])
        Wr = ph.sb("Wr", [P, 2, EX])
        br = ph.sb("br", [P, EX])
        lg = ph.sb("lg", [P, NB, EX])
        top = ph.sb("top", [P, NB, 8])
        topi = ph.sb("topi", [P, NB, 8], mybir.dt.uint32)
        topf = ph.sb("topf", [P, NB, 2])
        gap = ph.sb("gap", [P, NB])
        w = ph.sb("w", [P, NB, 2])
        den = ph.sb("den", [P, NB])
        pick = ph.sb("pick", [P, 2, NB, EX])
        psA = [ph.ps(f"psA{k}", [P, 512]) for k in range(2)]
        psL = [ph.ps(f"psL{k}", [P, 512]) for k in range(2)]
        router_in = ph.sem("router_in")
        staged = ph.sem("staged")
        turned = ph.sem("turned")
        xT_ready = ph.sem("xT_ready")
        kept = ph.sem("kept")
        logits = ph.sem("logits")
        biased = ph.sem("biased")
        topped = ph.sem("topped")
        found = ph.sem("found")
        chain = ph.sem("chain")
        gap_ready = ph.sem("gap_ready")
        exp_ready = ph.sem("exp_ready")
        block = ph.block()

        @block.sync
        def _(sp):
            sp.dma_start(Wr[:, :, :], io["ffn_Wr"].rearrange("(k p) e -> p k e", p=P)).then_inc(router_in, 16)
            sp.dma_start(br[:, :], broadcast_row(io["ffn_br"])).then_inc(router_in, 16)

        @block.gpsimd
        def _(g):
            stage_tiles(g, XN, stage, staged, turned)

        @block.tensor
        def _(pe):
            for s in (turned, logits):
                pe.sem_inc(s, 2)
            pe.wait_ge(router_in, 32)

            def step(i, half, last):
                b = 2 * i + half
                pe.wait_ge(staged, b + 1)
                pe.wait_ge(kept, b - 1 + 2)
                turn_tile(pe, stage, half, psA[half], ident).then_inc(turned, 1)
                pe.wait_ge(xT_ready, b + 3)
                pe.wait_ge(biased, b + 1)
                for k in range(2):
                    mm = pe.matmul(psL[half][:, 0:EX], xs[:, half, k * P:(k + 1) * P], Wr[:, k, :],
                                   start=(k == 0), stop=(k == 1))
                mm.then_inc(logits, 1)

            over_tiles(pe, step)

        @block.scalar
        def _(a):
            a.sem_inc(xT_ready, 2)
            a.sem_inc(kept, 2)

            def step(i, half, last):
                b = 2 * i + half
                a.wait_ge(turned, b + 3)
                a.wait_ge(logits, b + 1)
                a.activation(xs[:, half, :], psA[half][:, 0:C], ACT.Copy).then_inc(xT_ready, 1)
                a.activation(xT[:, :, bass.ds(b * P, P)], psA[half][:, 0:C].rearrange("p (k t) -> p k t", k=2), ACT.Copy
                             ).then_inc(kept, 1)

            over_tiles(a, step)
            a.wait_ge(gap_ready, 1)
            a.activation(w[:, :, 1], gap[:, :], ACT.Exp).then_inc(exp_ready, 1)

        @block.vector
        def _(v):
            v.sem_inc(biased, 2)
            v.wait_ge(router_in, 32)

            def step(i, half, last):
                b = 2 * i + half
                v.wait_ge(logits, b + 3)
                v.tensor_tensor(tile_of(lg, b), psL[half][:, 0:EX], br[:, :], ALU.add).then_inc(biased, 1)

            over_tiles(v, step)
            v.wait_ge(biased, NB + 2)
            for b in range(NB):
                v.max(top[:, b, :], lg[:, b, :]).then_inc(topped, 1)
            v.wait_ge(topped, NB)
            for b in range(NB):
                v.max_index(topi[:, b, :], top[:, b, :], lg[:, b, :]).then_inc(found, 1)
            v.tensor_tensor(gap[:, :], top[:, :, 1], top[:, :, 0], ALU.subtract).then_inc(gap_ready, 1)
            v.wait_ge(found, NB)
            ch = Chain(v, chain)
            ch.link(v.tensor_copy(topf[:, :, :], topi[:, :, 0:2]))
            v.wait_ge(exp_ready, 1)
            ch.link(v.tensor_scalar(den[:, :], w[:, :, 1], 1.0, None, ALU.add))
            ch.link(v.reciprocal(den[:, :], den[:, :]))
            ch.add(v.tensor_copy(w[:, :, 0], den[:, :]))
            ch.link(v.tensor_tensor(w[:, :, 1], w[:, :, 1], den[:, :], ALU.mult))
            places = iota[:, 0:EX].unsqueeze(1).broadcast_to([P, NB, EX])
            for k in range(2):
                ch.add(v.tensor_tensor(pick[:, k, :, :], places, topf[:, :, k:k + 1].broadcast_to([P, NB, EX]), ALU.is_equal))
            ch.wait()
            for k in range(2):
                ch.add(v.tensor_tensor(pick[:, k, :, :], pick[:, k, :, :], w[:, :, k:k + 1].broadcast_to([P, NB, EX]), ALU.mult))
            ch.wait()
            ch.link(v.tensor_tensor(wts[:, :, :], pick[:, 0, :, :], pick[:, 1, :, :], ALU.add))


def experts(nc, st, io, xT, wts, dr, out):
    ident = st["ident"]
    with Phase(nc, "experts") as ph:
        W1 = ph.sb("W1", [P, EX, 2, FH])
        W2 = ph.sb("W2", [P, EX, HC, C])
        b1 = ph.sb("b1", [P, EX, HC])
        b2 = ph.sb("b2", [EX, C])
        wst = ph.sb("wst", [P, GT, EX])
        wT = ph.sb("wT", [EX, GT * P])
        hT = ph.sb("hT", [P, 2, HC, GT * P])
        Y = ph.sb("Y", [P, 2, GT, C])
        X2 = ph.sb("X2", [P, 2, GT, C])
        psH = [ph.ps(f"psH{k}", [P, 512]) for k in range(HC)]
        psY = [ph.ps(f"psY{k}", [P, 512]) for k in range(GT)]
        w1_in = ph.sem("w1_in")
        w2_in = ph.sem("w2_in")
        x2_in = [ph.sem(f"x2_in{k}") for k in range(2)]
        staged = ph.sem("staged")
        w_turned = ph.sem("w_turned")
        wT_ready = ph.sem("wT_ready")
        hidden = ph.sem("hidden")
        gelu_ready = ph.sem("gelu_ready")
        y_ready = ph.sem("y_ready")
        y_read = ph.sem("y_read")
        stored = ph.sem("stored")
        y_out = [ph.sem(f"y_out{k}") for k in range(2)]
        block = ph.block()
        FULL = NB // GT
        assert NB % GT == 1 and FULL % 2 == 0
        R = EX + 1

        def over_groups(eng, step):
            with eng.Fori(0, FULL // 2) as i:
                step(i, 0, GT)
                step(i, 1, GT)
            step(FULL // 2, 0, 1)

        @block.sync
        def _(sp):
            for e in range(EX):
                sp.dma_start(W1[:, e, :, :], io["ffn_W1"][e].rearrange("(k p) f -> p k f", p=P)).then_inc(w1_in, 16)
            with nc.allow_non_contiguous_dma(reason="4096 words, once"):
                sp.dma_start(b1[:, :, :], io["ffn_b1"].rearrange("e (c p) -> p e c", p=P)).then_inc(w1_in, 16)
            sp.dma_start(b2[:, :], io["ffn_b2"]).then_inc(w2_in, 16)
            for e in range(EX):
                sp.dma_start(W2[:, e, :, :], io["ffn_W2"][e].rearrange("(c p) o -> p c o", p=P)).then_inc(w2_in, 16)

            def step(i, half, nt):
                q = 2 * i + half
                sp.wait_ge(stored, q + 1)
                sp.dma_start(X2[:, half, 0:nt, :], dr["x2"][bass.ds(q * GT * P, nt * P), :].rearrange("(t p) c -> p t c", p=P)
                             ).then_inc(x2_in[half], 16)

            over_groups(sp, step)

        @block.gpsimd
        def _(g):
            g.sem_inc(stored, 2)

            def step(i, half, nt):
                q = 2 * i + half
                g.wait_ge(w_turned, q + 1)
                g.tensor_copy(wst[:, 0:nt, :], wts[:, bass.ds(q * GT, nt), :]).then_inc(staged, 1)
                g.wait_ge(y_read, (q + 1) * R * GT + 1 if nt == GT else q * R * GT + R + 1)
                if nt == GT:
                    g.dma_start(out[bass.ds(q * GT * P, GT * P), :].rearrange("(t p) c -> p t c", p=P), Y[:, half, :, :]
                                ).then_inc(y_out[half], 16)
                else:
                    g.dma_start(out[(NB - 1) * P:N, :], Y[0:TAIL, half, 0, :]).then_inc(y_out[half], 16)
                g.wait_ge(y_out[half], 16 * (i + 1))
                g.sem_inc(stored, 1)

            over_groups(g, step)

        @block.tensor
        def _(pe):
            pe.sem_inc(w_turned, 1)
            pe.sem_inc(y_ready, 1)
            pe.wait_ge(w1_in, 16 * (EX + 1))
            pe.wait_ge(w2_in, 16 * (EX + 1))

            def step(i, half, nt):
                q = 2 * i + half
                h0 = q * EX * HC
                y0 = q * R * GT + 1

                def up(e):
                    for c in range(HC):
                        pe.wait_ge(gelu_ready, h0 + e * HC + c + 1)
                        if e == 0:
                            pe.wait_ge(wT_ready, q + 1)
                        for k in range(2):
                            mm = pe.matmul(psH[c][:, 0:nt * P], W1[:, e, k, c * P:(c + 1) * P],
                                           xT[:, k, bass.ds(q * GT * P, nt * P)], start=(k == 0), stop=(k == 1))
                        mm.then_inc(hidden, 1)

                def down(e):
                    pe.wait_ge(gelu_ready, h0 + (e + 2) * HC)
                    for t in range(nt):
                        pe.wait_ge(y_read, y0 + (e + 1) * nt + t + 1 - nt)
                        for c in range(HC):
                            mm = pe.matmul(psY[t][:, 0:C], hT[:, e % 2, c, t * P:(t + 1) * P], W2[:, e, c, :],
                                           start=(c == 0), stop=(c == HC - 1))
                        mm.then_inc(y_ready, 1)

                pe.wait_ge(staged, q + 1)
                pe.wait_ge(gelu_ready, h0 + HC)
                for t in range(nt):
                    mm = pe.transpose(psH[0][0:EX, t * P:(t + 1) * P], wst[:, t, :], ident[:, :])
                mm.then_inc(w_turned, 1)
                pe.wait_ge(wT_ready, q + 1)
                pe.wait_ge(y_read, y0)
                for t in range(nt):
                    pe.matmul(psY[t][:, 0:C], wT[:, t * P:(t + 1) * P], b2[:, :], start=True, stop=True).then_inc(y_ready, 1)
                up(0)
                for e in range(1, EX):
                    up(e)
                    down(e - 1)
                down(EX - 1)

            over_groups(pe, step)

        @block.scalar
        def _(a):
            a.sem_inc(gelu_ready, HC)
            a.wait_ge(w1_in, 16 * (EX + 1))

            def step(i, half, nt):
                q = 2 * i + half
                h0 = q * EX * HC
                y0 = q * R * GT + 1
                a.wait_ge(w_turned, q + 2)
                a.wait_ge(y_ready, y0)
                a.activation(wT[:, 0:nt * P], psH[0][0:EX, 0:nt * P], ACT.Copy).then_inc(wT_ready, 1)
                for e in range(EX):
                    if e >= 2:
                        a.wait_ge(y_ready, y0 + e * nt)
                    for c in range(HC):
                        a.wait_ge(hidden, h0 + e * HC + c + 1)
                        a.activation(hT[:, e % 2, c, 0:nt * P], psH[c][:, 0:nt * P], ACT.Gelu, bias=b1[:, e, c:c + 1]
                                     ).then_inc(gelu_ready, 1)

            over_groups(a, step)

        @block.vector
        def _(v):
            v.sem_inc(y_read, 1)

            def step(i, half, nt):
                q = 2 * i + half
                y0 = q * R * GT + 1
                v.wait_ge(x2_in[half], 16 * (i + 1))
                v.wait_ge(stored, q + 1)
                for e in range(-1, EX):
                    for t in range(nt):
                        v.wait_ge(y_ready, y0 + (e + 1) * nt + t + 1)
                        y = Y[:, half, t, :]
                        if e < 0:
                            ins = v.tensor_tensor(y, psY[t][:, 0:C], X2[:, half, t, :], ALU.add)
                        else:
                            v.wait_ge(y_read, y0 + e * nt + t + 1)
                            ins = v.scalar_tensor_tensor(out=y, in0=psY[t][:, 0:C],
                                                         scalar=wts[:, bass.ds(q * GT + t, 1), e:e + 1].rearrange("p a b -> p (a b)"),
                                                         in1=y, op0=ALU.mult, op1=ALU.add)
                        ins.then_inc(y_read, 1)

            over_groups(v, step)


def build(nc, io, out):
    def dram(name, shape, dt=F32):
        return nc.dram_tensor(name, shape, dt, kind="Internal").ap()

    dr = {"src_pad": dram("src_pad", (TG + 1, GE), I32), "dst_pad": dram("dst_pad", (TG + 1, GE), I32),
          "reset": dram("reset", (NG, H, 2, P), BF16), "rows": dram("rows", (NPAD, RW)),
          "h": dram("h", (NPAD, C)), "mix": dram("mix", (NPAD, C)), "x2": dram("x2", (NPAD, C))}

    with ExitStack() as ctx:
        def sb(name, shape, dt=F32):
            return ctx.enter_context(nc.sbuf_tensor(name, shape, dt))

        st = {"ident": sb("ident", [P, P]), "iota": sb("iota", [P, P])}
        with ExitStack() as inner:
            def sbi(name, shape, dt=F32):
                return inner.enter_context(nc.sbuf_tensor(name, shape, dt))

            for n in ("srcT", "relT", "lastT"):
                st[n] = sbi(n, [P, NG, 2])
            st["words"] = sbi("words", [P, NW], I32)
            st["rises"] = sbi("rises", [P, NW, 2, H * WG], BF16)
            prepare_walk(nc, io["src"], io["dst"], st, dr)

            with ExitStack() as mx:
                XN = mx.enter_context(nc.sbuf_tensor("XN", [P, NB, C], F32))
                WT = mx.enter_context(nc.sbuf_tensor("WT", [P, 2, 3 * C], F32))
                W1T = mx.enter_context(nc.sbuf_tensor("W1T", [P, 2, C], F32))
                W2T = mx.enter_context(nc.sbuf_tensor("W2T", [P, 2, C], F32))
                KV = mx.enter_context(nc.sbuf_tensor("KV", [P, 2, P + GH], F32))
                turn_weights(nc, "turn_qkv", io["mix_Wqkv"], WT, st["ident"])
                turn_weights(nc, "turn_w1", io["mix_W1"], W1T, st["ident"])
                turn_weights(nc, "turn_w2", io["mix_W2"], W2T, st["ident"])
                move_tiles(nc, "load_x", XN, io["x"])
                normalize_tiles(nc, "norm_x", XN, None, None)
                mix_keys(nc, st, XN, WT, KV)
                mix_queries(nc, st, XN, WT, KV)
                normalize_tiles(nc, "norm_mix1", XN, io["mix_ln1_g"], io["mix_ln1_b"])
                mix_mlp(nc, st, io, XN, W1T, W2T)
                normalize_tiles(nc, "norm_mix2", XN, io["mix_ln2_g"], io["mix_ln2_b"])
                move_tiles(nc, "store_mix", dr["mix"], XN)

            st["acc"] = sbi("acc", [P, NB, RW])
            st["ADM"] = sbi("ADM", [P, NB, 2 * H])
            st["own"] = sbi("own", [P, NB, H])
            node_phase(nc, 0, st, io, dr)
            for layer in range(3):
                edge_phase(nc, layer, st, dr)
                node_phase(nc, layer + 1, st, io, dr)

        xT = sb("xT", [P, 2, NPAD])
        wts = sb("wts", [P, NB, EX])
        with nc.sbuf_tensor("XF", [P, NB, C], F32) as XF:
            move_tiles(nc, "load_x2", XF, dr["x2"])
            normalize_tiles(nc, "norm_x2", XF, None, None)
            normalize_tiles(nc, "norm_ffn", XF, io["ffn_gamma"], io["ffn_beta"])
            route(nc, st, io, XF, xT, wts)
        experts(nc, st, io, xT, wts, dr, out)


_GNN = [f"L0_gnn_{n}{layer}" for layer in range(3) for n in ("W", "att_src", "att_dst", "bias", "ln_g", "ln_b")]
_MIX = [f"L0_mix_{n}" for n in ("Wqkv", "ln1_g", "ln1_b", "W1", "b1", "W2", "b2", "ln2_g", "ln2_b")]
_FFN = [f"L0_ffn_{n}" for n in ("gamma", "beta", "Wr", "br", "W1", "b1", "W2", "b2")]
_INS = ["x", "src", "dst"] + _GNN + _MIX + _FFN


def kernel(**inputs):
    import numpy as _np
    import concourse.bacc as _bacc
    from concourse.bass_utils import run_bass_kernel_spmd as _run

    nc = _bacc.Bacc("TRN2", target_bir_lowering=False, num_devices=1)
    arrays, io = {}, {}
    for name in _INS:
        a = _np.ascontiguousarray(inputs[name])
        arrays[f"in_{name}"] = a
        short = name.replace("L0_gnn_", "").replace("L0_", "")
        io[short] = nc.dram_tensor(f"in_{name}", a.shape, mybir.dt.from_np(a.dtype), kind="ExternalInput").ap()
    out = nc.dram_tensor("out", (N, C), F32, kind="ExternalOutput").ap()
    build(nc, io, out)
    r = _run(nc, [arrays], core_ids=[0])
    return r.results[0]["out"]
```

```python
from contextlib import ExitStack
from itertools import zip_longest

import concourse.bass as bass
from concourse import mybir

F32 = mybir.dt.float32
BF16 = mybir.dt.bfloat16
I32 = mybir.dt.int32
ALU = mybir.AluOpType
ACT = mybir.ActivationFunctionType
AX = mybir.AxisListType

P = 128
N = 6250
C = 256
E = 200000
NB = -(-N // P)
TAIL = N - (NB - 1) * P
NPAD = NB * P
H = 4
D = C // H
RW = C + H
GE = 2 * P
TG = -(-E // GE)
WG = 8
WS = 2 * WG
NW = 4 * (-(-(TG + NB - 1) // (4 * WG)))
NG = NW * WG
GC = -(-NG // P)
TC = -(-(TG + 1) // P)
BIG = float(2.0 ** 120)
SLOPE = 0.2
LN_EPS = 1e-5
RING = 4
ROWS_SEEN = "a node block is at most NB - 1, as the walk clamps it"


class Chain:

    def __init__(self, eng, sem, base=0):
        self.eng, self.sem, self.base, self.n = eng, sem, base, 0

    def add(self, ins):
        ins.then_inc(self.sem, 1)
        self.n += 1

    def wait(self):
        self.eng.wait_ge(self.sem, self.base + self.n)

    def link(self, ins):
        self.add(ins)
        self.wait()


def wait_apart(eng, sem, value, passed):
    eng.wait_ge(sem, value)
    eng.sem_inc(passed, 1)


class Phase:

    def __init__(self, nc, name):
        self.nc, self.name, self.ctx, self.sems = nc, name, ExitStack(), []

    def __enter__(self):
        self.ctx.__enter__()
        return self

    def __exit__(self, *a):
        done = self.ctx.__exit__(*a)
        self.nc.clear_and_free_semaphores(self.sems)
        self.nc.all_engine_barrier(sem_only=True)
        return done

    def sb(self, name, shape, dt=F32):
        return self.ctx.enter_context(self.nc.sbuf_tensor(f"{self.name}_{name}", shape, dt))

    def ps(self, name, shape, dt=F32):
        return self.ctx.enter_context(self.nc.psum_tensor(f"{self.name}_{name}", shape, dt))

    def sem(self, name):
        self.sems.append(self.nc.alloc_semaphore(f"{self.name}_{name}"))
        return self.sems[-1]

    def block(self):
        return self.ctx.enter_context(self.nc.Block())


def prepare_walk(nc, src, dst, st, dr):
    pad_rows = TG + 1
    with Phase(nc, "walk") as ph:
        pad = ph.sb("pad", [1, 2, pad_rows * GE - E], I32)
        dstI = ph.sb("dstI", [P, TC, GE], I32)
        dstF = ph.sb("dstF", [P, TC, GE])
        last_blk = ph.sb("last_blk", [P, TC])
        last_int = ph.sb("last_int", [P, TC], I32)
        threshold = ph.sb("threshold", [P, TC])
        passed = ph.sb("passed", [P, TC, GC * P], BF16)
        ones = ph.sb("ones", [P, P], BF16)
        iota_g = ph.sb("iota_g", [P, GC * P])
        iota_gp = ph.sb("iota_gp", [P, GC])
        grp = ph.sb("grp", [P, GC])
        grpI = ph.sb("grpI", [P, GC], I32)
        blk = ph.sb("blk", [P, GC])
        row_blk = ph.sb("row_blk", [P, GC * P])
        wordF = ph.sb("wordF", [P, NW, WG])
        wordS = ph.sb("wordS", [P, NW])
        pow2 = ph.sb("pow2", [P, WG])
        rise = ph.sb("rise", [P, NW, WG])
        Dg = ph.sb("Dg", [P, GC, 2, P], I32)
        Sg = ph.sb("Sg", [P, GC, 2, P], I32)
        Df = ph.sb("Df", [P, GC, 2, P])
        Sf = ph.sb("Sf", [P, GC, 2, P])
        rel = ph.sb("rel", [P, GC, 2, P])
        last = ph.sb("last", [P, GC, 2, P])
        rst = ph.sb("rst", [P, GC, 2, P], BF16)
        ps_row = ph.ps("ps_row", [P, 2, 512])
        ps_col = ph.ps("ps_col", [P, 512])
        ps_tr = ph.ps("ps_tr", [P, 4, 512])

        pads_set = ph.sem("pads_set")
        edges_in = ph.sem("edges_in")
        pads_in = ph.sem("pads_in")
        dst_in = ph.sem("dst_in")
        iotas = ph.sem("iotas")
        dve = ph.sem("dve")
        compared = ph.sem("compared")
        walked = ph.sem("walked")
        index_ready = ph.sem("index_ready")
        dst_rows = ph.sem("dst_rows")
        src_rows = ph.sem("src_rows")
        rows_ready = ph.sem("rows_ready")
        turned = ph.sem("turned")
        copied = ph.sem("copied")
        reset_ready = ph.sem("reset_ready")
        reset_out = ph.sem("reset_out")
        pool = ph.sem("pool")
        block = ph.block()
        rowT = -(-NG // 2)
        assert rowT <= 512

        flat = dr["dst_pad"].rearrange("t e -> (t e)")
        flat_s = dr["src_pad"].rearrange("t e -> (t e)")

        @block.sync
        def _(sp):
            for to, of in ((flat, dst), (flat_s, src)):
                sp.dma_start(to[0:E].rearrange("(a b) -> a b", a=16),
                             of.rearrange("(a b) -> a b", a=16)).then_inc(edges_in, 16)
            sp.wait_ge(pads_set, 2)
            for n, to in enumerate((flat, flat_s)):
                sp.dma_start(to[E:pad_rows * GE].rearrange("(a b) -> a b", a=1), pad[:, n, :]).then_inc(pads_in, 16)
            sp.wait_ge(edges_in, 32)
            sp.wait_ge(pads_in, 32)
            sp.wait_ge(pool, 1)
            full = (TC - 1) * P
            sp.dma_start(dstI[:, 0:TC - 1, :], dr["dst_pad"][0:full, :].rearrange("(c p) e -> p c e", p=P)).then_inc(dst_in, 16)
            sp.dma_start(dstI[0:pad_rows - full, TC - 1, :], dr["dst_pad"][full:pad_rows, :]).then_inc(dst_in, 16)
            sp.wait_ge(reset_ready, 1)
            for c in range(GC):
                n = min(P, NG - c * P)
                for h in range(H):
                    sp.dma_start(dr["reset"][c * P:c * P + n, h, :, :], rst[0:n, c, :, :]).then_inc(reset_out, 16)
            sp.wait_ge(reset_out, 16 * GC * H)

        @block.gpsimd
        def _(g):
            g.memset(dstI[:, TC - 1, :], 0).then_inc(pool, 1)
            g.memset(pad[:, 0, :], -1).then_inc(pads_set, 1)
            g.memset(pad[:, 1, :], 0).then_inc(pads_set, 1)
            g.iota(iota_g[:, :], [[1, GC * P]], base=0, channel_multiplier=0,
                   allow_small_or_imprecise_dtypes=True).then_inc(iotas, 1)
            g.iota(iota_gp[:, :], [[P, GC]], base=0, channel_multiplier=1,
                   allow_small_or_imprecise_dtypes=True).then_inc(iotas, 1)
            g.iota(st["iota"][:, :], [[1, P]], base=0, channel_multiplier=0,
                   allow_small_or_imprecise_dtypes=True).then_inc(iotas, 1)
            g.memset(st["ident"][:, :], 0.0).then_inc(pool, 1)
            g.wait_ge(pool, 2)
            g.affine_select(out=st["ident"][:, :], in_=st["ident"][:, :], compare_op=ALU.not_equal, fill=1.0,
                            base=0, pattern=[[-1, P]], channel_multiplier=1).then_inc(iotas, 1)
            g.iota(threshold[:, :], [[P, TC]], base=1, channel_multiplier=1,
                   allow_small_or_imprecise_dtypes=True).then_inc(pool, 1)
            g.wait_ge(pool, 3)
            g.affine_select(out=threshold[:, :], in_=threshold[:, :], compare_op=ALU.is_ge, fill=1e6,
                            base=TG - 1, pattern=[[-P, TC]], channel_multiplier=-1).then_inc(iotas, 1)
            g.wait_ge(index_ready, 1)
            for c in range(GC):
                g.indirect_dma_start(Dg[:, c, :, :].rearrange("p a b -> p (a b)"), None, dr["dst_pad"],
                                     bass.IndirectOffsetOnAxis(grpI[:, c:c + 1], 0)).then_inc(dst_rows, 16)
                g.indirect_dma_start(Sg[:, c, :, :].rearrange("p a b -> p (a b)"), None, dr["src_pad"],
                                     bass.IndirectOffsetOnAxis(grpI[:, c:c + 1], 0)).then_inc(src_rows, 16)

        @block.vector
        def _(v):
            ch = Chain(v, dve)
            v.memset(ones[:, :], 1.0).then_inc(iotas, 1)
            for n in range(1, WG):
                ch.add(v.memset(pow2[:, n:n + 1], float(64 * 2 ** (n - 1))))
            v.wait_ge(dst_in, 32)
            ch.link(v.tensor_copy(dstF[:, :, :], dstI[:, :, :]))
            ch.link(v.tensor_reduce(last_blk[:, :], dstF[:, :, :], AX.X, ALU.max))
            ch.link(v.tensor_scalar(last_blk[:, :], last_blk[:, :], 0.0, None, ALU.max))
            ch.link(v.tensor_copy(last_int[:, :], last_blk[:, :]))
            ch.link(v.tensor_scalar(last_int[:, :], last_int[:, :], 7, None, ALU.arith_shift_right))
            ch.link(v.tensor_copy(last_blk[:, :], last_int[:, :]))
            v.wait_ge(iotas, 6)
            ch.link(v.tensor_tensor(threshold[:, :], threshold[:, :], last_blk[:, :], ALU.add))
            for c in range(TC):
                v.tensor_scalar(passed[:, c, :], iota_g[:, :], threshold[:, c:c + 1], None, ALU.is_ge).then_inc(compared, 1)
            v.wait_ge(walked, 1)
            ch.link(v.tensor_copy(grp[:, :], ps_col[:, 0:GC]))
            v.tensor_copy(grpI[:, :], grp[:, :]).then_inc(index_ready, 1)
            ch.link(v.tensor_tensor(blk[:, :], iota_gp[:, :], grp[:, :], ALU.subtract))
            ch.link(v.tensor_scalar(blk[:, :], blk[:, :], float(NB - 1), float(P), ALU.min, ALU.mult))
            for c in range(2):
                ch.add(v.tensor_tensor(row_blk[:, c * rowT:(c + 1) * rowT], iota_g[:, c * rowT:(c + 1) * rowT],
                                       ps_row[:, c, 0:rowT], ALU.subtract))
            ch.wait()
            ch.link(v.tensor_scalar(row_blk[:, 0:NG], row_blk[:, 0:NG], float(NB - 1), None, ALU.min))
            rb = row_blk[:, 0:NG].rearrange("p (w g) -> p w g", g=WG)
            ch.add(v.tensor_copy(wordF[:, :, 0:1], rb[:, :, 0:1]))
            ch.link(v.tensor_tensor(wordF[:, :, 1:WG], rb[:, :, 1:WG], rb[:, :, 0:WG - 1], ALU.subtract))
            ch.link(v.tensor_scalar(rise[:, :, 1:WG], wordF[:, :, 1:WG], -BIG, None, ALU.mult))
            for h in range(H):
                up = st["rises"][:, :, 0, h * WG:(h + 1) * WG]
                down = st["rises"][:, :, 1, h * WG:(h + 1) * WG]
                ch.add(v.tensor_copy(up[:, :, 1:WG], rise[:, :, 1:WG]))
                for n in range(1, WG):
                    ch.add(v.tensor_copy(down[:, :, n:n + 1], rise[:, :, WG - n:WG - n + 1]))
                for to in (up, down):
                    ch.add(v.memset(to[:, :, 0:1], -BIG))
            ch.link(v.tensor_tensor(wordF[:, :, 1:WG], wordF[:, :, 1:WG],
                                    pow2[:, 1:WG].unsqueeze(1).broadcast_to([P, NW, WG - 1]), ALU.mult))
            ch.link(v.tensor_reduce(wordS[:, :], wordF[:, :, :], AX.X, ALU.add))
            ch.link(v.tensor_copy(st["words"][:, :], wordS[:, :]))
            v.wait_ge(dst_rows, 16 * GC)
            v.wait_ge(src_rows, 16 * GC)
            ch.add(v.tensor_copy(Df[:, :, :, :], Dg[:, :, :, :]))
            v.tensor_copy(Sf[:, :, :, :], Sg[:, :, :, :]).then_inc(rows_ready, 1)
            ch.add(v.memset(rst[:, :, :, 0:1], 0.0))
            ch.add(v.memset(last[:, :, :, P - 1:P], 1.0))
            ch.wait()
            for c in range(GC):
                v.tensor_scalar(rel[:, c, :, :], Df[:, c, :, :], blk[:, c:c + 1], None, ALU.subtract).then_inc(rows_ready, 1)
            v.tensor_tensor(last[:, :, :, 0:P - 1], Df[:, :, :, 0:P - 1], Df[:, :, :, 1:P], ALU.not_equal).then_inc(rows_ready, 1)
            v.wait_ge(rows_ready, 2 + GC)
            v.tensor_scalar(rst[:, :, :, 1:P], last[:, :, :, 0:P - 1], -BIG, None, ALU.mult).then_inc(reset_ready, 1)
            for c in range(GC):
                n = min(P, NG - c * P)
                v.wait_ge(turned, c + 1)
                for m, t in enumerate(("srcT", "relT", "lastT")):
                    for j in range(2):
                        o = (2 * m + j) * P
                        v.tensor_copy(st[t][:, c * P:c * P + n, j],
                                      ps_tr[:, 2 * (c % 2) + o // 512, o % 512:o % 512 + n]).then_inc(copied, 1)
            v.wait_ge(copied, 6 * GC)

        @block.tensor
        def _(pe):
            pe.wait_ge(iotas, 6)
            for c in range(TC):
                pe.wait_ge(compared, c + 1)
                for r in range(2):
                    pe.matmul(ps_row[:, r, 0:rowT], ones[:, :], passed[:, c, r * rowT:(r + 1) * rowT],
                              start=(c == 0), stop=(c == TC - 1))
            for m in range(GC):
                for c in range(TC):
                    mm = pe.matmul(ps_col[:, m:m + 1], passed[:, c, m * P:(m + 1) * P], ones[:, 0:1],
                                   start=(c == 0), stop=(c == TC - 1))
            mm.then_inc(walked, 1)
            pe.wait_ge(rows_ready, 2 + GC)
            for c in range(GC):
                if c >= 2:
                    pe.wait_ge(copied, 6 * (c - 1))
                for m, t in enumerate((Sf, rel, last)):
                    for j in range(2):
                        o = (2 * m + j) * P
                        mm = pe.transpose(ps_tr[:, 2 * (c % 2) + o // 512, o % 512:o % 512 + P],
                                          t[:, c, j, :], st["ident"][:, :])
                mm.then_inc(turned, 1)



def broadcast_row(vec):
    return vec.rearrange("(a n) -> a n", a=1).broadcast_to([P, vec.shape[0]])


def over_tiles(eng, step):
    step(0, 0, False)
    step(0, 1, False)
    with eng.Fori(1, (NB - 1) // 2) as i:
        step(i, 0, False)
        step(i, 1, False)
    step((NB - 1) // 2, 0, True)


TILE_RING = 4


def over_ring(eng, step, peeled=1):
    assert NB % TILE_RING == 1
    for i in range(peeled):
        for slot in range(TILE_RING):
            step(i, slot, False)
    with eng.Fori(peeled, NB // TILE_RING) as i:
        for slot in range(TILE_RING):
            step(i, slot, False)
    step(NB // TILE_RING, 0, True)


def ring_rows(dram, i, slot, last):
    if last:
        return dram[(NB - 1) * P:N, :]
    return padded_ring_rows(dram, i, slot)


def padded_ring_rows(dram, i, slot):
    return dram[bass.ds((TILE_RING * i + slot) * P, P), :]


def is_zero(i):
    return isinstance(i, int) and i == 0


def node_phase(nc, layer, st, io, dr):
    first, final = layer == 0, layer == 3
    acc, ADM, own = st["acc"], st["ADM"], st["own"]
    with Phase(nc, f"node{layer}") as ph:
        X = ph.sb("X", [P, TILE_RING, C])
        rows = ph.sb("rows", [P, TILE_RING, RW])
        prev = ph.sb("prev", [P, TILE_RING, C])
        mix = ph.sb("mix", [P, TILE_RING, C])
        O = ph.sb("O", [P, TILE_RING, C])
        Hn = ph.sb("Hn", [P, TILE_RING, C])
        hT = ph.sb("hT", [P, TILE_RING, 2, P])
        ext = ph.sb("ext", [P, TILE_RING, RW])
        stats = ph.sb("stats", [P, TILE_RING, 6])
        mv = ph.sb("mv", [P, TILE_RING, 2])
        sd = ph.sb("sd", [P, TILE_RING, 1])
        rstd = ph.sb("rstd", [P, TILE_RING, 1])
        eps = ph.sb("eps", [P, 1])
        vecs = ph.sb("vecs", [P, 3, C])
        W = ph.sb("W", [P, 2, C])
        WT = ph.sb("WT", [P, 2, C])
        att = ph.sb("att", [P, 2, 2 * H])
        Wx = ph.sb("Wx", [P, 2, RW + H])
        tu = ph.sb("tu", [P, 2, NB * H])
        lr = ph.sb("lr", [P, 2, NB * H])
        es = ph.sb("es", [P, NB, H])
        zr = ph.sb("zr", [P, NB, H])
        psA = [ph.ps(f"psA{k}", [P, 512]) for k in range(2)]
        psB = [ph.ps(f"psB{k}", [P, 512]) for k in range(2)]
        psW = ph.ps("psW", [P, 512])
        psS = ph.ps("psS", [P, 512])

        consts = ph.sem("consts")
        att_clear = ph.sem("att_clear")
        vecs_in = ph.sem("vecs_in")
        weights_in = ph.sem("weights_in")
        w_turned = ph.sem("w_turned")
        wT_ready = ph.sem("wT_ready")
        w_scored = ph.sem("w_scored")
        wx_ready = ph.sem("wx_ready")
        pre = ph.sem("pre")
        es_ready = ph.sem("es_ready")
        loaded = [ph.sem(f"loaded{k}") for k in range(TILE_RING)]
        chain1 = ph.sem("chain1")
        chain2 = ph.sem("chain2")
        passed = ph.sem("passed")
        stats_ready = ph.sem("stats_ready")
        sd_ready = ph.sem("sd_ready")
        h_ready = ph.sem("h_ready")
        turned = ph.sem("turned")
        hT_ready = ph.sem("hT_ready")
        projected = ph.sem("projected")
        ext_ready = ph.sem("ext_ready")
        h_out = [ph.sem(f"h_out{k}") for k in range(TILE_RING)]
        ext_out = [ph.sem(f"ext_out{k}") for k in range(TILE_RING)]
        block = ph.block()

        loads = (first or final) + (not first) + (layer >= 2) + final
        if not final:
            W_dram, a_src, a_dst = io[f"W{layer}"], io[f"att_src{layer}"], io[f"att_dst{layer}"]
            heads = a_src.shape[0]
        n_att = 0 if final else (2 * H if heads == H else 2 * 2 * H)

        def head_view(ap):
            return ap.rearrange("p (h f) -> p h f", h=H)[:, :, 0:D]

        def by_head(ap):
            return ap.rearrange("p (h f) -> p h f", h=H)

        @block.sync
        def _(sp):
            if not first:
                for n, name in enumerate(("bias", "ln_g", "ln_b")):
                    sp.dma_start(vecs[:, n, :], broadcast_row(io[f"{name}{layer - 1}"])).then_inc(vecs_in, 16)
            if not final:
                sp.dma_start(W[:, :, :], W_dram.rearrange("(k p) o -> p k o", p=P)).then_inc(weights_in, 16)
                sp.wait_ge(att_clear, 1)
                for n, a in enumerate((a_src, a_dst)):
                    if heads == H:
                        for h in range(H):
                            o = (h * D) % P
                            sp.dma_start(att[o:o + D, h * D // P, n * H + h:n * H + h + 1],
                                         a[h:h + 1, :].rearrange("a d -> d a")).then_inc(weights_in, 16)
                    else:
                        for k in range(2):
                            for h in range(H):
                                sp.dma_start(att[:, k, n * H + h:n * H + h + 1],
                                             a[0:1, k * P:(k + 1) * P].rearrange("a d -> d a")).then_inc(weights_in, 16)

            def load(i, slot, last):
                n = slice(0, TAIL) if last else slice(0, P)
                if first or final:
                    sp.dma_start(X[n, slot, :], ring_rows(io["x"], i, slot, last)).then_inc(loaded[slot], 16)
                if not first:
                    sp.dma_start(rows[:, slot, :], padded_ring_rows(dr["rows"], i, slot)).then_inc(loaded[slot], 16)
                if layer >= 2:
                    sp.dma_start(prev[:, slot, :], padded_ring_rows(dr["h"], i, slot)).then_inc(loaded[slot], 16)
                if final:
                    sp.dma_start(mix[:, slot, :], padded_ring_rows(dr["mix"], i, slot)).then_inc(loaded[slot], 16)

            for slot in range(TILE_RING):
                load(0, slot, False)
            with sp.Fori(1, NB // TILE_RING) as i:
                for slot in range(TILE_RING):
                    sp.wait_ge(h_ready, TILE_RING * (i - 1) + slot + 2)
                    load(i, slot, False)
            sp.wait_ge(h_ready, NB - TILE_RING + 1)
            load(NB // TILE_RING, 0, True)

        @block.gpsimd
        def _(g):
            g.memset(att[:, :, :], 0.0).then_inc(att_clear, 1)
            g.memset(eps[:, :], LN_EPS).then_inc(consts, 1)
            if first:
                g.memset(acc[:, :, :], 0.0).then_inc(consts, 1)

            def step(i, slot, last):
                b = TILE_RING * i + slot
                g.wait_ge(h_ready, b + 2)
                to = "x2" if final else "h"
                g.dma_start(padded_ring_rows(dr[to], i, slot), Hn[:, slot, :]).then_inc(h_out[slot], 16)
                if not final:
                    g.wait_ge(ext_ready, b + 3)
                    g.dma_start(padded_ring_rows(dr["rows"], i, slot), ext[:, slot, :]).then_inc(ext_out[slot], 16)

            over_ring(g, step)
            if not first and not final:
                g.memset(acc[:, :, :], 0.0).then_inc(consts, 1)
            for slot in range(TILE_RING):
                n = NB // TILE_RING + (slot == 0)
                g.wait_ge(h_out[slot], 16 * n)
                if not final:
                    g.wait_ge(ext_out[slot], 16 * n)

        @block.vector
        def _(v):
            v.sem_inc(h_ready, 1)
            c0 = Chain(v, pre)
            if not final:
                v.wait_ge(w_turned, 1)
                v.tensor_copy(WT[:, :, :].rearrange("p a b -> p (a b)"), psW[:, :]).then_inc(wT_ready, 1)
                v.wait_ge(w_scored, 1)
                for k in range(2):
                    for n in range(2):
                        sc = psS[:, k * 2 * H + n * H:k * 2 * H + (n + 1) * H]
                        if n:
                            v.tensor_copy(Wx[:, k, RW:RW + H], sc).then_inc(wx_ready, 1)
                        else:
                            v.tensor_copy(by_head(Wx[:, k, 0:RW])[:, :, D], sc).then_inc(wx_ready, 1)
                    v.tensor_copy(head_view(Wx[:, k, 0:RW]), by_head(W[:, k, :])).then_inc(wx_ready, 1)
            if not first:
                as_, ad_, ms_ = own[:, :, :], ADM[:, :, 0:H], ADM[:, :, H:2 * H]
                tv = [tu[:, k, :].rearrange("p (b h) -> p b h", h=H) for k in range(2)]
                c0.add(v.tensor_tensor(tv[0], as_, ad_, ALU.add))
                c0.link(v.tensor_tensor(tv[1], ms_, ad_, ALU.add))
                c0.link(v.scalar_tensor_tensor(out=lr[:, :, :], in0=tu[:, :, :], scalar=SLOPE, in1=tu[:, :, :],
                                               op0=ALU.mult, op1=ALU.max))
                c0.link(v.tensor_tensor(tu[:, 0, :], lr[:, 0, :], lr[:, 1, :], ALU.subtract))
                v.wait_ge(es_ready, 1)
                sums = acc[:, :, :].rearrange("p b (h f) -> p b h f", h=H)[:, :, :, D]
                c0.link(v.tensor_tensor(zr[:, :, :], sums, es[:, :, :], ALU.add))
                c0.link(v.tensor_scalar(zr[:, :, :], zr[:, :, :], 1e-16, None, ALU.add))
                c0.link(v.reciprocal(zr[:, :, :], zr[:, :, :]))
                v.wait_ge(vecs_in, 48)

            N1 = 1 if first else 5
            N2 = 1 if first else 3 + (layer >= 2) + final

            def gather_in(i, slot, last):
                b = TILE_RING * i + slot
                ch = Chain(v, chain1, b * N1)
                v.wait_ge(loaded[slot], 16 * loads * (i + 1))
                if first:
                    o = X[:, slot, :]
                else:
                    o = O[:, slot, :]
                    oh = by_head(o)
                    a = acc[:, bass.ds(b, 1), :].rearrange("p a (h f) -> p (a h) f", h=H)[:, :, 0:D]
                    e = es[:, bass.ds(b, 1), :].rearrange("p a h -> p (a h)").unsqueeze(2).broadcast_to([P, H, D])
                    z = zr[:, bass.ds(b, 1), :].rearrange("p a h -> p (a h)").unsqueeze(2).broadcast_to([P, H, D])
                    ch.add(v.tensor_tensor(oh, head_view(rows[:, slot, :]), e, ALU.mult))
                    yield
                    ch.wait()
                    ch.add(v.tensor_tensor(oh, oh, a, ALU.add))
                    yield
                    ch.wait()
                    ch.add(v.tensor_tensor(oh, oh, z, ALU.mult))
                    yield
                    ch.wait()
                    ch.add(v.tensor_tensor(o, o, vecs[:, 0, :], ALU.add))
                    yield
                    ch.wait()
                ch.add(v.bn_stats(stats[:, slot, :], o))
                yield
                wait_apart(v, chain1, ch.base + ch.n, passed)
                v.bn_aggr(mv[:, slot, :], stats[:, slot, :]).then_inc(stats_ready, 1)
                assert ch.n == N1

            def finish(i, slot, last):
                b = TILE_RING * i + slot
                ch = Chain(v, chain2, b * N2)
                o = X[:, slot, :] if first else O[:, slot, :]
                hn = Hn[:, slot, :]
                v.wait_ge(sd_ready, b + 1)
                ch.add(v.reciprocal(rstd[:, slot, :], sd[:, slot, :]))
                yield
                ch.wait()
                if not is_zero(i):
                    v.wait_ge(h_out[slot], 16 * i)
                if not final:
                    v.wait_ge(turned, b + 1)
                if first:
                    v.tensor_scalar(hn, o, mv[:, slot, 0:1], rstd[:, slot, :], ALU.subtract, ALU.mult).then_inc(h_ready, 1)
                else:
                    ch.add(v.scalar_tensor_tensor(out=o, in0=o, scalar=mv[:, slot, 0:1], in1=vecs[:, 1, :],
                                                  op0=ALU.subtract, op1=ALU.mult))
                    yield
                    ch.wait()
                    ch.add(v.scalar_tensor_tensor(out=o, in0=o, scalar=rstd[:, slot, :], in1=vecs[:, 2, :],
                                                  op0=ALU.mult, op1=ALU.add))
                    yield
                    ch.wait()
                    if layer >= 2:
                        ch.add(v.tensor_tensor(o, o, prev[:, slot, :], ALU.add))
                        yield
                        ch.wait()
                    if final:
                        ch.add(v.scalar_tensor_tensor(out=o, in0=o, scalar=0.0, in1=X[:, slot, :],
                                                      op0=ALU.max, op1=ALU.add))
                        yield
                        ch.wait()
                        v.tensor_tensor(hn, o, mix[:, slot, :], ALU.add).then_inc(h_ready, 1)
                    else:
                        v.tensor_scalar(hn, o, 0.0, None, ALU.max).then_inc(h_ready, 1)
                assert ch.n == N2

            for _ in gather_in(0, 0, False):
                pass

            def step(i, slot, last):
                following = iter(()) if last else gather_in(i + (slot + 1) // TILE_RING, (slot + 1) % TILE_RING, False)
                for _ in zip_longest(following, finish(i, slot, last)):
                    pass

            over_ring(v, step)

        @block.scalar
        def _(a):
            a.wait_ge(consts, 1 + first)
            if not final:
                for s in (hT_ready, ext_ready):
                    a.sem_inc(s, 2)
            if not first:
                a.wait_ge(pre, 4)
                a.activation(es[:, :, :], tu[:, 0, :].rearrange("p (b h) -> p b h", h=H), ACT.Exp).then_inc(es_ready, 1)

            def std(slot, b):
                a.wait_ge(stats_ready, b + 1)
                a.activation(sd[:, slot, :], mv[:, slot, 1:2], ACT.Sqrt, bias=eps[:, :]).then_inc(sd_ready, 1)

            std(0, 0)

            def step(i, slot, last):
                b = TILE_RING * i + slot
                if not last:
                    std((slot + 1) % TILE_RING, b + 1)
                if final:
                    return
                a.wait_ge(turned, b + 3)
                a.wait_ge(projected, b + 1)
                a.activation(hT[:, slot, :, :].rearrange("p a b -> p (a b)"), psA[slot % 2][:, 0:C], ACT.Copy).then_inc(hT_ready, 1)
                if slot or not is_zero(i):
                    extend(i - (slot == 0), (slot - 1) % TILE_RING)

            def extend(i, slot):
                b = TILE_RING * i + slot
                a.wait_ge(projected, b + 3)
                if not is_zero(i):
                    a.wait_ge(ext_out[slot], 16 * i)
                scores = by_head(psB[slot % 2][:, 0:RW])[:, :, D]
                a.activation(ADM[:, bass.ds(b, 1), 0:H].rearrange("p a h -> p (a h)"), psB[slot % 2][:, RW:RW + H], ACT.Copy)
                a.activation(ADM[:, bass.ds(b, 1), H:2 * H].rearrange("p a h -> p (a h)"), scores, ACT.Copy)
                a.activation(own[:, bass.ds(b, 1), :].rearrange("p a h -> p (a h)"), scores, ACT.Copy)
                a.activation(ext[:, slot, :], psB[slot % 2][:, 0:RW], ACT.Copy).then_inc(ext_ready, 1)

            over_ring(a, step, peeled=2)
            if not final:
                extend(NB // TILE_RING, 0)

        @block.tensor
        def _(pe):
            if final:
                return
            pe.sem_inc(turned, 2)
            pe.sem_inc(projected, 2)
            pe.wait_ge(weights_in, 16 * (1 + n_att))
            for k in range(2):
                for o in range(2):
                    mm = pe.transpose(psW[:, (o * 2 + k) * P:(o * 2 + k + 1) * P], W[:, k, o * P:(o + 1) * P], st["ident"][:, :])
            mm.then_inc(w_turned, 1)
            pe.wait_ge(wT_ready, 1)
            for k in range(2):
                for o in range(2):
                    mm = pe.matmul(psS[:, k * 2 * H:(k + 1) * 2 * H], WT[:, o, k * P:(k + 1) * P], att[:, o, :],
                                   start=(o == 0), stop=(o == 1))
            mm.then_inc(w_scored, 1)
            pe.wait_ge(wx_ready, 6)

            def step(i, slot, last):
                b = TILE_RING * i + slot
                pe.wait_ge(h_ready, b + 2)
                pe.wait_ge(hT_ready, b + 1)
                for k in range(2):
                    mm = pe.transpose(psA[slot % 2][:, k * P:(k + 1) * P], Hn[:, slot, k * P:(k + 1) * P], st["ident"][:, :])
                mm.then_inc(turned, 1)
                if slot or not is_zero(i):
                    project(b - 1, slot - 1)

            def project(b, slot):
                pe.wait_ge(hT_ready, b + 3)
                pe.wait_ge(ext_ready, b + 1)
                for k in range(2):
                    mm = pe.matmul(psB[slot % 2][:, 0:RW + H], hT[:, slot % TILE_RING, k, :], Wx[:, k, :], start=(k == 0), stop=(k == 1))
                mm.then_inc(projected, 1)

            over_ring(pe, step, peeled=2)
            project(NB - 1, 0)


def edge_phase(nc, layer, st, dr):
    acc, ADM, ident, iota = st["acc"], st["ADM"], st["ident"], st["iota"]
    srcT, relT, lastT, words, rises = (st[n] for n in ("srcT", "relT", "lastT", "words", "rises"))
    S3 = WS * H
    GH4 = WG * H
    BANKS = 4
    with Phase(nc, f"edges{layer}") as ph:
        G = [ph.sb(f"G{r}", [P, WS, RW]) for r in range(RING)]
        index = [ph.sb(f"index{r}", [P, WS], I32) for r in range(RING)]
        reset = ph.sb("reset", [S3, RING, P], BF16)
        identb = ph.sb("identb", [P, P], BF16)
        OHb = [ph.sb(f"OHb{k}", [P, WS, P], BF16) for k in range(2)]
        OH = [ph.sb(f"OH{k}", [P, WS, P]) for k in range(2)]
        OHT = ph.sb("OHT", [P, WS, P], BF16)
        score = [ph.sb(f"score{k}", [P, S3]) for k in range(2)]
        run = ph.sb("run", [S3, P])
        masked = ph.sb("masked", [P, S3])
        rest = ph.sb("rest", [P, S3])
        lastv = ph.sb("lastv", [P, 3, WS, 8], BF16)
        absent = ph.sb("absent", [P, WS])
        seg = ph.sb("seg", [P, WS, H])
        here = ph.sb("here", [P, H, WG])
        before = ph.sb("before", [P, H, WG])
        after = ph.sb("after", [P, H, WG])
        node = [ph.sb(f"node{k}", [P, WG, 2 * H]) for k in range(2)]
        top = ph.sb("top", [P, WG, H])
        logit = ph.sb("logit", [P, WG + 1, H])
        fin = ph.sb("fin", [P, WG + 1, 2 * H])
        rest2 = ph.sb("rest2", [P, WG * 2 * H])
        parts = ph.sb("parts", [P, 3, WG, 2 * H], BF16)
        tu = ph.sb("tu", [P, S3])
        lr = ph.sb("lr", [P, S3])
        diff = ph.sb("diff", [P, S3])
        fd = ph.sb("fd", [P, H])
        fade = ph.sb("fade", [P, H])
        ps_s = ph.ps("ps_s", [P, 512])
        ps_t = [ph.ps(f"ps_t{k}", [P, 1024], BF16) for k in range(2)]
        ps_small = ph.ps("ps_small", [P, 2, WS, 8])
        ps_seg, ps_ad = ps_small[:, 0, :, :], ps_small[:, 1, :, :]
        ps_o = [ph.ps(f"ps_o{k}", [P, 512]) for k in range(BANKS)]

        consts = ph.sem("consts")
        index_ready = ph.sem("index_ready")
        gathered = [ph.sem(f"gathered{r}") for r in range(RING)]
        reset_in = [ph.sem(f"reset_in{r}") for r in range(RING)]
        score_ready = ph.sem("score_ready")
        score_turned = ph.sem("score_turned")
        ran = ph.sem("ran")
        run_turned = ph.sem("run_turned")
        lastv_ready = ph.sem("lastv_ready")
        oh_ready = ph.sem("oh_ready")
        oh_turned = ph.sem("oh_turned")
        oht_ready = ph.sem("oht_ready")
        ohf_ready = ph.sem("ohf_ready")
        node_ready = ph.sem("node_ready")
        seg_ready = ph.sem("seg_ready")
        top_ready = ph.sem("top_ready")
        top_kept = ph.sem("top_kept")
        parts_ready = ph.sem("parts_ready")
        ad_ready = ph.sem("ad_ready")
        diff_ready = ph.sem("diff_ready")
        weights_ready = ph.sem("weights_ready")
        fd_ready = ph.sem("fd_ready")
        fade_ready = ph.sem("fade_ready")
        weighed = ph.sem("weighed")
        summed = ph.sem("summed")
        added = ph.sem("added")
        faded = ph.sem("faded")
        chain = ph.sem("chain")
        passed = ph.sem("passed")
        passed_pool = ph.sem("passed_pool")
        block = ph.block()

        def by_head(ap):
            return ap.rearrange("p s (h f) -> p s h f", h=H)

        def ghj(ap):
            return ap.rearrange("p (g j) h -> p g h j", j=2)

        def as_ghj(ap):
            return ap.rearrange("p (g h j) -> p g h j", h=H, j=2)

        def row(ap, b):
            return ap[:, bass.ds(b, 1), :].rearrange("p a h -> p (a h)")

        def over_windows(eng, step):
            with eng.Fori(0, NW // RING - 1) as i:
                for r in range(RING):
                    step(i, r, False)
            for r in range(RING):
                step(NW // RING - 1, r, r == RING - 1)

        def exists(i, r, ahead):
            return not isinstance(i, int) or r + ahead < RING

        def blocks_of(eng, w):
            word = eng.value_load(words[0:1, bass.ds(w, 1)], min_val=0, max_val=64 * 2 ** (WG - 1) - 1)
            b = eng.snap(word & 63)
            for g in range(WG):
                b = nc.s_assert_within(b, 0, NB - 1, skip_runtime_bounds_check_because=ROWS_SEEN)
                yield b
                if g < WG - 1:
                    b = eng.snap(b + ((word >> (6 + g)) & 1))

        @block.sync
        def _(sp):
            def step(i, r, last):
                w = 4 * i + r
                sp.wait_ge(ran, w + 1)
                sp.dma_start(reset[:, r, :], dr["reset"].rearrange("g h j e -> (g h j) e")[bass.ds(w * S3, S3), :]
                             ).then_inc(reset_in[r], 16)

            over_windows(sp, step)

        @block.gpsimd
        def _(g):
            def step(i, r, last):
                w = 4 * i + r
                g.wait_ge(index_ready, w + 1)
                wait_apart(g, summed, WG * (w + 1), passed_pool)
                for s in range(WS):
                    g.indirect_dma_start(G[r][:, s, :], None, dr["rows"],
                                         bass.IndirectOffsetOnAxis(index[r][:, s:s + 1], 0)).then_inc(gathered[r], 16)

            over_windows(g, step)

        @block.scalar
        def _(a):
            a.sem_inc(oht_ready, 2)

            def make_index(w, r, i):
                if i is not None:
                    a.wait_ge(gathered[r], 16 * WS * i)
                a.activation(index[r][:, :], srcT[:, bass.ds(w * WG, WG), :].rearrange("p g j -> p (g j)"), ACT.Copy
                             ).then_inc(index_ready, 1)

            def copy_onehots(w, r):
                for c in range(2):
                    a.wait_ge(oh_turned, 2 * w + c + 1)
                    if c == 0:
                        a.wait_ge(ad_ready, w + 1)
                    a.activation(OHT[:, 8 * c:8 * c + 8, :].rearrange("p s e -> p (s e)"), ps_t[c][:, :], ACT.Copy
                                 ).then_inc(oht_ready, 1)
                a.wait_ge(summed, WG * w + WG * (RING - 1))
                for c in range(2):
                    a.activation(OH[r % 2][:, 8 * c:8 * c + 8, :], OHb[r % 2][:, 8 * c:8 * c + 8, :], ACT.Copy
                                 ).then_inc(ohf_ready, 1)

            def copy_scores(w, i, r):
                a.wait_ge(gathered[r], 16 * WS * (i + 1))
                a.wait_ge(diff_ready, w + 1)
                a.activation(as_ghj(score[r % 2][:, :]), ghj(by_head(G[r][:, :, :])[:, :, :, D]), ACT.Copy
                             ).then_inc(score_ready, 1)

            def load_node(w, r):
                for g, b in enumerate(blocks_of(a, w)):
                    if g == 0:
                        a.wait_ge(top_kept, WG * w + 1)
                    ins = a.activation(node[r % 2][:, g, :], row(ADM, b), ACT.Copy)
                ins.then_inc(node_ready, 1)

            def keep_top(w):
                for g, b in enumerate(blocks_of(a, w)):
                    if g == 0:
                        a.wait_ge(top_ready, w + 1)
                    else:
                        a.wait_ge(top_kept, WG * w + g + 1)
                    a.activation(row(ADM[:, :, H:2 * H], b), top[:, g, :], ACT.Copy).then_inc(top_kept, 1)

            def exponentials(w, r):
                a.wait_ge(diff_ready, w + 3)
                a.activation(ghj(by_head(G[r][:, :, :])[:, :, :, D]), as_ghj(diff[:, :]), ACT.Exp).then_inc(weights_ready, 1)
                a.wait_ge(fd_ready, w + 1)
                a.wait_ge(faded, w)
                a.activation(fade[:, :], fd[:, :], ACT.Exp).then_inc(fade_ready, 1)

            for r in range(RING):
                make_index(r, r, None)
            a.sem_inc(top_kept, 1)
            load_node(0, 0)
            copy_onehots(0, 0)
            copy_scores(0, 0, 0)
            exponentials(0, 0)
            copy_scores(1, 0, 1)
            keep_top(0)
            load_node(1, 1)

            def step(i, r, last):
                w = 4 * i + r
                n = (r + 1) % RING
                if not isinstance(i, int):
                    make_index(w + RING, r, i + 1)
                if last:
                    return
                copy_onehots(w + 1, n)
                if exists(i, r, 2):
                    copy_scores(w + 2, i + (r + 2) // RING, (r + 2) % RING)
                exponentials(w + 1, n)
                keep_top(w + 1)
                if exists(i, r, 2):
                    load_node(w + 2, r)

            over_windows(a, step)

        @block.tensor
        def _(pe):
            pe.sem_inc(summed, WG * RING)
            pe.sem_inc(ad_ready, 1)
            pe.wait_ge(consts, 3)

            def turn_onehots(w, r, c):
                pe.wait_ge(oh_ready, 4 * w + 2 * c + 2)
                pe.wait_ge(oht_ready, 2 * w + c + 1)
                for s in range(8):
                    mm = pe.transpose(ps_t[c][:, s * P:(s + 1) * P], OHb[r % 2][:, 8 * c + s, :], identb[:, :])
                mm.then_inc(oh_turned, 1)

            def turn_scores(w, r):
                pe.wait_ge(score_ready, w + 1)
                wait_apart(pe, ran, w + RING, passed)
                pe.transpose(ps_s[0:S3, 0:P], score[r % 2][:, :], ident[:, :]).then_inc(score_turned, 1)

            def turn_run(w):
                pe.wait_ge(ran, w + 1 + RING)
                wait_apart(pe, lastv_ready, w, passed)
                pe.transpose(ps_s[:, 256:256 + S3], run[:, :], ident[0:S3, 0:S3]).then_inc(run_turned, 1)

            def segments(w, r):
                pe.wait_ge(lastv_ready, w + 1)
                for s in range(WS):
                    for k in range(3):
                        mm = pe.matmul(ps_seg[:, s, 0:H + 1], OHb[r % 2][:, s, :], lastv[:, k, s, 0:H + 1],
                                       start=(k == 0), stop=(k == 2))
                mm.then_inc(seg_ready, 1)

            def spread(w, r):
                pe.wait_ge(oht_ready, 2 * w + 4)
                pe.wait_ge(parts_ready, w + 1)
                for s in range(WS):
                    for k in range(3):
                        mm = pe.matmul(ps_ad[:, s, :], OHT[:, s, :], parts[:, k, s // 2, :],
                                       start=(k == 0), stop=(k == 2))
                mm.then_inc(ad_ready, 1)

            def sums(w, r, groups):
                for g in groups:
                    if g % 4 == 0:
                        pe.wait_ge(ohf_ready, 2 * w + g // 4 + 1)
                    if g % 2 == 0:
                        pe.wait_ge(weighed, 4 * w + g // 2 + 1)
                    pe.wait_ge(added, WG * w + g + 1)
                    for j in range(2):
                        mm = pe.matmul(ps_o[g % BANKS][:, 0:RW], OH[r % 2][:, 2 * g + j, :], G[r][:, 2 * g + j, :],
                                       start=(j == 0), stop=(j == 1))
                    mm.then_inc(summed, 1)

            turn_onehots(0, 0, 0)
            turn_onehots(0, 0, 1)
            turn_scores(0, 0)
            turn_run(0)
            segments(0, 0)
            spread(0, 0)
            turn_onehots(1, 1, 0)
            turn_onehots(1, 1, 1)
            turn_scores(1, 1)

            def step(i, r, last):
                w = 4 * i + r
                n = (r + 1) % RING
                if not last:
                    turn_run(w + 1)
                sums(w, r, range(0, 1))
                if not last:
                    segments(w + 1, n)
                sums(w, r, range(1, 4))
                if exists(i, r, 2):
                    turn_scores(w + 2, r)
                if exists(i, r, 2):
                    turn_onehots(w + 2, r, 0)
                if not last:
                    spread(w + 1, n)
                sums(w, r, range(4, 8))
                if exists(i, r, 2):
                    turn_onehots(w + 2, r, 1)

            over_windows(pe, step)

        @block.vector
        def _(v):
            v.sem_inc(ran, RING)
            v.sem_inc(diff_ready, 2)
            v.sem_inc(added, BANKS)
            v.tensor_copy(identb[:, :], ident[:, :]).then_inc(consts, 1)
            v.memset(lastv[:, :, :, :], 0.0).then_inc(consts, 1)
            v.memset(fin[:, :, :], 0.0).then_inc(consts, 1)
            v.wait_ge(consts, 3)

            def onehots(w, r, c, again=True):
                if again and c == 0:
                    v.wait_ge(ohf_ready, 2 * (w - 2) + 2)
                rel = relT[:, bass.ds(w * WG + 2 * c, 2), :].rearrange("p g j -> p (g j)")
                v.tensor_tensor(OHb[r % 2][:, 4 * c:4 * c + 4, :], iota[:, :].unsqueeze(1).broadcast_to([P, 4, P]),
                                rel.unsqueeze(2).broadcast_to([P, 4, P]), ALU.is_equal).then_inc(oh_ready, 1)

            STEPS = 21

            def step_of(ch, ins):
                ch.add(ins)
                yield
                ch.wait()

            def split(ch, x, to, left, sem):
                yield from step_of(ch, v.tensor_copy(to[0], x))
                yield from step_of(ch, v.tensor_tensor(left, x, to[0], ALU.subtract))
                yield from step_of(ch, v.tensor_copy(to[1], left))
                v.tensor_tensor(to[2], left, to[1], ALU.subtract).then_inc(sem, 1)

            def scan(w, i, r):
                v.wait_ge(score_turned, w + 1)
                v.wait_ge(reset_in[r], 16 * (i + 1))
                v.wait_ge(run_turned, w)
                v.tensor_tensor_scan(run[:, :], reset[:, r, :], ps_s[0:S3, 0:P], -BIG, ALU.add, ALU.max).then_inc(ran, 1)
                return Chain(v, chain, STEPS * w)

            def last_values(w, ch):
                v.wait_ge(run_turned, w + 1)
                v.wait_ge(seg_ready, w)
                ls = lastT[:, bass.ds(w * WG, WG), :]
                ch.add(v.tensor_copy(lastv[:, 0, :, H], ls.rearrange("p g j -> p (g j)")))
                yield from step_of(ch, v.tensor_tensor(as_ghj(masked[:, :]), as_ghj(ps_s[:, 256:256 + S3]),
                                        ls.unsqueeze(2).broadcast_to([P, WG, H, 2]), ALU.mult))
                yield from split(ch, as_ghj(masked[:, :]), [ghj(lastv[:, k, :, 0:H]) for k in range(3)],
                                 as_ghj(rest[:, :]), lastv_ready)
                yield

            def node_terms(w, r, ch):
                v.wait_ge(node_ready, w + 1)
                nd = node[r % 2]
                ch.add(v.tensor_tensor(logit[:, WG, :], nd[:, 0, 0:H], nd[:, 0, H:2 * H], ALU.add))
                ch.add(v.tensor_copy(fin[:, 0:WG, 0:H], nd[:, :, 0:H]))

            def maxima(w, r, ch):
                v.wait_ge(seg_ready, w + 1)
                yield from step_of(ch, v.tensor_scalar(absent[:, :], ps_seg[:, :, H], 1.0, BIG, ALU.subtract, ALU.mult))
                yield from step_of(ch, v.tensor_tensor(seg[:, :, :], ps_seg[:, :, 0:H], absent[:, :].unsqueeze(2).broadcast_to([P, WS, H]), ALU.add))
                pair = seg[:, :, :].rearrange("p (g j) h -> p h g j", j=2)
                yield from step_of(ch, v.tensor_tensor(here[:, :, :], pair[:, :, :, 0], pair[:, :, :, 1], ALU.max))
                yield from step_of(ch, v.tensor_tensor(here[:, :, :], here[:, :, :], node[r % 2][:, :, H:2 * H].rearrange("p g h -> p h g"), ALU.max))
                flat = [t[:, :, :].rearrange("p h g -> p (h g)") for t in (here, before, after)]
                rise = [rises[:, bass.ds(w, 1), k, :].rearrange("p a x -> p (a x)") for k in range(2)]
                ch.add(v.tensor_tensor_scan(flat[1], rise[0], flat[0], -BIG, ALU.add, ALU.max))
                yield from step_of(ch, v.tensor_tensor_scan(flat[2][:, ::-1], rise[1], flat[0][:, ::-1], -BIG, ALU.add, ALU.max))
                v.wait_ge(top_kept, WG * w + 1)
                v.tensor_tensor(top[:, :, :].rearrange("p g h -> p h g"), before[:, :, :], after[:, :, :], ALU.max).then_inc(top_ready, 1)
                yield
                v.wait_ge(top_ready, w + 1)

            def greatest(w, r, ch):
                yield from step_of(ch, v.tensor_tensor(logit[:, 0:WG, :], top[:, :, :], node[r % 2][:, :, 0:H], ALU.add))
                yield from step_of(ch, v.scalar_tensor_tensor(out=fin[:, :, H:2 * H], in0=logit[:, :, :], scalar=SLOPE, in1=logit[:, :, :],
                                               op0=ALU.mult, op1=ALU.max))
                x = fin[:, 0:WG, :]
                yield from split(ch, x, [parts[:, k, :, :] for k in range(3)],
                                 rest2[:, :].rearrange("p (g x) -> p g x", g=WG), parts_ready)
                v.wait_ge(fade_ready, w)
                v.tensor_tensor(fd[:, :], fin[:, WG, H:2 * H], fin[:, 0, H:2 * H], ALU.subtract).then_inc(fd_ready, 1)
                yield

            def spread_terms(w, r, ch):
                v.wait_ge(ad_ready, w + 2)
                yield from step_of(ch, v.tensor_tensor(as_ghj(tu[:, :]), as_ghj(score[r % 2][:, :]), ghj(ps_ad[:, :, 0:H]), ALU.add))
                yield from step_of(ch, v.scalar_tensor_tensor(out=lr[:, :], in0=tu[:, :], scalar=SLOPE, in1=tu[:, :],
                                               op0=ALU.mult, op1=ALU.max))
                v.wait_ge(weights_ready, w)
                yield from step_of(ch, v.tensor_tensor(as_ghj(diff[:, :]), as_ghj(lr[:, :]), ghj(ps_ad[:, :, H:2 * H]), ALU.subtract))
                v.tensor_scalar(diff[:, :], diff[:, :], 0.0, None, ALU.min).then_inc(diff_ready, 1)
                assert ch.n == STEPS, ch.n
                yield

            def first_stage(w, r, ch):
                yield from last_values(w, ch)
                node_terms(w, r, ch)
                yield from maxima(w, r, ch)
                yield from greatest(w, r, ch)
                yield from spread_terms(w, r, ch)

            def weigh(w, r, c):
                v.wait_ge(weights_ready, w + 1)
                g4 = G[r][:, 4 * c:4 * c + 4, :].rearrange("p s (h f) -> p (s h) f", h=H)
                v.tensor_tensor(g4[:, :, 0:D], g4[:, :, 0:D], g4[:, :, D:D + 1].broadcast_to([P, 4 * H, D]), ALU.mult
                                ).then_inc(weighed, 1)

            def fade_sums(w, b):
                v.wait_ge(fade_ready, w + 1)
                v.wait_ge(added, WG * w + BANKS)
                a = row(acc, b).rearrange("p (h f) -> p h f", h=H)
                v.tensor_tensor(a, a, fade[:, :].unsqueeze(2).broadcast_to([P, H, D + 1]), ALU.mult).then_inc(faded, 1)

            def add(w, g, b):
                v.wait_ge(summed, WG * w + g + 1 + WG * RING)
                if g == 0:
                    v.wait_ge(faded, w + 1)
                else:
                    v.wait_ge(added, WG * w + g + BANKS)
                a = row(acc, b)
                v.tensor_tensor(a, a, ps_o[g % BANKS][:, 0:RW], ALU.add).then_inc(added, 1)

            for w in range(2):
                for c in range(4):
                    onehots(w, w, c, False)
            ch = scan(0, 0, 0)
            assert len(list(first_stage(0, 0, ch))) == 21

            def step(i, r, last):
                w = 4 * i + r
                n = (r + 1) % RING
                more = exists(i, r, 2)
                stage = iter(())
                if not last:
                    stage = first_stage(w + 1, n, scan(w + 1, i + (r + 1) // RING, n))
                def first(steps):
                    for _ in range(steps):
                        next(stage, None)

                this = blocks_of(v, w)
                weigh(w, r, 0)
                first(5)
                weigh(w, r, 1)
                b = next(this)
                fade_sums(w, b)
                first(2)
                add(w, 0, b)
                first(2)
                if more:
                    onehots(w + 2, r, 0)
                first(2)
                add(w, 1, next(this))
                first(2)
                if more:
                    onehots(w + 2, r, 1)
                first(2)
                if more:
                    onehots(w + 2, r, 2)
                first(2)
                weigh(w, r, 2)
                add(w, 2, next(this))
                first(4)
                weigh(w, r, 3)
                add(w, 3, next(this))
                add(w, 4, next(this))
                if more:
                    onehots(w + 2, r, 3)
                for g in range(5, WG):
                    add(w, g, next(this))

            over_windows(v, step)
            v.wait_ge(added, WG * NW + BANKS)


def normalize_tiles(nc, name, buf, gain, offset):
    with Phase(nc, name) as ph:
        stats = ph.sb("stats", [P, NB, 6])
        mv = ph.sb("mv", [P, NB, 2])
        sd = ph.sb("sd", [P, NB])
        rstd = ph.sb("rstd", [P, NB])
        eps = ph.sb("eps", [P, 1])
        vecs = ph.sb("vecs", [P, 2, C])
        eps_set = ph.sem("eps_set")
        vecs_in = ph.sem("vecs_in")
        stats_done = ph.sem("stats_done")
        moments = ph.sem("moments")
        sd_ready = ph.sem("sd_ready")
        rstd_ready = ph.sem("rstd_ready")
        centred = ph.sem("centred")
        scaled = ph.sem("scaled")
        block = ph.block()

        @block.sync
        def _(sp):
            if gain is not None:
                for n, vec in enumerate((gain, offset)):
                    sp.dma_start(vecs[:, n, :], broadcast_row(vec)).then_inc(vecs_in, 16)

        @block.gpsimd
        def _(g):
            g.memset(eps[:, :], LN_EPS).then_inc(eps_set, 1)

        @block.scalar
        def _(a):
            a.wait_ge(eps_set, 1)
            a.wait_ge(moments, NB)
            a.activation(sd[:, :], mv[:, :, 1], ACT.Sqrt, bias=eps[:, :]).then_inc(sd_ready, 1)

        @block.vector
        def _(v):
            for b in range(NB):
                v.bn_stats(stats[:, b, :], buf[:, b, :]).then_inc(stats_done, 1)
            v.wait_ge(stats_done, NB)
            for b in range(NB):
                v.bn_aggr(mv[:, b, :], stats[:, b, :]).then_inc(moments, 1)
            v.wait_ge(sd_ready, 1)
            v.reciprocal(rstd[:, :], sd[:, :]).then_inc(rstd_ready, 1)
            v.wait_ge(rstd_ready, 1)
            if gain is None:
                for b in range(NB):
                    v.tensor_scalar(buf[:, b, :], buf[:, b, :], mv[:, b, 0:1], rstd[:, b:b + 1],
                                    ALU.subtract, ALU.mult).then_inc(scaled, 1)
            else:
                v.wait_ge(vecs_in, 32)
                for b in range(NB):
                    v.scalar_tensor_tensor(out=buf[:, b, :], in0=buf[:, b, :], scalar=mv[:, b, 0:1],
                                           in1=vecs[:, 0, :], op0=ALU.subtract, op1=ALU.mult).then_inc(centred, 1)
                v.wait_ge(centred, NB)
                for b in range(NB):
                    v.scalar_tensor_tensor(out=buf[:, b, :], in0=buf[:, b, :], scalar=rstd[:, b:b + 1],
                                           in1=vecs[:, 1, :], op0=ALU.mult, op1=ALU.add).then_inc(scaled, 1)
            v.wait_ge(scaled, NB)


def move_tiles(nc, name, to, of):
    with Phase(nc, name) as ph:
        moved = ph.sem("moved")
        cleared = ph.sem("cleared")
        block = ph.block()

        def rows(ap, a, z):
            return ap[:, :, :] if len(ap.shape) == 3 else ap.rearrange("(b p) c -> p b c", p=P)[:, a:z, :]

        @block.vector
        def _(v):
            if len(of.shape) == 2 and of.shape[0] == N:
                v.memset(to[:, NB - 1, :], 0.0).then_inc(cleared, 1)

        @block.sync
        def _(sp):
            if len(of.shape) == 2 and of.shape[0] == N:
                full = (NB - 1) * P
                sp.dma_start(to[:, 0:NB - 1, :], of[0:full, :].rearrange("(b p) c -> p b c", p=P)).then_inc(moved, 16)
                sp.wait_ge(cleared, 1)
                sp.dma_start(to[0:TAIL, NB - 1, :], of[full:N, :]).then_inc(moved, 16)
                sp.wait_ge(moved, 32)
            else:
                sp.dma_start(rows(to, 0, NB), rows(of, 0, NB)).then_inc(moved, 16)
                sp.wait_ge(moved, 16)


M_HEADS = 8
M_D = C // M_HEADS
GH = P // M_D


def turn_weights(nc, name, w_dram, out, ident):
    rows = w_dram.shape[0]
    with Phase(nc, name) as ph:
        w = ph.sb("w", [P, rows // P, C])
        ps = [ph.ps(f"ps{k}", [P, 512]) for k in range(2)]
        w_in = ph.sem("w_in")
        turned = ph.sem("turned")
        copied = ph.sem("copied")
        block = ph.block()

        @block.sync
        def _(sp):
            sp.dma_start(w[:, :, :], w_dram.rearrange("(r p) c -> p r c", p=P)).then_inc(w_in, 16)

        @block.tensor
        def _(pe):
            pe.wait_ge(w_in, 16)
            for r in range(rows // P):
                if r >= 2:
                    pe.wait_ge(copied, r - 1)
                for k in range(2):
                    mm = pe.transpose(ps[r % 2][:, k * P:(k + 1) * P], w[:, r, k * P:(k + 1) * P], ident[:, :])
                mm.then_inc(turned, 1)

        @block.vector
        def _(v):
            for r in range(rows // P):
                v.wait_ge(turned, r + 1)
                v.tensor_copy(out[:, :, r * P:(r + 1) * P], ps[r % 2][:, 0:C].rearrange("p (k o) -> p k o", k=2)
                              ).then_inc(copied, 1)
            v.wait_ge(copied, rows // P)


def tile_of(t, b):
    return t[:, bass.ds(b, 1), :].rearrange("p a c -> p (a c)")


def stage_tiles(g, buf, stage, staged, turned):
    def step(i, half, last):
        b = 2 * i + half
        g.wait_ge(turned, b + 1)
        g.tensor_copy(stage[:, half, :], tile_of(buf, b)).then_inc(staged, 1)

    over_tiles(g, step)


def turn_tile(pe, stage, half, ps, ident):
    for k in range(2):
        mm = pe.transpose(ps[:, k * P:(k + 1) * P], stage[:, half, k * P:(k + 1) * P], ident[:, :])
    return mm


def mix_keys(nc, st, XN, WT, KV, xslot):
    ident = st["ident"]
    VW = P + 2
    with Phase(nc, "keys") as ph:
        stage = ph.sb("stage", [P, 2, C])
        xs = ph.sb("xs", [P, 2, C])
        low = ph.sb("low", [P, 2, C])
        ex = ph.sb("ex", [P, 2, C])
        kp = ph.sb("kp", [P, 2, C])
        v1 = ph.sb("v1", [P, 2, 2, VW])
        psA = [ph.ps(f"psA{k}", [P, 512]) for k in range(2)]
        psK = [ph.ps(f"psK{k}", [P, 512]) for k in range(2)]
        psV = [ph.ps(f"psV{k}", [P, 512]) for k in range(2)]
        staged = ph.sem("staged")
        turned = ph.sem("turned")
        xT_ready = ph.sem("xT_ready")
        kv_ready = ph.sem("kv_ready")
        low_ready = ph.sem("low_ready")
        ex_ready = ph.sem("ex_ready")
        v_ready = ph.sem("v_ready")
        kp_ready = ph.sem("kp_ready")
        outer = ph.sem("outer")
        ones_set = ph.sem("ones_set")
        cleared = ph.sem("cleared")
        kv_out = ph.sem("kv_out")
        zeros = ph.sb("zeros", [P, 8 * C])
        zeros_set = ph.sem("zeros_set")
        slots_cleared = ph.sem("slots_cleared")
        block = ph.block()

        @block.sync
        def _(sp):
            sp.wait_ge(zeros_set, 1)
            for t in range(0, NT, 8):
                k = min(8, NT - t)
                sp.dma_start(xslot[t * P:(t + k) * P, :].rearrange("(p k) c -> p (k c)", p=P), zeros[:, 0:k * C]
                             ).then_inc(slots_cleared, 16)
            sp.wait_ge(slots_cleared, 16 * (-(-NT // 8)))

        @block.gpsimd
        def _(g):
            g.memset(zeros[:, :], 0.0).then_inc(zeros_set, 1)
            g.memset(v1[:, :, :, P:VW], 1.0).then_inc(ones_set, 1)
            g.memset(KV[:, :, :], 0.0).then_inc(cleared, 1)
            stage_tiles(g, XN, stage, staged, turned)

        @block.tensor
        def _(pe):
            for s in (turned, kv_ready, outer):
                pe.sem_inc(s, 2)
            pe.wait_ge(ones_set, 1)

            def turn(b, half):
                pe.wait_ge(staged, b + 1)
                pe.wait_ge(xT_ready, b + 1)
                turn_tile(pe, stage, half, psA[half], ident).then_inc(turned, 1)

            def keys_values(b, half):
                pe.wait_ge(xT_ready, b + 3)
                pe.wait_ge(kp_ready, b + 1)
                pe.wait_ge(v_ready, b + 1)
                for k in range(2):
                    mm = pe.matmul(psK[half][:, :], xs[:, half, k * P:(k + 1) * P], WT[:, k, C:3 * C],
                                   start=(k == 0), stop=(k == 1))
                mm.then_inc(kv_ready, 1)

            def outers(b, half, first, last):
                n = TAIL if last else P
                pe.wait_ge(kp_ready, b + 3)
                pe.wait_ge(v_ready, b + 3)
                for g in range(2):
                    mm = pe.matmul(psV[g][:, 0:VW], kp[0:n, half, g * P:(g + 1) * P], v1[0:n, half, g, :],
                                   start=first, stop=last)
                mm.then_inc(outer, 1)

            turn(0, 0)
            turn(1, 1)
            keys_values(0, 0)
            turn(2, 0)
            keys_values(1, 1)
            outers(0, 0, True, False)
            with pe.Fori(1, (NB - 1) // 2) as i:
                turn(2 * i + 1, 1)
                keys_values(2 * i, 0)
                outers(2 * i - 1, 1, False, False)
                turn(2 * i + 2, 0)
                keys_values(2 * i + 1, 1)
                outers(2 * i, 0, False, False)
            keys_values(NB - 1, 0)
            outers(NB - 2, 1, False, False)
            outers(NB - 1, 0, False, True)

        @block.scalar
        def _(a):
            a.sem_inc(xT_ready, 2)
            a.sem_inc(v_ready, 2)
            a.wait_ge(ones_set, 1)

            def copy_x(b, half):
                a.wait_ge(turned, b + 3)
                a.wait_ge(kv_ready, b + 1)
                a.activation(xs[:, half, :], psA[half][:, 0:C], ACT.Copy).then_inc(xT_ready, 1)

            copy_x(0, 0)

            def step(i, half, last):
                b = 2 * i + half
                if not last:
                    copy_x(b + 1, 1 - half)
                a.wait_ge(kv_ready, b + 3)
                a.wait_ge(outer, b + 1)
                a.activation(v1[:, half, :, 0:P], psK[half][:, C:2 * C].rearrange("p (g c) -> p g c", g=2), ACT.Copy
                             ).then_inc(v_ready, 1)
                a.wait_ge(low_ready, b + 1)
                a.wait_ge(kp_ready, b + 1)
                a.activation(ex[:, half, :], low[:, half, :], ACT.Exp).then_inc(ex_ready, 1)

            over_tiles(a, step)

        @block.vector
        def _(v):
            v.sem_inc(kp_ready, 2)

            def step(i, half, last):
                b = 2 * i + half
                v.wait_ge(kv_ready, b + 3)
                v.wait_ge(kp_ready, b + 1)
                v.wait_ge(v_ready, b + 3)
                v.tensor_scalar(low[:, half, :], psK[half][:, 0:C], 0.0, None, ALU.min).then_inc(low_ready, 1)
                v.wait_ge(ex_ready, b + 1)
                v.wait_ge(outer, b + 1)
                v.scalar_tensor_tensor(out=kp[:, half, :], in0=psK[half][:, 0:C], scalar=0.0, in1=ex[:, half, :],
                                       op0=ALU.max, op1=ALU.add).then_inc(kp_ready, 1)

            over_tiles(v, step)
            v.wait_ge(outer, NB + 2)
            v.wait_ge(cleared, 1)
            for g in range(2):
                for h in range(GH):
                    r = slice(h * M_D, (h + 1) * M_D)
                    v.tensor_copy(KV[r, g, r], psV[g][r, r]).then_inc(kv_out, 1)
                    v.tensor_copy(KV[r, g, P + h:P + h + 1], psV[g][r, P:P + 1]).then_inc(kv_out, 1)
            v.wait_ge(kv_out, 4 * GH)


def mix_queries(nc, st, XN, WT, KV):
    ident = st["ident"]
    with Phase(nc, "queries") as ph:
        stage = ph.sb("stage", [P, 2, C])
        xs = ph.sb("xs", [P, 2, C])
        low = ph.sb("low", [P, 2, C])
        ex = ph.sb("ex", [P, 2, C])
        qp = ph.sb("qp", [P, 2, C])
        den = ph.sb("den", [P, 2, M_HEADS])
        t = ph.sb("t", [P, 2, C])
        psA = [ph.ps(f"psA{k}", [P, 512]) for k in range(2)]
        psQ = [ph.ps(f"psQ{k}", [P, 512]) for k in range(2)]
        psT = [ph.ps(f"psT{k}", [P, 512]) for k in range(2)]
        staged = ph.sem("staged")
        turned = ph.sem("turned")
        xT_ready = ph.sem("xT_ready")
        q_ready = ph.sem("q_ready")
        low_ready = ph.sem("low_ready")
        ex_ready = ph.sem("ex_ready")
        qp_ready = ph.sem("qp_ready")
        read = ph.sem("read")
        chain = ph.sem("chain")
        mixed = ph.sem("mixed")
        block = ph.block()
        KW = P + GH

        @block.gpsimd
        def _(g):
            stage_tiles(g, XN, stage, staged, turned)

        @block.tensor
        def _(pe):
            for s in (turned, q_ready, read):
                pe.sem_inc(s, 2)

            def turn(b, half):
                pe.wait_ge(staged, b + 1)
                pe.wait_ge(xT_ready, b + 1)
                turn_tile(pe, stage, half, psA[half], ident).then_inc(turned, 1)

            def queries(b, half):
                pe.wait_ge(xT_ready, b + 3)
                pe.wait_ge(qp_ready, b + 1)
                for g in range(2):
                    for k in range(2):
                        mm = pe.matmul(psQ[half][:, g * P:(g + 1) * P], WT[:, k, g * P:(g + 1) * P],
                                       xs[:, half, k * P:(k + 1) * P], start=(k == 0), stop=(k == 1))
                mm.then_inc(q_ready, 1)

            def reads(b, half):
                pe.wait_ge(qp_ready, b + 3)
                pe.wait_ge(mixed, b + 1)
                for g in range(2):
                    mm = pe.matmul(psT[half][:, g * KW:(g + 1) * KW], qp[:, half, g * P:(g + 1) * P], KV[:, g, :],
                                   start=True, stop=True)
                mm.then_inc(read, 1)

            turn(0, 0)

            def step(i, half, last):
                b = 2 * i + half
                if not last:
                    turn(b + 1, 1 - half)
                queries(b, half)
                if half or not is_zero(i):
                    reads(b - 1, 1 - half)

            over_tiles(pe, step)
            reads(NB - 1, 0)

        @block.scalar
        def _(a):
            a.sem_inc(xT_ready, 2)

            def copy_x(b, half):
                a.wait_ge(turned, b + 3)
                a.wait_ge(q_ready, b + 1)
                a.activation(xs[:, half, :], psA[half][:, 0:C], ACT.Copy).then_inc(xT_ready, 1)

            copy_x(0, 0)

            def step(i, half, last):
                b = 2 * i + half
                if not last:
                    copy_x(b + 1, 1 - half)
                a.wait_ge(low_ready, b + 1)
                a.wait_ge(qp_ready, b + 1)
                a.activation(ex[:, half, :], low[:, half, :], ACT.Exp).then_inc(ex_ready, 1)

            over_tiles(a, step)

        @block.vector
        def _(v):
            v.sem_inc(qp_ready, 2)
            v.sem_inc(mixed, 2)

            def feature(b, half):
                v.wait_ge(q_ready, b + 3)
                v.wait_ge(qp_ready, b + 1)
                v.tensor_scalar(low[:, half, :], psQ[half][:, 0:C], 0.0, None, ALU.min).then_inc(low_ready, 1)
                v.wait_ge(ex_ready, b + 1)
                v.wait_ge(read, b + 1)
                v.scalar_tensor_tensor(out=qp[:, half, :], in0=psQ[half][:, 0:C], scalar=0.0, in1=ex[:, half, :],
                                       op0=ALU.max, op1=ALU.add).then_inc(qp_ready, 1)

            def result(b, half):
                ch = Chain(v, chain, 3 * b)
                v.wait_ge(read, b + 3)
                v.wait_ge(mixed, b + 1)
                r = psT[half][:, 0:2 * KW].rearrange("p (g k) -> p g k", g=2)
                d = den[:, half, :].rearrange("p (g h) -> p g h", g=2)
                ch.link(v.tensor_scalar(d, r[:, :, P:KW], 1e-6, None, ALU.add))
                ch.link(v.reciprocal(den[:, half, :], den[:, half, :]))
                for g in range(2):
                    ins = v.tensor_tensor(t[:, half, g * P:(g + 1) * P].rearrange("p (h m) -> p h m", h=GH),
                                          r[:, g, 0:P].rearrange("p (h m) -> p h m", h=GH),
                                          d[:, g, :].unsqueeze(2).broadcast_to([P, GH, M_D]), ALU.mult)
                    if g:
                        ch.link(ins)
                assert ch.n == 3
                v.wait_ge(staged, b + 1)
                v.tensor_tensor(tile_of(XN, b), tile_of(XN, b), t[:, half, :], ALU.add).then_inc(mixed, 1)

            feature(0, 0)

            def step(i, half, last):
                b = 2 * i + half
                if not last:
                    feature(b + 1, 1 - half)
                result(b, half)

            over_tiles(v, step)
            v.wait_ge(mixed, NB + 2)


def mix_mlp(nc, st, io, XN, W1T, W2T):
    ident = st["ident"]
    with Phase(nc, "mlp") as ph:
        stage = ph.sb("stage", [P, 2, C])
        xs = ph.sb("xs", [P, 2, C])
        hs = ph.sb("hs", [P, 2, C])
        b1 = ph.sb("b1", [P, 2])
        b2 = ph.sb("b2", [P, C])
        t = ph.sb("t", [P, 2, C])
        psA = [ph.ps(f"psA{k}", [P, 512]) for k in range(2)]
        psH = [ph.ps(f"psH{k}", [P, 512]) for k in range(2)]
        psY = [ph.ps(f"psY{k}", [P, 512]) for k in range(2)]
        biases_in = ph.sem("biases_in")
        staged = ph.sem("staged")
        turned = ph.sem("turned")
        xT_ready = ph.sem("xT_ready")
        hidden = ph.sem("hidden")
        gelu_ready = ph.sem("gelu_ready")
        y_ready = ph.sem("y_ready")
        biased = ph.sem("biased")
        added = ph.sem("added")
        block = ph.block()

        @block.sync
        def _(sp):
            with nc.allow_non_contiguous_dma(reason="256 words, once"):
                sp.dma_start(b1[:, :], io["mix_b1"].rearrange("(k p) -> p k", p=P)).then_inc(biases_in, 16)
            sp.dma_start(b2[:, :], broadcast_row(io["mix_b2"])).then_inc(biases_in, 16)

        @block.gpsimd
        def _(g):
            stage_tiles(g, XN, stage, staged, turned)

        @block.tensor
        def _(pe):
            for s in (turned, hidden, y_ready):
                pe.sem_inc(s, 2)

            def turn(b, half):
                pe.wait_ge(staged, b + 1)
                pe.wait_ge(xT_ready, b + 1)
                turn_tile(pe, stage, half, psA[half], ident).then_inc(turned, 1)

            def up(b, half):
                pe.wait_ge(xT_ready, b + 3)
                pe.wait_ge(gelu_ready, b + 1)
                for g in range(2):
                    for k in range(2):
                        mm = pe.matmul(psH[half][:, g * P:(g + 1) * P], W1T[:, k, g * P:(g + 1) * P],
                                       xs[:, half, k * P:(k + 1) * P], start=(k == 0), stop=(k == 1))
                mm.then_inc(hidden, 1)

            def down(b, half):
                pe.wait_ge(gelu_ready, b + 3)
                pe.wait_ge(biased, b + 1)
                for k in range(2):
                    mm = pe.matmul(psY[half][:, 0:C], hs[:, half, k * P:(k + 1) * P], W2T[:, k, :],
                                   start=(k == 0), stop=(k == 1))
                mm.then_inc(y_ready, 1)

            turn(0, 0)

            def step(i, half, last):
                b = 2 * i + half
                if not last:
                    turn(b + 1, 1 - half)
                up(b, half)
                if half or not is_zero(i):
                    down(b - 1, 1 - half)

            over_tiles(pe, step)
            down(NB - 1, 0)

        @block.scalar
        def _(a):
            a.sem_inc(xT_ready, 2)
            a.sem_inc(gelu_ready, 2)
            a.wait_ge(biases_in, 32)

            def turn(b, half):
                a.wait_ge(turned, b + 3)
                a.wait_ge(hidden, b + 1)
                a.activation(xs[:, half, :], psA[half][:, 0:C], ACT.Copy).then_inc(xT_ready, 1)

            turn(0, 0)

            def step(i, half, last):
                b = 2 * i + half
                if not last:
                    turn(b + 1, 1 - half)
                a.wait_ge(hidden, b + 3)
                a.wait_ge(y_ready, b + 1)
                for g in range(2):
                    ins = a.activation(hs[:, half, g * P:(g + 1) * P], psH[half][:, g * P:(g + 1) * P], ACT.Gelu,
                                       bias=b1[:, g:g + 1])
                ins.then_inc(gelu_ready, 1)

            over_tiles(a, step)

        @block.vector
        def _(v):
            v.sem_inc(biased, 2)
            v.sem_inc(added, 1)
            v.wait_ge(biases_in, 32)

            def step(i, half, last):
                b = 2 * i + half
                v.wait_ge(y_ready, b + 3)
                v.wait_ge(added, b + 1)
                v.tensor_tensor(t[:, half, :], psY[half][:, 0:C], b2[:, :], ALU.add).then_inc(biased, 1)
                v.wait_ge(biased, b + 3)
                v.wait_ge(staged, b + 1)
                v.tensor_tensor(tile_of(XN, b), tile_of(XN, b), t[:, half, :], ALU.add).then_inc(added, 1)

            over_tiles(v, step)
            v.wait_ge(added, NB + 1)


EX = 8
FH = 512
HC = FH // P
NT = (2 * N + EX * (P - 1)) // P


def route(nc, st, io, XN, W1, W2, b1, b2, wts, slots, owner, dr):
    ident, iota = st["ident"], st["iota"]
    with Phase(nc, "route") as ph:
        stage = ph.sb("stage", [P, 2, C])
        xs = ph.sb("xs", [P, 2, C])
        Wr = ph.sb("Wr", [P, 2, EX])
        br = ph.sb("br", [P, EX])
        lg = ph.sb("lg", [P, NB, EX])
        top = ph.sb("top", [P, NB, 8])
        topi = ph.sb("topi", [P, NB, 8], mybir.dt.uint32)
        topf = ph.sb("topf", [P, NB, 2])
        gap = ph.sb("gap", [P, NB])
        w = wts
        upper = ph.sb("upper", [P, P])
        upperb = ph.sb("upperb", [P, P], BF16)
        onesb = ph.sb("onesb", [P, P], BF16)
        valid = ph.sb("valid", [P, 1])
        chosen = ph.sb("chosen", [P, EX, NB], BF16)
        go_on = ph.sb("go_on", [P, EX, NB])
        total = ph.sb("total", [P, EX, NB])
        upto = ph.sb("upto", [P, EX, NB])
        place = ph.sb("place", [P, EX, NB])
        tilesF = ph.sb("tilesF", [P, EX])
        tilesI = ph.sb("tilesI", [P, EX], I32)
        ends = ph.sb("ends", [P, EX])
        starts = ph.sb("starts", [P, EX])
        slotF = ph.sb("slotF", [P, 2, NB])
        ownerF = ph.sb("ownerF", [P, NT])
        den = ph.sb("den", [P, NB])
        pick = ph.sb("pick", [P, 2, NB, EX])
        psA = [ph.ps(f"psA{k}", [P, 512]) for k in range(2)]
        psL = [ph.ps(f"psL{k}", [P, 512]) for k in range(2)]
        psR = ph.ps("psR", [P, 512])
        psC = ph.ps("psC", [P, 512])
        router_in = ph.sem("router_in")
        staged = ph.sem("staged")
        turned = ph.sem("turned")
        xT_ready = ph.sem("xT_ready")
        shapes = ph.sem("shapes")
        chosen_ready = ph.sem("chosen_ready")
        ranked = ph.sem("ranked")
        slots_ready = ph.sem("slots_ready")
        scattered = ph.sem("scattered")
        experts_in = ph.sem("experts_in")
        logits = ph.sem("logits")
        biased = ph.sem("biased")
        topped = ph.sem("topped")
        found = ph.sem("found")
        chain = ph.sem("chain")
        gap_ready = ph.sem("gap_ready")
        exp_ready = ph.sem("exp_ready")
        block = ph.block()

        @block.sync
        def _(sp):
            sp.dma_start(Wr[:, :, :], io["ffn_Wr"].rearrange("(k p) e -> p k e", p=P)).then_inc(router_in, 16)
            sp.dma_start(br[:, :], broadcast_row(io["ffn_br"])).then_inc(router_in, 16)
            for e in range(EX):
                sp.dma_start(W1[:, e, :, :], io["ffn_W1"][e].rearrange("(k p) f -> p k f", p=P)).then_inc(experts_in, 16)
                sp.dma_start(W2[:, e, :, :], io["ffn_W2"][e].rearrange("(c p) o -> p c o", p=P)).then_inc(experts_in, 16)
                sp.dma_start(b1[:, e, :], broadcast_row(io["ffn_b1"][e])).then_inc(experts_in, 16)
                sp.dma_start(b2[:, e, :], broadcast_row(io["ffn_b2"][e])).then_inc(experts_in, 16)
            sp.wait_ge(experts_in, 16 * 4 * EX)

        @block.gpsimd
        def _(g):
            g.memset(upper[:, :], 1.0).then_inc(shapes, 1)
            g.memset(valid[:, :], 1.0).then_inc(shapes, 1)
            g.wait_ge(shapes, 2)
            g.affine_select(out=upper[:, :], in_=upper[:, :], compare_op=ALU.is_ge, fill=0.0,
                            base=-1, pattern=[[1, P]], channel_multiplier=-1).then_inc(shapes, 1)
            g.affine_select(out=valid[:, :], in_=valid[:, :], compare_op=ALU.is_ge, fill=0.0,
                            base=TAIL - 1, pattern=[[0, 1]], channel_multiplier=-1).then_inc(shapes, 1)
            stage_tiles(g, XN, stage, staged, turned)
            g.wait_ge(slots_ready, 2)
            for b in range(NB):
                n = TAIL if b == NB - 1 else P
                for k in range(2):
                    g.indirect_dma_start(dr["xslot"], bass.IndirectOffsetOnAxis(slots[0:n, k, b:b + 1], 0),
                                         XN[0:n, b, :], None).then_inc(scattered, 16)
            g.wait_ge(scattered, 16 * 2 * NB)

        @block.tensor
        def _(pe):
            for s in (turned, logits):
                pe.sem_inc(s, 2)
            pe.wait_ge(router_in, 32)

            def turn(b, half):
                pe.wait_ge(staged, b + 1)
                pe.wait_ge(xT_ready, b + 1)
                turn_tile(pe, stage, half, psA[half], ident).then_inc(turned, 1)

            turn(0, 0)

            def step(i, half, last):
                b = 2 * i + half
                if not last:
                    turn(b + 1, 1 - half)
                pe.wait_ge(xT_ready, b + 3)
                pe.wait_ge(biased, b + 1)
                for k in range(2):
                    mm = pe.matmul(psL[half][:, 0:EX], xs[:, half, k * P:(k + 1) * P], Wr[:, k, :],
                                   start=(k == 0), stop=(k == 1))
                mm.then_inc(logits, 1)

            over_tiles(pe, step)
            pe.wait_ge(chosen_ready, 1)
            flat = chosen[:, :, :].rearrange("p e b -> p (e b)")
            pe.matmul(psR[:, 0:EX * NB], upperb[:, :], flat, start=True, stop=True)
            pe.matmul(psC[:, 0:EX * NB], onesb[:, :], flat, start=True, stop=True).then_inc(ranked, 1)

        @block.scalar
        def _(a):
            a.sem_inc(xT_ready, 2)

            def step(i, half, last):
                b = 2 * i + half
                a.wait_ge(turned, b + 3)
                a.wait_ge(logits, b + 1)
                a.activation(xs[:, half, :], psA[half][:, 0:C], ACT.Copy).then_inc(xT_ready, 1)

            over_tiles(a, step)
            a.wait_ge(gap_ready, 1)
            a.activation(w[:, :, 1], gap[:, :], ACT.Exp).then_inc(exp_ready, 1)

        @block.vector
        def _(v):
            v.sem_inc(biased, 2)
            v.wait_ge(router_in, 32)

            def step(i, half, last):
                b = 2 * i + half
                v.wait_ge(logits, b + 3)
                v.tensor_tensor(tile_of(lg, b), psL[half][:, 0:EX], br[:, :], ALU.add).then_inc(biased, 1)

            over_tiles(v, step)
            v.wait_ge(biased, NB + 2)
            for b in range(NB):
                v.max(top[:, b, :], lg[:, b, :]).then_inc(topped, 1)
            v.wait_ge(topped, NB)
            for b in range(NB):
                v.max_index(topi[:, b, :], top[:, b, :], lg[:, b, :]).then_inc(found, 1)
            v.tensor_tensor(gap[:, :], top[:, :, 1], top[:, :, 0], ALU.subtract).then_inc(gap_ready, 1)
            v.wait_ge(found, NB)
            ch = Chain(v, chain)
            ch.link(v.tensor_copy(topf[:, :, :], topi[:, :, 0:2]))
            v.wait_ge(exp_ready, 1)
            ch.link(v.tensor_scalar(den[:, :], w[:, :, 1], 1.0, None, ALU.add))
            ch.link(v.reciprocal(den[:, :], den[:, :]))
            ch.add(v.tensor_copy(w[:, :, 0], den[:, :]))
            ch.link(v.tensor_tensor(w[:, :, 1], w[:, :, 1], den[:, :], ALU.mult))
            places = iota[:, 0:EX].unsqueeze(1).broadcast_to([P, NB, EX])
            for k in range(2):
                ch.add(v.tensor_tensor(pick[:, k, :, :], places, topf[:, :, k:k + 1].broadcast_to([P, NB, EX]), ALU.is_equal))
            ch.wait()
            v.wait_ge(shapes, 4)
            for k in range(2):
                ch.add(v.tensor_scalar(pick[:, k, NB - 1, :], pick[:, k, NB - 1, :], valid[:, :], None, ALU.mult))
            ch.add(v.tensor_copy(upperb[:, :], upper[:, :]))
            ch.add(v.memset(onesb[:, :], 1.0))
            ch.link(v.memset(go_on[:, :, 1:NB], 1.0))
            ch.link(v.memset(go_on[:, :, 0:1], 0.0))
            v.tensor_tensor(chosen[:, :, :].rearrange("p e b -> p b e"), pick[:, 0, :, :], pick[:, 1, :, :], ALU.add
                            ).then_inc(chosen_ready, 1)
            v.wait_ge(ranked, 1)
            flat = [t[:, :, :].rearrange("p e b -> p (e b)") for t in (go_on, total, upto, place)]
            ch.link(v.tensor_copy(flat[1], psC[:, 0:EX * NB]))
            ch.link(v.tensor_tensor_scan(flat[2], flat[0], flat[1], 0.0, ALU.mult, ALU.add))
            ch.link(v.tensor_scalar(tilesF[:, :], upto[:, :, NB - 1], float(P - 1), None, ALU.add))
            ch.link(v.tensor_copy(tilesI[:, :], tilesF[:, :]))
            ch.link(v.tensor_scalar(tilesI[:, :], tilesI[:, :], 7, None, ALU.arith_shift_right))
            ch.link(v.tensor_copy(tilesF[:, :], tilesI[:, :]))
            ch.link(v.tensor_tensor_scan(ends[:, :], go_on[:, 0, 1:EX + 1], tilesF[:, :], 0.0, ALU.mult, ALU.add))
            ch.link(v.tensor_tensor(starts[:, :], ends[:, :], tilesF[:, :], ALU.subtract))
            ch.link(v.tensor_scalar(starts[:, :], starts[:, :], float(P), None, ALU.mult))
            ch.link(v.tensor_tensor(flat[3], flat[2], flat[1], ALU.subtract))
            ch.link(v.tensor_tensor(flat[3], flat[3], psR[:, 0:EX * NB], ALU.add))
            ch.link(v.tensor_tensor(place[:, :, :], place[:, :, :], starts[:, :].unsqueeze(2).broadcast_to([P, EX, NB]), ALU.add))
            for k in range(2):
                ch.link(v.tensor_tensor(pick[:, k, :, :], pick[:, k, :, :], place[:, :, :].rearrange("p e b -> p b e"), ALU.mult))
                ch.link(v.tensor_reduce(slotF[:, k, :], pick[:, k, :, :], AX.X, ALU.add))
                v.tensor_copy(slots[:, k, :], slotF[:, k, :]).then_inc(slots_ready, 1)
            ch.link(v.tensor_scalar(ownerF[:, :], iota[:, 0:NT], ends[:, 0:1], None, ALU.is_ge))
            for e in range(1, EX - 1):
                ch.link(v.scalar_tensor_tensor(out=ownerF[:, :], in0=iota[:, 0:NT], scalar=ends[:, e:e + 1], in1=ownerF[:, :],
                                               op0=ALU.is_ge, op1=ALU.add))
            ch.link(v.tensor_copy(owner[:, :], ownerF[:, :]))


def experts(nc, st, W1, W2, b1, b2, owner, dr):
    ident = st["ident"]
    with Phase(nc, "experts") as ph:
        X = ph.sb("X", [P, TILE_RING, C])
        xs = ph.sb("xs", [P, 2, C])
        hid = ph.sb("hid", [P, 2, FH])
        gel = ph.sb("gel", [P, 2, FH])
        hT = ph.sb("hT", [P, 2, FH])
        Y = ph.sb("Y", [P, TILE_RING, C])
        psX = [ph.ps(f"psX{k}", [P, 512]) for k in range(2)]
        psH = [ph.ps(f"psH{k}", [P, 512]) for k in range(2)]
        psT = [ph.ps(f"psT{k}", [P, 512]) for k in range(2)]
        psY = [ph.ps(f"psY{k}", [P, 512]) for k in range(2)]
        x_in = [ph.sem(f"x_in{k}") for k in range(TILE_RING)]
        y_out = [ph.sem(f"y_out{k}") for k in range(TILE_RING)]
        x_turned2 = ph.sem("x_turned2")
        xs_ready2 = ph.sem("xs_ready2")
        up2 = ph.sem("up2")
        hid_ready2 = ph.sem("hid_ready2")
        gel_ready2 = ph.sem("gel_ready2")
        h_turned2 = ph.sem("h_turned2")
        hT_ready2 = ph.sem("hT_ready2")
        down2 = ph.sem("down2")
        y_ready2 = ph.sem("y_ready2")
        block = ph.block()
        assert NT % TILE_RING == 1

        def over_slots(eng, step):
            for slot in range(TILE_RING):
                step(0, slot, False)
            with eng.Fori(1, NT // TILE_RING) as i:
                for slot in range(TILE_RING):
                    step(i, slot, False)
            step(NT // TILE_RING, 0, True)

        def owner_of(eng, j):
            return eng.value_load(owner[0:1, bass.ds(j, 1)], min_val=0, max_val=EX - 1)

        @block.sync
        def _(sp):
            def step(i, slot, last):
                j = TILE_RING * i + slot
                if not is_zero(i):
                    sp.wait_ge(x_turned2, j - 1)
                sp.dma_start(X[:, slot, :], dr["xslot"][bass.ds(j * P, P), :]).then_inc(x_in[slot], 16)

            over_slots(sp, step)

        @block.gpsimd
        def _(g):
            def step(i, slot, last):
                j = TILE_RING * i + slot
                g.wait_ge(y_ready2, j + 3)
                g.dma_start(dr["yslot"][bass.ds(j * P, P), :], Y[:, slot, :]).then_inc(y_out[slot], 16)

            over_slots(g, step)
            for slot in range(TILE_RING):
                g.wait_ge(y_out[slot], 16 * (NT // TILE_RING + (slot == 0)))

        @block.tensor
        def _(pe):
            for s in (x_turned2, up2, h_turned2, down2):
                pe.sem_inc(s, 2)

            def turn_x(i, slot):
                j = TILE_RING * i + slot
                pe.wait_ge(x_in[slot], 16 * (i + 1))
                pe.wait_ge(xs_ready2, j + 1)
                for k in range(2):
                    mm = pe.transpose(psX[slot % 2][:, k * P:(k + 1) * P], X[:, slot, k * P:(k + 1) * P], ident[:, :])
                mm.then_inc(x_turned2, 1)

            def up(j, slot, e):
                pe.wait_ge(xs_ready2, j + 3)
                pe.wait_ge(hid_ready2, j + 1)
                for k in range(2):
                    mm = pe.matmul(psH[slot % 2][:, :], xs[:, slot % 2, k * P:(k + 1) * P],
                                   W1[:, bass.ds(e, 1), k, :].rearrange("p a f -> p (a f)"), start=(k == 0), stop=(k == 1))
                mm.then_inc(up2, 1)

            def turn_h(j, slot):
                pe.wait_ge(gel_ready2, j + 3)
                pe.wait_ge(hT_ready2, j + 1)
                for c in range(HC):
                    mm = pe.transpose(psT[slot % 2][:, c * P:(c + 1) * P], gel[:, slot % 2, c * P:(c + 1) * P], ident[:, :])
                mm.then_inc(h_turned2, 1)

            def down(j, slot, e):
                pe.wait_ge(hT_ready2, j + 3)
                pe.wait_ge(y_ready2, j + 1)
                for c in range(HC):
                    mm = pe.matmul(psY[slot % 2][:, 0:C], hT[:, slot % 2, c * P:(c + 1) * P],
                                   W2[:, bass.ds(e, 1), c, :].rearrange("p a o -> p (a o)"), start=(c == 0), stop=(c == HC - 1))
                mm.then_inc(down2, 1)

            turn_x(0, 0)
            turn_x(0, 1)
            up(0, 0, owner_of(pe, 0))

            def step(i, slot, turn):
                j = TILE_RING * i + slot
                turn_h(j, slot)
                up(j + 1, slot + 1, owner_of(pe, j + 1))
                if turn:
                    turn_x(i + (slot + 2) // TILE_RING, (slot + 2) % TILE_RING)
                down(j, slot, owner_of(pe, j))

            for slot in range(TILE_RING):
                step(0, slot, True)
            with pe.Fori(1, NT // TILE_RING - 1) as i:
                for slot in range(TILE_RING):
                    step(i, slot, True)
            for slot in range(TILE_RING):
                step(NT // TILE_RING - 1, slot, slot < TILE_RING - 1)
            turn_h(NT - 1, 0)
            down(NT - 1, 0, owner_of(pe, NT - 1))

        @block.scalar
        def _(a):
            a.sem_inc(xs_ready2, 2)
            a.sem_inc(gel_ready2, 2)

            def copy_x(i, slot):
                j = TILE_RING * i + slot
                a.wait_ge(x_turned2, j + 3)
                a.wait_ge(up2, j + 1)
                a.activation(xs[:, slot % 2, :], psX[slot % 2][:, 0:C], ACT.Copy).then_inc(xs_ready2, 1)

            def gelu(i, slot):
                j = TILE_RING * i + slot
                a.wait_ge(hid_ready2, j + 3)
                a.wait_ge(h_turned2, j + 1)
                a.activation(gel[:, slot % 2, :], hid[:, slot % 2, :], ACT.Gelu).then_inc(gel_ready2, 1)

            copy_x(0, 0)

            def step(i, slot, last):
                if not last:
                    copy_x(i + (slot + 1) // TILE_RING, (slot + 1) % TILE_RING)
                gelu(i, slot)

            over_slots(a, step)

        @block.vector
        def _(v):
            for s in (hid_ready2, hT_ready2, y_ready2):
                v.sem_inc(s, 2)

            def bias(j, slot, e):
                v.wait_ge(up2, j + 3)
                v.wait_ge(gel_ready2, j + 1)
                v.tensor_tensor(hid[:, slot % 2, :], psH[slot % 2][:, :],
                                b1[:, bass.ds(e, 1), :].rearrange("p a f -> p (a f)"), ALU.add).then_inc(hid_ready2, 1)

            def copy_h(j, slot):
                v.wait_ge(h_turned2, j + 3)
                v.wait_ge(down2, j + 1)
                v.tensor_copy(hT[:, slot % 2, :], psT[slot % 2][:, :]).then_inc(hT_ready2, 1)

            def result(i, j, slot, e):
                v.wait_ge(down2, j + 3)
                if not is_zero(i):
                    v.wait_ge(y_out[slot], 16 * i)
                v.tensor_tensor(Y[:, slot, :], psY[slot % 2][:, 0:C],
                                b2[:, bass.ds(e, 1), :].rearrange("p a o -> p (a o)"), ALU.add).then_inc(y_ready2, 1)

            bias(0, 0, owner_of(v, 0))

            def step(i, slot, last):
                j = TILE_RING * i + slot
                copy_h(j, slot)
                if not last:
                    bias(j + 1, slot + 1, owner_of(v, j + 1))
                result(i, j, slot, owner_of(v, j))

            over_slots(v, step)


def combine(nc, wts, slots, dr, out):
    with Phase(nc, "combine") as ph:
        X2 = ph.sb("X2", [P, NB, C])
        Y = ph.sb("Y", [P, TILE_RING, 2, C])
        x2_in = ph.sem("x2_in")
        gathered = [ph.sem(f"gathered{k}") for k in range(TILE_RING)]
        first = ph.sem("first")
        summed = ph.sem("summed")
        stored = ph.sem("stored")
        block = ph.block()

        @block.gpsimd
        def _(g):
            for b in range(NB):
                if b >= TILE_RING:
                    g.wait_ge(summed, b - TILE_RING + 1)
                for k in range(2):
                    n = TAIL if b == NB - 1 else P
                    g.indirect_dma_start(Y[0:n, b % TILE_RING, k, :], None, dr["yslot"],
                                         bass.IndirectOffsetOnAxis(slots[0:n, k, b:b + 1], 0)).then_inc(gathered[b % TILE_RING], 16)

        @block.vector
        def _(v):
            v.wait_ge(x2_in, 16)
            for b in range(NB):
                n = TAIL if b == NB - 1 else P
                v.wait_ge(gathered[b % TILE_RING], 32 * (b // TILE_RING + 1))
                for k in range(2):
                    if k == 1:
                        v.wait_ge(first, b + 1)
                    v.scalar_tensor_tensor(out=X2[0:n, b, :], in0=Y[0:n, b % TILE_RING, k, :], scalar=wts[0:n, b, k:k + 1],
                                           in1=X2[0:n, b, :], op0=ALU.mult, op1=ALU.add).then_inc(summed if k else first, 1)

        @block.sync
        def _(sp):
            sp.dma_start(X2[:, :, :], dr["x2"].rearrange("(b p) c -> p b c", p=P)).then_inc(x2_in, 16)
            for b in range(NB):
                n = TAIL if b == NB - 1 else P
                sp.wait_ge(summed, b + 1)
                sp.dma_start(out[b * P:b * P + n, :], X2[0:n, b, :]).then_inc(stored, 16)
            sp.wait_ge(stored, 16 * NB)


def build(nc, io, out):
    def dram(name, shape, dt=F32):
        return nc.dram_tensor(name, shape, dt, kind="Internal").ap()

    dr = {"src_pad": dram("src_pad", (TG + 1, GE), I32), "dst_pad": dram("dst_pad", (TG + 1, GE), I32),
          "reset": dram("reset", (NG, H, 2, P), BF16), "rows": dram("rows", (NPAD, RW)),
          "h": dram("h", (NPAD, C)), "mix": dram("mix", (NPAD, C)), "x2": dram("x2", (NPAD, C)),
          "xslot": dram("xslot", (NT * P, C)), "yslot": dram("yslot", (NT * P, C))}

    with ExitStack() as ctx:
        def sb(name, shape, dt=F32):
            return ctx.enter_context(nc.sbuf_tensor(name, shape, dt))

        st = {"ident": sb("ident", [P, P]), "iota": sb("iota", [P, P])}
        with ExitStack() as inner:
            def sbi(name, shape, dt=F32):
                return inner.enter_context(nc.sbuf_tensor(name, shape, dt))

            for n in ("srcT", "relT", "lastT"):
                st[n] = sbi(n, [P, NG, 2])
            st["words"] = sbi("words", [P, NW], I32)
            st["rises"] = sbi("rises", [P, NW, 2, H * WG], BF16)
            prepare_walk(nc, io["src"], io["dst"], st, dr)

            with ExitStack() as mx:
                XN = mx.enter_context(nc.sbuf_tensor("XN", [P, NB, C], F32))
                WT = mx.enter_context(nc.sbuf_tensor("WT", [P, 2, 3 * C], F32))
                W1T = mx.enter_context(nc.sbuf_tensor("W1T", [P, 2, C], F32))
                W2T = mx.enter_context(nc.sbuf_tensor("W2T", [P, 2, C], F32))
                KV = mx.enter_context(nc.sbuf_tensor("KV", [P, 2, P + GH], F32))
                turn_weights(nc, "turn_qkv", io["mix_Wqkv"], WT, st["ident"])
                turn_weights(nc, "turn_w1", io["mix_W1"], W1T, st["ident"])
                turn_weights(nc, "turn_w2", io["mix_W2"], W2T, st["ident"])
                move_tiles(nc, "load_x", XN, io["x"])
                normalize_tiles(nc, "norm_x", XN, None, None)
                mix_keys(nc, st, XN, WT, KV, dr["xslot"])
                mix_queries(nc, st, XN, WT, KV)
                normalize_tiles(nc, "norm_mix1", XN, io["mix_ln1_g"], io["mix_ln1_b"])
                mix_mlp(nc, st, io, XN, W1T, W2T)
                normalize_tiles(nc, "norm_mix2", XN, io["mix_ln2_g"], io["mix_ln2_b"])
                move_tiles(nc, "store_mix", dr["mix"], XN)

            st["acc"] = sbi("acc", [P, NB, RW])
            st["ADM"] = sbi("ADM", [P, NB, 2 * H])
            st["own"] = sbi("own", [P, NB, H])
            node_phase(nc, 0, st, io, dr)
            for layer in range(3):
                edge_phase(nc, layer, st, dr)
                node_phase(nc, layer + 1, st, io, dr)

        wts = sb("wts", [P, NB, 2])
        slots = sb("slots", [P, 2, NB], I32)
        owner = sb("owner", [P, NT], I32)
        with ExitStack() as ffn:
            W1 = ffn.enter_context(nc.sbuf_tensor("W1", [P, EX, 2, FH], F32))
            W2 = ffn.enter_context(nc.sbuf_tensor("W2", [P, EX, HC, C], F32))
            b1 = ffn.enter_context(nc.sbuf_tensor("b1", [P, EX, FH], F32))
            b2 = ffn.enter_context(nc.sbuf_tensor("b2", [P, EX, C], F32))
            with nc.sbuf_tensor("XF", [P, NB, C], F32) as XF:
                move_tiles(nc, "load_x2", XF, dr["x2"])
                normalize_tiles(nc, "norm_x2", XF, None, None)
                normalize_tiles(nc, "norm_ffn", XF, io["ffn_gamma"], io["ffn_beta"])
                route(nc, st, io, XF, W1, W2, b1, b2, wts, slots, owner, dr)
            experts(nc, st, W1, W2, b1, b2, owner, dr)
        combine(nc, wts, slots, dr, out)


_GNN = [f"L0_gnn_{n}{layer}" for layer in range(3) for n in ("W", "att_src", "att_dst", "bias", "ln_g", "ln_b")]
_MIX = [f"L0_mix_{n}" for n in ("Wqkv", "ln1_g", "ln1_b", "W1", "b1", "W2", "b2", "ln2_g", "ln2_b")]
_FFN = [f"L0_ffn_{n}" for n in ("gamma", "beta", "Wr", "br", "W1", "b1", "W2", "b2")]
_INS = ["x", "src", "dst"] + _GNN + _MIX + _FFN


def kernel(**inputs):
    import numpy as _np
    import concourse.bacc as _bacc
    from concourse.bass_utils import run_bass_kernel_spmd as _run

    nc = _bacc.Bacc("TRN2", target_bir_lowering=False, num_devices=1)
    arrays, io = {}, {}
    for name in _INS:
        a = _np.ascontiguousarray(inputs[name])
        arrays[f"in_{name}"] = a
        short = name.replace("L0_gnn_", "").replace("L0_", "")
        io[short] = nc.dram_tensor(f"in_{name}", a.shape, mybir.dt.from_np(a.dtype), kind="ExternalInput").ap()
    out = nc.dram_tensor("out", (N, C), F32, kind="ExternalOutput").ap()
    build(nc, io, out)
    r = _run(nc, [arrays], core_ids=[0])
    return r.results[0]["out"]
```
